# Optimizing a Trainium2 kernel written in Bass

```python
import numpy as np
import jax
import jax.numpy as jnp

def _softmax(x, axis=-1):
    return jax.nn.softmax(x, axis=axis)

def _gelu(x):
    return jax.nn.gelu(x, approximate=True)

def _silu(x):
    return jax.nn.silu(x)

def _sigmoid(x):
    return jax.nn.sigmoid(x)

def _layernorm(x, axis=-1, eps=1e-05):
    m = jnp.mean(x, axis=axis, keepdims=True)
    v = jnp.var(x, axis=axis, keepdims=True)
    return (x - m) / jnp.sqrt(v + eps)

def _scatter_add(tgt, idx, src, axis=0):
    return tgt.at[idx].add(src)

def _segment_sum(src, seg, n):
    return jax.ops.segment_sum(src, seg, n)
kernel_name = 'mk_recurrent_d2_jaxref_r8_695a0a'

def setup_inputs(seed: int=0):
    np.random.seed(seed)
    _w = jnp.asarray

    def _L0_attn_setup():
        import jax, jax.numpy as jnp
        import numpy as np
        B, L, D = (8, 512, 128)
        LN_EPS = 1e-05

        def _linear_attn(q, k, v):
            d = q.shape[-1]
            q = jax.nn.softmax(q, axis=-1) * d ** (-0.5)
            k = jax.nn.softmax(k, axis=-2)
            context = jnp.einsum('bld,ble->bde', k, v)
            return jnp.einsum('bld,bde->ble', q, context)

        def _layernorm(x, gamma, beta):
            mu = jnp.mean(x, axis=-1, keepdims=True)
            var = jnp.var(x, axis=-1, keepdims=True)
            return (x - mu) * jax.lax.rsqrt(var + LN_EPS) * gamma + beta
        key = jax.random.key(seed)
        ks = jax.random.split(key, 5)
        scale = 1.0 / np.sqrt(D)
        return {'x': jax.random.normal(ks[0], (B, L, D), dtype=jnp.float32), 'Wq': jax.random.normal(ks[1], (D, D), dtype=jnp.float32) * scale, 'Wk': jax.random.normal(ks[2], (D, D), dtype=jnp.float32) * scale, 'Wv': jax.random.normal(ks[3], (D, D), dtype=jnp.float32) * scale, 'Wo': jax.random.normal(ks[4], (D, D), dtype=jnp.float32) * scale, 'bo': jnp.zeros((D,), dtype=jnp.float32), 'gamma': jnp.ones((D,), dtype=jnp.float32), 'beta': jnp.zeros((D,), dtype=jnp.float32)}
    _L0_attn_in = _L0_attn_setup()

    def _L0_ffn_setup():
        import jax, jax.numpy as jnp
        import numpy as np
        TOP_K = 2
        key = jax.random.key(seed)
        k1, k2, k3, k4 = jax.random.split(key, 4)
        B, S, D, H, E = (2, 256, 128, 512, 8)
        x = jax.random.normal(k1, (B, S, D), dtype=jnp.float32)
        router_w = jax.random.normal(k2, (E, D), dtype=jnp.float32) * 0.01
        w1 = jax.random.normal(k3, (E, H, D), dtype=jnp.float32) * (2.0 / D) ** 0.5
        b1 = jnp.zeros((E, H), dtype=jnp.float32)
        w2 = jax.random.normal(k4, (E, D, H), dtype=jnp.float32) * (2.0 / H) ** 0.5
        b2 = jnp.zeros((E, D), dtype=jnp.float32)
        return {'x': x, 'router_w': router_w, 'w1': w1, 'b1': b1, 'w2': w2, 'b2': b2}
    _L0_ffn_in = _L0_ffn_setup()

    def _L1_attn_setup():
        import jax, jax.numpy as jnp
        import numpy as np
        HID = 128
        NH = 16
        HD = HID // NH
        RD = int(HD * 0.25)
        B = 2
        S = 256
        ROPE_BASE = 10000.0

        def _rotary_tables(seq_len):
            inv_freq = 1.0 / ROPE_BASE ** (jnp.arange(0, RD, 2, dtype=jnp.float32) / RD)
            t = jnp.arange(seq_len, dtype=jnp.float32)
            freqs = jnp.outer(t, inv_freq)
            emb = jnp.concatenate([freqs, freqs], axis=-1)
            return (jnp.cos(emb)[None, None], jnp.sin(emb)[None, None])

        def _rotate_half(x):
            x1, x2 = jnp.split(x, 2, axis=-1)
            return jnp.concatenate([-x2, x1], axis=-1)
        key = jax.random.key(seed)
        ks = jax.random.split(key, 4)
        hidden_states = jax.random.normal(ks[0], (B, S, HID), jnp.float32)
        Wqkv = jax.random.normal(ks[1], (3 * HID, HID), jnp.float32) * HID ** (-0.5)
        bqkv = jnp.zeros((3 * HID,), jnp.float32)
        Wd = jax.random.normal(ks[2], (HID, HID), jnp.float32) * HID ** (-0.5)
        bd = jnp.zeros((HID,), jnp.float32)
        return {'hidden_states': hidden_states, 'Wqkv': Wqkv, 'bqkv': bqkv, 'Wd': Wd, 'bd': bd}
    _L1_attn_in = _L1_attn_setup()

    def _L1_ffn_setup():
        import jax, jax.numpy as jnp
        import numpy as np
        import math
        N_EXP = 8
        TOP_K = 2
        CAPACITY_FACTOR = 1.25

        def _capacity(num_tokens):
            cap = math.floor(TOP_K * CAPACITY_FACTOR * num_tokens / N_EXP)
            cap += cap % 2
            return int(cap)
        key = jax.random.key(seed)
        k1, k2, k3, k4 = jax.random.split(key, 4)
        B, C, d = (4, 128, 128)
        x = jax.random.normal(k1, (B, C, d), dtype=jnp.float32)
        w_g = jax.random.normal(k2, (d, N_EXP), dtype=jnp.float32) * 0.02
        c_fc = jax.random.normal(k3, (N_EXP, d, 4 * d), dtype=jnp.float32) * 0.02
        c_proj = jax.random.normal(k4, (N_EXP, 4 * d, d), dtype=jnp.float32) * 0.02
        return {'x': x, 'w_g': w_g, 'c_fc': c_fc, 'c_proj': c_proj}
    _L1_ffn_in = _L1_ffn_setup()
    _d = {'L0_attn_x': _L0_attn_in['x'], 'L0_attn_Wq': _L0_attn_in['Wq'], 'L0_attn_Wk': _L0_attn_in['Wk'], 'L0_attn_Wv': _L0_attn_in['Wv'], 'L0_attn_Wo': _L0_attn_in['Wo'], 'L0_attn_bo': _L0_attn_in['bo'], 'L0_attn_gamma': _L0_attn_in['gamma'], 'L0_attn_beta': _L0_attn_in['beta'], 'L0_ffn_router_w': _L0_ffn_in['router_w'], 'L0_ffn_w1': _L0_ffn_in['w1'], 'L0_ffn_b1': _L0_ffn_in['b1'], 'L0_ffn_w2': _L0_ffn_in['w2'], 'L0_ffn_b2': _L0_ffn_in['b2'], 'L1_attn_Wqkv': _L1_attn_in['Wqkv'], 'L1_attn_bqkv': _L1_attn_in['bqkv'], 'L1_attn_Wd': _L1_attn_in['Wd'], 'L1_attn_bd': _L1_attn_in['bd'], 'L1_ffn_w_g': _L1_ffn_in['w_g'], 'L1_ffn_c_fc': _L1_ffn_in['c_fc'], 'L1_ffn_c_proj': _L1_ffn_in['c_proj']}
    _x0 = _d['L0_attn_x']
    _d['L0_attn_x'] = jax.random.normal(jax.random.fold_in(jax.random.key(seed), 1), (8, 512, 128), dtype=_x0.dtype)
    del _x0
    return _d

def reference(L0_attn_x, L0_attn_Wq, L0_attn_Wk, L0_attn_Wv, L0_attn_Wo, L0_attn_bo, L0_attn_gamma, L0_attn_beta, L0_ffn_router_w, L0_ffn_w1, L0_ffn_b1, L0_ffn_w2, L0_ffn_b2, L1_attn_Wqkv, L1_attn_bqkv, L1_attn_Wd, L1_attn_bd, L1_ffn_w_g, L1_ffn_c_fc, L1_ffn_c_proj):

    def _L0_attn_ref(x, Wq, Wk, Wv, Wo, bo, gamma, beta):
        import jax, jax.numpy as jnp
        import numpy as np
        B, L, D = (8, 512, 128)
        LN_EPS = 1e-05

        def _linear_attn(q, k, v):
            d = q.shape[-1]
            q = jax.nn.softmax(q, axis=-1) * d ** (-0.5)
            k = jax.nn.softmax(k, axis=-2)
            context = jnp.einsum('bld,ble->bde', k, v)
            return jnp.einsum('bld,bde->ble', q, context)

        def _layernorm(x, gamma, beta):
            mu = jnp.mean(x, axis=-1, keepdims=True)
            var = jnp.var(x, axis=-1, keepdims=True)
            return (x - mu) * jax.lax.rsqrt(var + LN_EPS) * gamma + beta
        q = jnp.einsum('bld,de->ble', x, Wq)
        k = jnp.einsum('bld,de->ble', x, Wk)
        v = jnp.einsum('bld,de->ble', x, Wv)
        attn = _linear_attn(q, k, v)
        out = jnp.einsum('ble,ed->bld', attn, Wo) + bo
        return _layernorm(x + out, gamma, beta)

    def _L0_ffn_ref(x, router_w, w1, b1, w2, b2):
        import jax, jax.numpy as jnp
        import numpy as np
        TOP_K = 2
        B, S, D = x.shape
        E = w1.shape[0]
        T = B * S
        x_flat = x.reshape(T, D)
        logits = jnp.einsum('td,ed->te', x_flat, router_w)
        probs = jax.nn.softmax(logits, axis=-1)
        topw, topi = jax.lax.top_k(probs, TOP_K)
        topw = topw / jnp.sum(topw, axis=-1, keepdims=True)
        cw = jnp.zeros((T, E), dtype=x.dtype)
        cw = cw.at[jnp.arange(T)[:, None], topi].add(topw)
        out = jnp.zeros((T, w2.shape[1]), dtype=x.dtype)
        for e in range(E):
            h = jax.nn.gelu(x_flat @ w1[e].T + b1[e], approximate=False)
            o = h @ w2[e].T + b2[e]
            out = out + cw[:, e:e + 1] * o
        return out.reshape(B, S, -1)

    def _L1_attn_ref(hidden_states, Wqkv, bqkv, Wd, bd):
        import jax, jax.numpy as jnp
        import numpy as np
        HID = 128
        NH = 16
        HD = HID // NH
        RD = int(HD * 0.25)
        B = 2
        S = 256
        ROPE_BASE = 10000.0

        def _rotary_tables(seq_len):
            inv_freq = 1.0 / ROPE_BASE ** (jnp.arange(0, RD, 2, dtype=jnp.float32) / RD)
            t = jnp.arange(seq_len, dtype=jnp.float32)
            freqs = jnp.outer(t, inv_freq)
            emb = jnp.concatenate([freqs, freqs], axis=-1)
            return (jnp.cos(emb)[None, None], jnp.sin(emb)[None, None])

        def _rotate_half(x):
            x1, x2 = jnp.split(x, 2, axis=-1)
            return jnp.concatenate([-x2, x1], axis=-1)
        b, s, _ = hidden_states.shape
        qkv = hidden_states @ Wqkv.T + bqkv
        qkv = qkv.reshape(b, s, 3, NH, HD).transpose(2, 0, 3, 1, 4)
        q, k, v = (qkv[0], qkv[1], qkv[2])
        cos, sin = _rotary_tables(s)
        q_rot, q_pass = (q[..., :RD], q[..., RD:])
        k_rot, k_pass = (k[..., :RD], k[..., RD:])
        q_rot = q_rot * cos + _rotate_half(q_rot) * sin
        k_rot = k_rot * cos + _rotate_half(k_rot) * sin
        q = jnp.concatenate([q_rot, q_pass], axis=-1)
        k = jnp.concatenate([k_rot, k_pass], axis=-1)
        scale = HD ** (-0.5)
        logits = jnp.einsum('bhqd,bhkd->bhqk', q, k) * scale
        causal_mask = jnp.triu(jnp.full((s, s), -jnp.inf, dtype=logits.dtype), 1)
        probs = jax.nn.softmax(logits + causal_mask, axis=-1)
        L = jnp.eye(s, dtype=probs.dtype) - jnp.tril(probs, -1)
        rhs = jnp.diagonal(probs, axis1=-2, axis2=-1)[..., None] * v
        A = jax.scipy.linalg.solve_triangular(L, rhs, lower=True)
        attn_output = A.transpose(0, 2, 1, 3).reshape(b, s, HID)
        return attn_output @ Wd.T + bd

    def _L1_ffn_ref(x, w_g, c_fc, c_proj):
        import jax, jax.numpy as jnp
        import numpy as np
        import math
        N_EXP = 8
        TOP_K = 2
        CAPACITY_FACTOR = 1.25

        def _capacity(num_tokens):
            cap = math.floor(TOP_K * CAPACITY_FACTOR * num_tokens / N_EXP)
            cap += cap % 2
            return int(cap)
        B, C, d = x.shape
        T = B * C
        cap = _capacity(T)
        xt = x.reshape(T, d)
        logits = xt @ w_g
        top_v, top_i = jax.lax.top_k(logits, TOP_K)
        full = jnp.full_like(logits, -jnp.inf)
        full = full.at[jnp.arange(T)[:, None], top_i].set(top_v)
        probs = jax.nn.softmax(full, axis=-1)
        exp_mask = jax.nn.one_hot(top_i, N_EXP, dtype=jnp.int32)
        exp_mask = jnp.transpose(exp_mask, (1, 0, 2))
        exp_rank = jnp.cumsum(exp_mask.reshape(TOP_K * T, N_EXP), axis=0) - 1
        exp_rank = exp_rank.reshape(TOP_K, T, N_EXP)
        exp_mask = exp_mask * (exp_rank < cap).astype(jnp.int32)
        exp_rank = jnp.sum(exp_mask * exp_rank, axis=-1)
        exp_weights = exp_mask.astype(x.dtype) * probs[None]
        rank_oh = jax.nn.one_hot(exp_rank, cap, dtype=x.dtype)
        cb_weight = jnp.einsum('kte,ktc->tec', exp_weights, rank_oh)
        sec_mask = (cb_weight != 0).astype(x.dtype)
        exp_batches = jnp.einsum('tec,td->ecd', sec_mask, xt)
        h = jax.nn.gelu(jnp.einsum('ecd,edf->ecf', exp_batches, c_fc), approximate=False)
        exp_out = jnp.einsum('ecf,efd->ecd', h, c_proj)
        out = cb_weight.reshape(T, N_EXP * cap) @ exp_out.reshape(N_EXP * cap, d)
        return out.reshape(B, C, d)
    x = L0_attn_x
    xn = _layernorm(x, axis=-1)
    s = _L0_attn_ref(xn, L0_attn_Wq, L0_attn_Wk, L0_attn_Wv, L0_attn_Wo, L0_attn_bo, L0_attn_gamma, L0_attn_beta)
    g = _silu(_L0_ffn_ref(xn, L0_ffn_router_w, L0_ffn_w1, L0_ffn_b1, L0_ffn_w2, L0_ffn_b2))
    x = x + s * g
    xn = _layernorm(x, axis=-1)
    s = _L1_attn_ref(xn, L1_attn_Wqkv, L1_attn_bqkv, L1_attn_Wd, L1_attn_bd)
    g = _silu(_L1_ffn_ref(xn, L1_ffn_w_g, L1_ffn_c_fc, L1_ffn_c_proj))
    x = x + s * g
    return x

_drawn_inputs = setup_inputs


def setup_inputs(seed=0):
    import zlib

    import numpy as np

    out = dict(_drawn_inputs(seed))
    spreads = {'L0_attn_bo': (0.0, 0.1),
     'L0_attn_gamma': (1.0, 0.2),
     'L0_attn_beta': (0.0, 0.1),
     'L0_ffn_b1': (0.0, 0.1),
     'L0_ffn_b2': (0.0, 0.1),
     'L1_attn_bqkv': (0.0, 0.8),
     'L1_attn_bd': (0.0, 2.0)}
    factors = {'L0_attn_Wq': 8.0,
     'L0_attn_Wk': 8.0,
     'L0_attn_Wv': 8.0,
     'L0_attn_Wo': 8.0,
     'L1_attn_Wqkv': 7.819,
     'L1_attn_Wd': 7.458,
     'L1_ffn_w_g': 8.0,
     'L1_ffn_c_fc': 7.439,
     'L1_ffn_c_proj': 7.331}
    for name, (base, spread) in spreads.items():
        noise = np.random.default_rng([zlib.crc32(name.encode()), seed]).standard_normal(out[name].shape)
        drawn = base * np.exp(spread * noise) if base else spread * noise
        out[name] = jnp.asarray(drawn.astype(out[name].dtype))
    for name, factor in factors.items():
        out[name] = (out[name] * factor).astype(out[name].dtype)
    return out
```

```python
from contextlib import ExitStack
from itertools import count

import concourse.bass as bass
import numpy as np
from concourse import mybir

P = 128
B, L, D = 8, 512, 128
T = B * L
NT = T // P
LT = L // P
E, H = 8, 512
HC = H // P
NH = 16
HD = D // NH
BH = B * NH
CAP = 1280
SB = 64
NSUB = P // SB
EPS = 1e-5
BIG = -2.0 ** 100

F32 = mybir.dt.float32
BF16 = mybir.dt.bfloat16
U32 = mybir.dt.uint32
ALU = mybir.AluOpType
ACT = mybir.ActivationFunctionType
AX_X = mybir.AxisListType.X


STAGES = count()


class Chain:

    def __init__(self, eng, sem):
        self.eng, self.sem, self.n = eng, sem, 0

    def __call__(self, ins):
        self.n += 1
        ins.then_inc(self.sem, 1)
        self.eng.wait_ge(self.sem, self.n)


def tensors(nc, ctx):
    sems, stage = [], next(STAGES)

    def sb(name, shape, dt=F32):
        return ctx.enter_context(nc.sbuf_tensor(name, shape, dt))

    def sem(name):
        sems.append(nc.alloc_semaphore(f"{name}_{stage}"))
        return sems[-1]

    def clear():
        if sems:
            nc.clear_and_free_semaphores(sems)
            nc.all_engine_barrier()

    ctx.callback(clear)

    return sb, sem


def normalise(nc, name, x_dram, x, xn, xnT, ident, bank):
    G = LT
    with ExitStack() as ctx:
        sb, sem = tensors(nc, ctx)
        stats = sb(name + "stats", [P, NT, 6])
        mv = sb(name + "mv", [P, NT, 2])
        rstd = sb(name + "rstd", [P, NT])
        x_in = [sem(f"{name}x_in{g}") for g in range(B)]
        dve_done, xn_ready = sem(name + "dve_done"), sem(name + "xn_ready")
        turned, copied = sem(name + "turned"), sem(name + "copied")
        var_ready, std_ready = sem(name + "var_ready"), sem(name + "std_ready")
        block = ctx.enter_context(nc.Block())

        @block.sync
        def _(sp):
            if x_dram is not None:
                for g in range(B):
                    sp.dma_start(x[:, g * G:(g + 1) * G, :],
                                 x_dram[g].rearrange("(t p) d -> p t d", p=P)).then_inc(x_in[g], 16)

        @block.vector
        def _(dve):
            link = Chain(dve, dve_done)
            for g in range(B):
                s = slice(g * G, (g + 1) * G)
                if x_dram is not None:
                    dve.wait_ge(x_in[g], 16)
                for t in range(g * G, (g + 1) * G):
                    last = nc.vector.bn_stats(stats[:, t, :], x[:, t, :])
                link(last)
                for t in range(g * G, (g + 1) * G):
                    last = nc.vector.bn_aggr(mv[:, t, :], stats[:, t, :])
                link(last)
                nc.vector.tensor_scalar(rstd[:, s], mv[:, s, 1], EPS, None, ALU.add).then_inc(var_ready, 1)
            for g in range(B):
                dve.wait_ge(std_ready, g + 1)
                s = slice(g * G, (g + 1) * G)
                link(nc.vector.reciprocal(rstd[:, s], rstd[:, s]))
                for t in range(g * G, (g + 1) * G):
                    last = nc.vector.tensor_scalar(xn[:, t, :], x[:, t, :], mv[:, t, 0:1], rstd[:, t:t + 1],
                                                   ALU.subtract, ALU.mult)
                last.then_inc(xn_ready, 1)

        @block.tensor
        def _(pe):
            for g in range(B):
                pe.wait_ge(xn_ready, g + 1)
                if g >= 2:
                    pe.wait_ge(copied, g - 1)
                for t in range(G):
                    last = nc.tensor.transpose(bank[g % 2][:, t * P:(t + 1) * P], xn[:, g * G + t, :], ident[:, :])
                last.then_inc(turned, 1)

        @block.scalar
        def _(act):
            for g in range(B):
                act.wait_ge(var_ready, g + 1)
                nc.scalar.activation(rstd[:, g * G:(g + 1) * G], rstd[:, g * G:(g + 1) * G], ACT.Sqrt).then_inc(std_ready, 1)
            for g in range(B):
                act.wait_ge(turned, g + 1)
                nc.scalar.copy(xnT[:, g * L:(g + 1) * L], bank[g % 2][:, :]).then_inc(copied, 1)


def linear_attention(nc, xn, xnT, s, w, ident, bank):
    with ExitStack() as ctx:
        sb, sem = tensors(nc, ctx)
        wk, wqv, wo = sb("wk", [P, D]), sb("wqv", [P, 2, D]), sb("wo", [P, D])
        rows = sb("rows", [P, 3, D])
        ek, ekT = sb("ek", [P, L]), sb("ekT", [P, LT, P])
        eq, eqT = sb("eq", [P, LT, P]), sb("eqT", [P, L])
        v = sb("v", [P, LT, P])
        ctxT, cw = sb("ctxT", [P, P]), sb("cw", [P, P])
        neg_kmax, ksum, rk = sb("neg_kmax", [P, 1]), sb("ksum", [P, 1]), sb("rk", [P, 1])
        neg_qmax, qsum, rq = sb("neg_qmax", [P, LT]), sb("qsum", [P, LT]), sb("rq", [P, LT])
        stats, mv, rstd = sb("ystats", [P, LT, 6]), sb("ymv", [P, NT, 2]), sb("yrstd", [P, NT])
        w_in = sem("attn_w_in")
        k_mm, qv_mm, k_max, q_max = sem("k_mm"), sem("qv_mm"), sem("k_max"), sem("q_max")
        k_exp, q_exp, v_copy = sem("k_exp"), sem("q_exp"), sem("v_copy")
        k_turned, q_turned, k_copied, q_copied = sem("k_turned"), sem("q_turned"), sem("k_copied"), sem("q_copied")
        ctx_mm, ctx_copied, cw_mm, cw_copied = sem("ctx_mm"), sem("ctx_copied"), sem("cw_mm"), sem("cw_copied")
        var_ready, std_ready = sem("yvar_ready"), sem("ystd_ready")
        out_mm, out_read, dve_done = sem("out_mm"), sem("out_read"), sem("attn_dve_done")
        block = ctx.enter_context(nc.Block())
        ps_k, ps_qv, ps_kT, ps_qT, ps_c, ps_o = bank[0], (bank[1], bank[2]), bank[3], bank[4], bank[5], bank[6]

        @block.sync
        def _(sp):
            for dst, src in ((wk[:, :], w["Wk"]), (wqv[:, 0, :], w["Wq"]), (wqv[:, 1, :], w["Wv"]), (wo[:, :], w["Wo"])):
                sp.dma_start(dst, src).then_inc(w_in, 16)
            for i, n in enumerate(("bo", "gamma", "beta")):
                sp.dma_start(rows[:, i, :], w[n].rearrange("(a d) -> a d", a=1).broadcast_to([P, D])).then_inc(w_in, 16)

        @block.tensor
        def _(pe):
            def project(b):
                if b >= 1:
                    pe.wait_ge(k_exp, b)
                nc.tensor.matmul(ps_k[:, :], wk[:, :], xnT[:, b * L:(b + 1) * L], start=True, stop=True).then_inc(k_mm, 1)
                if b >= 1:
                    pe.wait_ge(q_exp, b)
                    pe.wait_ge(v_copy, b)
                for t in range(LT):
                    last = nc.tensor.matmul(ps_qv[t // 2][:, (t % 2) * 256:(t % 2 + 1) * 256],
                                            xnT[:, b * L + t * P:b * L + (t + 1) * P],
                                            wqv[:, :, :].rearrange("p a d -> p (a d)"), start=True, stop=True)
                last.then_inc(qv_mm, 1)

            pe.wait_ge(w_in, 16 * 7)
            project(0)
            for b in range(B):
                pe.wait_ge(k_exp, b + 1)
                if b >= 1:
                    pe.wait_ge(k_copied, b)
                for t in range(LT):
                    last = nc.tensor.transpose(ps_kT[:, t * P:(t + 1) * P], ek[:, t * P:(t + 1) * P], ident[:, :])
                last.then_inc(k_turned, 1)
                pe.wait_ge(q_exp, b + 1)
                if b >= 1:
                    pe.wait_ge(q_copied, b)
                for t in range(LT):
                    last = nc.tensor.transpose(ps_qT[:, t * P:(t + 1) * P], eq[:, t, :], ident[:, :])
                last.then_inc(q_turned, 1)
                if b + 1 < B:
                    project(b + 1)
                pe.wait_ge(k_copied, b + 1)
                pe.wait_ge(v_copy, b + 1)
                if b >= 1:
                    pe.wait_ge(cw_copied, b)
                for t in range(LT):
                    last = nc.tensor.matmul(ps_c[:, 0:P], v[:, t, :], ekT[:, t, :], start=(t == 0), stop=(t == LT - 1))
                last.then_inc(ctx_mm, 1)
                pe.wait_ge(ctx_copied, b + 1)
                nc.tensor.matmul(ps_c[:, P:2 * P], ctxT[:, :], wo[:, :], start=True, stop=True).then_inc(cw_mm, 1)
                pe.wait_ge(cw_copied, b + 1)
                pe.wait_ge(q_copied, b + 1)
                if b >= 1:
                    pe.wait_ge(out_read, b)
                for t in range(LT):
                    last = nc.tensor.matmul(ps_o[:, t * P:(t + 1) * P], eqT[:, t * P:(t + 1) * P], cw[:, :],
                                            start=True, stop=True)
                last.then_inc(out_mm, 1)

        @block.scalar
        def _(act):
            for b in range(B):
                act.wait_ge(k_max, b + 1)
                if b >= 1:
                    act.wait_ge(k_turned, b)
                    act.wait_ge(cw_copied, b)
                nc.scalar.activation(ek[:, :], ps_k[:, :], ACT.Exp, bias=neg_kmax[:, 0:1],
                                     accum_out=ksum[:, 0:1]).then_inc(k_exp, 1)
                act.wait_ge(qv_mm, b + 1)
                act.wait_ge(q_max, b + 1)
                if b >= 1:
                    act.wait_ge(ctx_mm, b)
                for i in range(2):
                    last = nc.scalar.copy(v[:, 2 * i:2 * i + 2, :],
                                          ps_qv[i][:, :].rearrange("p (t a d) -> p t a d", t=2, a=2)[:, :, 1, :])
                last.then_inc(v_copy, 1)
                if b >= 1:
                    act.wait_ge(q_turned, b)
                    act.wait_ge(out_read, b)
                for t in range(LT):
                    last = nc.scalar.activation(eq[:, t, :], ps_qv[t // 2][:, (t % 2) * 256:(t % 2) * 256 + P], ACT.Exp,
                                                bias=neg_qmax[:, t:t + 1], accum_out=qsum[:, t:t + 1])
                last.then_inc(q_exp, 1)
                act.wait_ge(q_turned, b + 1)
                if b >= 1:
                    act.wait_ge(out_mm, b)
                nc.scalar.copy(eqT[:, :], ps_qT[:, :]).then_inc(q_copied, 1)
            act.wait_ge(var_ready, 1)
            nc.scalar.activation(rstd[:, :], rstd[:, :], ACT.Sqrt).then_inc(std_ready, 1)

        @block.vector
        def _(dve):
            link = Chain(dve, dve_done)

            def row(i):
                return rows[:, i:i + 1, :].broadcast_to([P, LT, D])

            def maxima(b):
                dve.wait_ge(k_mm, b + 1)
                nc.vector.tensor_reduce(neg_kmax[:, :], ps_k[:, :], AX_X, ALU.max, negate=True).then_inc(k_max, 1)
                dve.wait_ge(qv_mm, b + 1)
                for i in range(2):
                    last = nc.vector.tensor_reduce(neg_qmax[:, 2 * i:2 * i + 2],
                                                   ps_qv[i][:, :].rearrange("p (t a d) -> p t a d", t=2, a=2)[:, :, 0, :],
                                                   AX_X, ALU.max, negate=True)
                last.then_inc(q_max, 1)

            dve.wait_ge(w_in, 16 * 7)
            maxima(0)
            for b in range(B):
                dve.wait_ge(k_turned, b + 1)
                if b >= 1:
                    dve.wait_ge(ctx_mm, b)
                nc.vector.tensor_copy(ekT[:, :, :].rearrange("p t d -> p (t d)"), ps_kT[:, :]).then_inc(k_copied, 1)
                link(nc.vector.reciprocal(rk[:, :], ksum[:, :]))
                dve.wait_ge(q_exp, b + 1)
                link(nc.vector.reciprocal(rq[:, :], qsum[:, :]))
                if b + 1 < B:
                    maxima(b + 1)
                dve.wait_ge(ctx_mm, b + 1)
                if b >= 1:
                    dve.wait_ge(cw_mm, b)
                nc.vector.tensor_copy(ctxT[:, :], ps_c[:, 0:P]).then_inc(ctx_copied, 1)
                dve.wait_ge(cw_mm, b + 1)
                if b >= 1:
                    dve.wait_ge(out_mm, b)
                nc.vector.tensor_scalar(cw[:, :], ps_c[:, P:2 * P], rk[:, 0:1], float(D) ** -0.5, ALU.mult,
                                        ALU.mult).then_inc(cw_copied, 1)
                dve.wait_ge(out_mm, b + 1)
                y = s[:, b * LT:(b + 1) * LT, :]
                for t in range(LT):
                    last = nc.vector.scalar_tensor_tensor(out=y[:, t, :], in0=ps_o[:, t * P:(t + 1) * P],
                                                          scalar=rq[:, t:t + 1], in1=xn[:, b * LT + t, :],
                                                          op0=ALU.mult, op1=ALU.add)
                last.then_inc(out_read, 1)
                dve.wait_ge(out_read, b + 1)
                link(nc.vector.tensor_tensor(y, y, row(0), ALU.add))
                for t in range(LT):
                    last = nc.vector.bn_stats(stats[:, t, :], y[:, t, :])
                link(last)
                for t in range(LT):
                    last = nc.vector.bn_aggr(mv[:, b * LT + t, :], stats[:, t, :])
                link(last)
            nc.vector.tensor_scalar(rstd[:, :], mv[:, :, 1], EPS, None, ALU.add).then_inc(var_ready, 1)
            dve.wait_ge(std_ready, 1)
            link(nc.vector.reciprocal(rstd[:, :], rstd[:, :]))
            for b in range(B):
                y = s[:, b * LT:(b + 1) * LT, :]
                for t in range(b * LT, (b + 1) * LT):
                    last = nc.vector.tensor_scalar(s[:, t, :], s[:, t, :], mv[:, t, 0:1], rstd[:, t:t + 1],
                                                   ALU.subtract, ALU.mult)
                link(last)
                link(nc.vector.tensor_tensor(y, y, row(1), ALU.mult))
                link(nc.vector.tensor_tensor(y, y, row(2), ALU.add))


def gate(nc, name, xnT, wg_dram, capacity, cwT_dram, const, bank):
    with ExitStack() as ctx:
        sb, sem = tensors(nc, ctx)
        wg = sb(name + "wg", [P, E])
        logit = sb(name + "logit", [P, NT, E])
        top = sb(name + "top", [P, NT, 8])
        idx = sb(name + "idx", [P, NT, 8], U32)
        idxf = sb(name + "idxf", [P, 2, NT])
        oh = sb(name + "oh", [P, 2, E, NT])
        wt = sb(name + "wt", [P, 2, NT])
        gap = sb(name + "gap", [P, NT])
        cw = sb(name + "cw", [P, E, NT])
        cw2 = sb(name + "cw2", [P, E, NT])
        cwT = sb(name + "cwT", [P, 2, P])
        totals = sb(name + "totals", [P, 2, E, NT])
        before = sb(name + "before", [P, 2, E, NT])
        w_in, logits_mm, oh_ready = sem(name + "w_in"), sem(name + "logits_mm"), sem(name + "oh_ready")
        gap_ready, gap_exp, dve_done = sem(name + "gap_ready"), sem(name + "gap_exp"), sem(name + "dve_done")
        ranks_mm, cw_ready, cw_turned = sem(name + "ranks_mm"), sem(name + "cw_ready"), sem(name + "cw_turned")
        cw_copied, cw_out = sem(name + "cw_copied"), sem(name + "cw_out")
        block = ctx.enter_context(nc.Block())
        iota8, ones, upper, ident = const["iota8"], const["ones"], const["upper"], const["ident"]

        @block.sync
        def _(sp):
            sp.dma_start(wg[:, :], wg_dram).then_inc(w_in, 16)
            sp.wait_ge(cw_copied, 1)
            for h in range(2):
                sp.dma_start(cwT_dram.rearrange("(h e) (t p) -> h (e t) p", h=2, p=P)[h],
                             cwT[:, h, :]).then_inc(cw_out, 16)
            sp.wait_ge(cw_out, 32)

        @block.tensor
        def _(pe):
            pe.wait_ge(w_in, 16)
            for t in range(NT):
                last = nc.tensor.matmul(bank[0][:, t * E:(t + 1) * E], xnT[:, t * P:(t + 1) * P], wg[:, :],
                                        start=True, stop=True)
            last.then_inc(logits_mm, 1)
            if capacity:
                pe.wait_ge(oh_ready, 1)
                ohf = oh[:, :, :, :].rearrange("p k e t -> p (k e t)")
                nc.tensor.matmul(bank[1][:, :], upper[:, :], ohf, start=True, stop=True)
                nc.tensor.matmul(bank[2][:, :], ones[:, :], ohf, start=True, stop=True).then_inc(ranks_mm, 1)
            pe.wait_ge(cw_ready, 1)
            for h in range(2):
                last = nc.tensor.transpose(bank[3][:, h * P:(h + 1) * P],
                                           cw[:, h * 4:(h + 1) * 4, :].rearrange("p e t -> p (e t)"), ident[:, :])
            last.then_inc(cw_turned, 1)

        @block.scalar
        def _(act):
            act.wait_ge(gap_ready, 1)
            nc.scalar.activation(gap[:, :], gap[:, :], ACT.Exp).then_inc(gap_exp, 1)

        @block.vector
        def _(dve):
            link = Chain(dve, dve_done)
            dve.wait_ge(logits_mm, 1)
            link(nc.vector.tensor_copy(logit[:, :, :].rearrange("p t e -> p (t e)"), bank[0][:, 0:NT * E]))
            for t in range(NT):
                last = nc.vector.max(top[:, t, :], logit[:, t, :])
            link(last)
            for t in range(NT):
                last = nc.vector.max_index(idx[:, t, :], top[:, t, :], logit[:, t, :])
            link(last)
            nc.vector.tensor_tensor(gap[:, :], top[:, :, 1], top[:, :, 0], ALU.subtract).then_inc(gap_ready, 1)
            link(nc.vector.tensor_copy(idxf[:, :, :], idx[:, :, 0:2].rearrange("p t k -> p k t")))
            for k in range(2):
                last = nc.vector.tensor_tensor(oh[:, k, :, :], iota8[:, :].rearrange("p (e a) -> p e a", a=1).broadcast_to([P, E, NT]),
                                               idxf[:, k:k + 1, :].broadcast_to([P, E, NT]), ALU.is_equal)
            last.then_inc(oh_ready, 1)
            dve.wait_ge(oh_ready, 1)
            dve.wait_ge(gap_exp, 1)
            link(nc.vector.tensor_scalar(wt[:, 1, :], gap[:, :], 1.0, None, ALU.add))
            link(nc.vector.reciprocal(wt[:, 0, :], wt[:, 1, :]))
            link(nc.vector.tensor_tensor(wt[:, 1, :], gap[:, :], wt[:, 0, :], ALU.mult))
            if capacity:
                flat = "p k e t -> p (k e t)"
                dve.wait_ge(ranks_mm, 1)
                link(nc.vector.tensor_copy(totals[:, :, :, :].rearrange(flat), bank[2][:, :]))
                for k in range(2):
                    for e in range(E):
                        last = nc.vector.tensor_tensor_scan(before[:, k, e, :], ones[:, 0:NT], totals[:, k, e, :],
                                                            0.0 if k == 0 else before[:, 0, e, NT - 1:NT],
                                                            ALU.mult, ALU.add)
                    link(last)
                link(nc.vector.tensor_tensor(before[:, :, :, :], before[:, :, :, :], totals[:, :, :, :], ALU.subtract))
                link(nc.vector.tensor_tensor(before[:, :, :, :].rearrange(flat), before[:, :, :, :].rearrange(flat), bank[1][:, :], ALU.add))
                link(nc.vector.scalar_tensor_tensor(out=oh[:, :, :, :].rearrange(flat), in0=before[:, :, :, :].rearrange(flat),
                                                    scalar=float(capacity), in1=oh[:, :, :, :].rearrange(flat),
                                                    op0=ALU.is_lt, op1=ALU.mult))
            link(nc.vector.tensor_tensor(cw2[:, :, :], oh[:, 0, :, :], wt[:, 0:1, :].broadcast_to([P, E, NT]), ALU.mult))
            link(nc.vector.tensor_tensor(cw[:, :, :], oh[:, 1, :, :], wt[:, 1:2, :].broadcast_to([P, E, NT]), ALU.mult))
            nc.vector.tensor_tensor(cw[:, :, :], cw[:, :, :], cw2[:, :, :], ALU.add).then_inc(cw_ready, 1)
            dve.wait_ge(cw_turned, 1)
            nc.vector.tensor_copy(cwT[:, :, :].rearrange("p h q -> p (h q)"), bank[3][:, 0:2 * P]).then_inc(cw_copied, 1)


def experts(nc, name, xnT, acc, w1_dram, w2_dram, b1_dram, b2_dram, cwT_dram, bank):
    NC = T // L
    with ExitStack() as ctx:
        sb, sem = tensors(nc, ctx)
        w1 = [sb(f"{name}w1_{i}", [P, H]) for i in range(2)]
        w2 = [sb(f"{name}w2_{i}", [P, HC, D]) for i in range(2)]
        b1 = [sb(f"{name}b1_{i}", [P, HC]) for i in range(2)]
        cwb = [sb(f"{name}cwb_{i}", [P, T]) for i in range(2)]
        b2 = sb(name + "b2", [E, D])
        cwT = sb(name + "cwT8", [E, T])
        h = [sb(f"{name}h{i}", [P, HC, L]) for i in range(2)]
        term = sb(name + "term", [P, 2, L])
        w_in = [sem(f"{name}w_in{i}") for i in range(2)]
        b2_in, up_mm, gelu_done = sem(name + "b2_in"), sem(name + "up_mm"), sem(name + "gelu_done")
        down_mm, term_done, acc_done = sem(name + "down_mm"), sem(name + "term_done"), sem(name + "acc_done")
        bias_mm, acc_set = sem(name + "bias_mm"), sem(name + "acc_set")
        block = ctx.enter_context(nc.Block())
        n_loads = 3 + (b1_dram is not None)

        def landed(eng, i, pair):
            eng.wait_ge(w_in[i], (pair + 1) * 16 * n_loads)

        @block.sync
        def _(sp):
            def load(pair, i):
                e = pair * 2 + i
                sp.dma_start(w1[i][:, :], w1_dram[bass.ds(e, 1)].rearrange("a d h -> (a d) h")).then_inc(w_in[i], 16)
                if b1_dram is not None:
                    sp.dma_start(b1[i][:, :], b1_dram[bass.ds(e, 1)].rearrange("a p c -> (a p) c")).then_inc(w_in[i], 16)
                sp.dma_start(w2[i][:, :, :], w2_dram[bass.ds(e, 1)].rearrange("a (c p) d -> p (a c) d", p=P)).then_inc(w_in[i], 16)
                sp.dma_start(cwb[i][:, :], cwT_dram[bass.ds(e, 1), :].broadcast_to([P, T])).then_inc(w_in[i], 16)

            load(0, 0)
            if b2_dram is not None:
                sp.dma_start(b2[:, :], b2_dram).then_inc(b2_in, 16)
                sp.dma_start(cwT[:, :], cwT_dram).then_inc(b2_in, 16)
            load(0, 1)
            with sp.Fori(1, E // 2) as pair:
                for i in range(2):
                    sp.wait_ge(down_mm, (pair * 2 + i - 1) * NC)
                    sp.wait_ge(term_done, (pair * 2 + i - 1) * NC)
                    load(pair, i)

        @block.tensor
        def _(pe):
            def up(pair, i, c, first):
                k = (pair * 2 + i) * NC + c
                if c == 0:
                    landed(pe, i, pair)
                for hc in range(HC):
                    if not first:
                        pe.wait_ge(gelu_done, k * HC + (hc + 1 - HC))
                    nc.tensor.matmul(bank[hc][:, :], w1[i][:, hc * P:(hc + 1) * P], xnT[:, c * L:(c + 1) * L],
                                     start=True, stop=True).then_inc(up_mm, 1)

            def down(pair, i, c, first):
                k = (pair * 2 + i) * NC + c
                pe.wait_ge(gelu_done, k * HC + HC)
                if not first:
                    pe.wait_ge(term_done, k - 1)
                for hc in range(HC):
                    last = nc.tensor.matmul(bank[4 + c % 2][:, :], w2[i][:, hc, :], h[c % 2][:, hc, :],
                                            start=(hc == 0), stop=(hc == HC - 1))
                last.then_inc(down_mm, 1)

            def step(pair, i, c, peeled):
                up(pair, i, c, peeled and i == 0 and c == 0)
                if c:
                    down(pair, i, c - 1, peeled and i == 0 and c < 3)
                elif i:
                    down(pair, 0, NC - 1, False)
                elif not peeled:
                    down(pair - 1, 1, NC - 1, False)

            if b2_dram is not None:
                pe.wait_ge(b2_in, 32)
                for c in range(NC):
                    if c >= 2:
                        pe.wait_ge(acc_set, c - 1)
                    nc.tensor.matmul(bank[6 + c % 2][:, :], b2[:, :], cwT[:, c * L:(c + 1) * L],
                                     start=True, stop=True).then_inc(bias_mm, 1)
            for i in range(2):
                for c in range(NC):
                    step(0, i, c, True)
            with pe.Fori(1, E // 2) as pair:
                for i in range(2):
                    for c in range(NC):
                        step(pair, i, c, False)
            down(E // 2 - 1, 1, NC - 1, False)

        @block.scalar
        def _(act):
            def step(pair, i, c, first):
                k = (pair * 2 + i) * NC + c
                if c == 0 and b1_dram is not None:
                    landed(act, i, pair)
                if not first:
                    act.wait_ge(down_mm, k - 1)
                for hc in range(HC):
                    act.wait_ge(up_mm, k * HC + (hc + 1))
                    bias = b1[i][:, hc:hc + 1] if b1_dram is not None else 0.0
                    nc.scalar.activation(h[c % 2][:, hc, :], bank[hc][:, :], ACT.Gelu, bias=bias).then_inc(gelu_done, 1)

            for i in range(2):
                for c in range(NC):
                    step(0, i, c, i == 0 and c < 2)
            with act.Fori(1, E // 2) as pair:
                for i in range(2):
                    for c in range(NC):
                        step(pair, i, c, False)

        @block.vector
        def _(dve):
            def weigh(pair, i, c, first):
                k = (pair * 2 + i) * NC + c
                if c == 0:
                    landed(dve, i, pair)
                if not first:
                    dve.wait_ge(acc_done, k - 1)
                dve.wait_ge(down_mm, k + 1)
                nc.vector.tensor_tensor(term[:, c % 2, :], bank[4 + c % 2][:, :], cwb[i][:, c * L:(c + 1) * L],
                                        ALU.mult).then_inc(term_done, 1)

            def add(pair, i, c):
                k = (pair * 2 + i) * NC + c
                dve.wait_ge(term_done, k + 1)
                nc.vector.tensor_tensor(acc[:, c * L:(c + 1) * L], acc[:, c * L:(c + 1) * L], term[:, c % 2, :],
                                        ALU.add).then_inc(acc_done, 1)

            def step(pair, i, c, peeled):
                weigh(pair, i, c, peeled and i == 0 and c < 2)
                if c:
                    add(pair, i, c - 1)
                elif i:
                    add(pair, 0, NC - 1)
                elif not peeled:
                    add(pair - 1, 1, NC - 1)

            if b2_dram is None:
                nc.vector.memset(acc[:, :], 0.0).then_inc(acc_set, NC)
            for c in range(NC if b2_dram is not None else 0):
                dve.wait_ge(bias_mm, c + 1)
                nc.vector.tensor_copy(acc[:, c * L:(c + 1) * L], bank[6 + c % 2][:, :]).then_inc(acc_set, 1)
            dve.wait_ge(acc_set, NC)
            for i in range(2):
                for c in range(NC):
                    step(0, i, c, True)
            with dve.Fori(1, E // 2) as pair:
                for i in range(2):
                    for c in range(NC):
                        step(pair, i, c, False)
            add(E // 2 - 1, 1, NC - 1)


def combine(nc, name, x, s, acc, out, out_dram, ident, bank):
    with ExitStack() as ctx:
        sb, sem = tensors(nc, ctx)
        g = sb(name + "g", [P, 2, LT, P])
        turned, silu_done, prod_done, done = sem(name + "turned"), sem(name + "silu"), sem(name + "prod"), sem(name + "done")
        stored = sem(name + "stored")
        block = ctx.enter_context(nc.Block())

        @block.tensor
        def _(pe):
            for b in range(B):
                if b >= 2:
                    pe.wait_ge(silu_done, b - 1)
                for t in range(LT):
                    last = nc.tensor.transpose(bank[b % 2][:, t * P:(t + 1) * P],
                                               acc[:, (b * LT + t) * P:(b * LT + t + 1) * P], ident[:, :])
                last.then_inc(turned, 1)

        @block.scalar
        def _(act):
            for b in range(B):
                act.wait_ge(turned, b + 1)
                if b >= 2:
                    act.wait_ge(done, b - 1)
                nc.scalar.activation(g[:, b % 2, :, :].rearrange("p t d -> p (t d)"), bank[b % 2][:, :],
                                     ACT.Silu).then_inc(silu_done, 1)

        @block.vector
        def _(dve):
            for b in range(B):
                ts = slice(b * LT, (b + 1) * LT)
                dve.wait_ge(silu_done, b + 1)
                nc.vector.tensor_tensor(g[:, b % 2, :, :], g[:, b % 2, :, :], s[:, ts, :], ALU.mult).then_inc(prod_done, 1)
                dve.wait_ge(prod_done, b + 1)
                nc.vector.tensor_tensor(out[:, ts, :], g[:, b % 2, :, :], x[:, ts, :], ALU.add).then_inc(done, 1)

        @block.sync
        def _(sp):
            if out_dram is not None:
                for b in range(B):
                    sp.wait_ge(done, b + 1)
                    sp.dma_start(out_dram[b].rearrange("(t p) d -> p t d", p=P),
                                 out[:, b * LT:(b + 1) * LT, :]).then_inc(stored, 16)
                sp.wait_ge(stored, 16 * B)


def project_qkv(nc, xnT, q, k, w, vT_dram, v_heads):
    bank = w["bank"]
    with ExitStack() as ctx:
        sb, sem = tensors(nc, ctx)
        wT, wsT = sb("wqkvT", [P, 3 * D]), sb("wswapT", [P, 2 * D])
        bias = sb("qkv_bias", [P, 5])
        rot = sb("rot", [P, 2, L])
        part = sb("rot_part", [P, 2, L])
        v = sb("v_chunk", [P, 2, L])
        w_in, mm, rotated = sem("qkv_w_in"), sem("qkv_mm"), sem("rotated")
        part_done, v_done, v_out, v_in = sem("part_done"), sem("v_done"), [sem(f"v_out{i}") for i in range(2)], sem("v_in")
        block = ctx.enter_context(nc.Block())

        @block.sync
        def _(sp):
            sp.dma_start(wT[:, :], w["wqkvT"]).then_inc(w_in, 16)
            sp.dma_start(wsT[:, :], w["wswapT"]).then_inc(w_in, 16)
            sp.dma_start(bias[:, :], w["qkv_bias"]).then_inc(w_in, 16)
            sp.dma_start(rot[:, :, :], w["rot"]).then_inc(w_in, 16)
            for b in range(B):
                sp.wait_ge(v_done, b + 1)
                sp.dma_start(vT_dram[:, b * L:(b + 1) * L], v[:, b % 2, :]).then_inc(v_out[b % 2], 16)
            for i in range(2):
                sp.wait_ge(v_out[i], 16 * (B // 2))
            for b in range(B):
                sp.dma_start(v_heads[b * NH:(b + 1) * NH, :, :],
                             vT_dram.rearrange("(h d) (b t) -> b h d t", h=NH, b=B)[b]).then_inc(v_in, 16)
            sp.wait_ge(v_in, 16 * B)

        @block.tensor
        def _(pe):
            pe.wait_ge(w_in, 64)
            for b in range(B):
                rhs = xnT[:, b * L:(b + 1) * L]
                if b >= 1:
                    pe.wait_ge(rotated, 2 * b)
                    pe.wait_ge(v_done, b)
                for i in range(5):
                    lhsT = wT[:, i * D:(i + 1) * D] if i < 3 else wsT[:, (i - 3) * D:(i - 2) * D]
                    nc.tensor.matmul(bank[i][:, :], lhsT, rhs, start=True, stop=True).then_inc(mm, 1)

        @block.scalar
        def _(act):
            act.wait_ge(w_in, 64)
            for b in range(B):
                act.wait_ge(mm, 5 * b + 3)
                if b >= 2:
                    act.wait_ge(v_out[b % 2], 16 * (b // 2))
                nc.scalar.activation(v[:, b % 2, :], bank[2][:, :], ACT.Identity, bias=bias[:, 2:3]).then_inc(v_done, 1)

        @block.vector
        def _(dve):
            dve.wait_ge(w_in, 64)
            for b in range(B):
                dve.wait_ge(mm, 5 * b + 5)
                for i, dst in enumerate((q, k)):
                    d = dst[:, b * L:(b + 1) * L]
                    nc.vector.scalar_tensor_tensor(out=d, in0=bank[i][:, :], scalar=bias[:, i:i + 1], in1=rot[:, 0, :],
                                                   op0=ALU.add, op1=ALU.mult)
                    if b or i:
                        dve.wait_ge(rotated, 2 * b + i)
                    nc.vector.scalar_tensor_tensor(out=part[:, i, :], in0=bank[3 + i][:, :], scalar=bias[:, 3 + i:4 + i],
                                                   in1=rot[:, 1, :], op0=ALU.add, op1=ALU.mult).then_inc(part_done, 1)
                    dve.wait_ge(part_done, 2 * b + i + 1)
                    nc.vector.tensor_tensor(d, d, part[:, i, :], ALU.add).then_inc(rotated, 1)


def head_order(b):
    for v in range(4):
        for g in range(4):
            yield b * NH + g * 4 + v, v, g


def solve_attention(nc, q, k, A, w, a_dram):
    bank, ident = w["bank"], w["ident"]
    scale = float(HD) ** -0.5
    with ExitStack() as ctx:
        sb, sem = tensors(nc, ctx)
        assert SB * SB <= 4 * B * P
        shared = sb("Qm_Pn", [P, 4 * B * P])
        Qm = shared[:, :].rearrange("p (v b q) -> p v b q", v=4, b=B)
        Pn = shared[:, 0:SB * SB].rearrange("p (i j) -> p i j", i=SB)
        Ed = sb("Ed", [P, BH, P])
        Eoff = sb("Eoff", [P, 4, 3, P])
        Apos = sb("Apos", [P, 4, BH, HD + 1])
        R = sb("R", [P, BH, HD + 1])
        Rb = sb("Rb", [P, HD, P])
        rZ = sb("rZ", [P, P])
        pd = sb("pd", [P, SB])
        prod = sb("prod", [P, HD, SB])
        mx = sb("mx", [P, BH])
        mxh, mxl = sb("mxh", [P, BH], BF16), sb("mxl", [P, BH], BF16)
        mxT = sb("mxT", [P, 2, P], BF16)
        keep = sb("keep", [P, 4])
        masks = sb("masks", [P, 2, P], BF16)
        identb, nidentb = sb("identb", [P, P], BF16), sb("nidentb", [P, P], BF16)
        ones9 = sb("ones9", [P, HD + 1])
        c_in, set_done = sem("solve_c_in"), sem("set_done")
        with nc.Block() as block:
            @block.sync
            def _(sp):
                sp.dma_start(keep[:, :], w["keep"]).then_inc(c_in, 16)
                sp.dma_start(Rb[:, 0:2, :], w["masks"]).then_inc(c_in, 16)
                sp.wait_ge(c_in, 32)

            @block.vector
            def _(dve):
                nc.vector.tensor_copy(identb[:, :], ident[:, :])
                nc.vector.tensor_scalar(nidentb[:, :], ident[:, :], -1.0, None, ALU.mult)
                dve.wait_ge(c_in, 32)
                nc.vector.tensor_copy(masks[:, :, :], Rb[:, 0:2, :])

            @block.gpsimd
            def _(pool):
                nc.gpsimd.memset(Apos[:, :, :, HD:HD + 1], 1.0)
                nc.gpsimd.memset(ones9[:, 0:HD], 0.0)
                nc.gpsimd.memset(ones9[:, HD:HD + 1], 1.0).then_inc(set_done, 1)
                pool.wait_ge(set_done, 1)

        for I in range(LT):
            row_maxima(nc, I, q, k, Qm, mx, mxh, mxl, mxT, keep, masks, identb, bank)
            exp_and_sums(nc, I, k, Qm, mxT, masks, identb, nidentb, Ed, Eoff, Apos, ones9, R, bank, scale)
            for s in range(NSUB):
                solve_block(nc, I, s, Ed, R, Rb, rZ, Pn, pd, prod, A, Apos, ident, bank)
        a_out = sem("a_out")
        with nc.Block() as block:
            @block.sync
            def _(sp):
                sp.dma_start(a_dram, A[:, :, :]).then_inc(a_out, 16)
                sp.wait_ge(a_out, 16)


def row_maxima(nc, I, q, k, Qm, mx, mxh, mxl, mxT, keep, masks, identb, bank):
    with ExitStack() as ctx:
        sb, sem = tensors(nc, ctx)
        masked, logit_mm, max_done = sem("q_masked"), sem("max_logit_mm"), sem("max_done")
        hi_done, lo_done, max_turned, turned_read = sem("hi_done"), sem("lo_done"), sem("max_turned"), sem("turned_read")
        block = ctx.enter_context(nc.Block())
        keys = (I + 1) * P

        @block.tensor
        def _(pe):
            pe.wait_ge(masked, 4)
            for b in range(B):
                order = list(head_order(b))
                for v in range(4):
                    n = b * 4 + v
                    if n >= 2:
                        pe.wait_ge(max_done, 4 * (n - 1))
                    for _, _, g in order[4 * v:4 * v + 4]:
                        r = slice(32 * g, 32 * g + 32)
                        nc.tensor.matmul(bank[4 * (n % 2) + g][:, 0:keys], Qm[r, v, b, :], k[r, b * L:b * L + keys],
                                         start=True, stop=False, skip_group_check=True)
                    for g in range(4):
                        last = nc.tensor.matmul(bank[4 * (n % 2) + g][:, I * P:keys], identb[:, :], masks[:, 0, :],
                                                start=False, stop=True, skip_group_check=True)
                    last.then_inc(logit_mm, 1)
            pe.wait_ge(lo_done, 1)
            pe.wait_ge(max_done, BH)
            psT = bank[0][:, :].bitcast(BF16)
            nc.tensor.transpose(psT[:, 0:P], mxh[:, :], identb[:, :])
            nc.tensor.transpose(psT[:, P:2 * P], mxl[:, :], identb[:, :]).then_inc(max_turned, 1)

        @block.vector
        def _(dve):
            for v in range(4):
                nc.vector.tensor_scalar(Qm[:, v, :, :], q[:, :].rearrange("p (b t) -> p b t", b=B)[:, :, I * P:(I + 1) * P],
                                        keep[:, v:v + 1], None, ALU.mult).then_inc(masked, 1)
            for b in range(B):
                for i, (bh, v, g) in enumerate(head_order(b)):
                    n = b * 4 + v
                    dve.wait_ge(logit_mm, n + 1)
                    nc.vector.tensor_reduce(mx[:, bh:bh + 1], bank[4 * (n % 2) + g][:, 0:keys], AX_X,
                                            ALU.max).then_inc(max_done, 1)
            dve.wait_ge(max_done, BH)
            nc.vector.tensor_copy(mxh[:, :], mx[:, :]).then_inc(hi_done, 1)
            dve.wait_ge(hi_done, 1)
            nc.vector.tensor_tensor(mxl[:, :], mx[:, :], mxh[:, :], ALU.subtract).then_inc(lo_done, 1)
            dve.wait_ge(max_turned, 1)
            nc.vector.tensor_copy(mxT[:, :, :].rearrange("p a q -> p (a q)"),
                                  bank[0][:, :].bitcast(BF16)[:, 0:2 * P]).then_inc(turned_read, 1)


def exp_and_sums(nc, I, k, Qm, mxT, masks, identb, nidentb, Ed, Eoff, Apos, ones9, R, bank, scale):
    with ExitStack() as ctx:
        sb, sem = tensors(nc, ctx)
        logit_mm, exp_done, sum_mm, sum_read = sem("exp_logit_mm"), sem("exp_done"), sem("sum_mm"), sem("sum_read")
        block = ctx.enter_context(nc.Block())
        keys = (I + 1) * P
        order = [(b,) + o for b in range(B) for o in head_order(b)]
        RING = 6

        @block.tensor
        def _(pe):
            def logits(n):
                pair = [(2 * n + j,) + order[2 * n + j] for j in range(2)]
                if 2 * n + 1 >= RING:
                    pe.wait_ge(exp_done, 2 * n + 2 - RING)
                for kk, b, bh, v, g in pair:
                    for i in range(2):
                        nc.tensor.matmul(bank[kk % RING][:, 0:keys], nidentb[:, bh:bh + 1].broadcast_to([P, P]),
                                         mxT[:, i:i + 1, :].broadcast_to([P, I + 1, P]), start=(i == 0), stop=False,
                                         skip_group_check=True)
                    nc.tensor.matmul(bank[kk % RING][:, I * P:keys], identb[:, :], masks[:, 1, :], start=False,
                                     stop=False, skip_group_check=True)
                for J in range(I + 1):
                    for kk, b, bh, v, g in pair:
                        r = slice(32 * g, 32 * g + 32)
                        last = nc.tensor.matmul(bank[kk % RING][:, J * P:(J + 1) * P],
                                                k[r, b * L + J * P:b * L + (J + 1) * P], Qm[r, v, b, :],
                                                start=False, stop=(J == I), skip_group_check=True)
                last.then_inc(logit_mm, 1)

            def sums(n):
                for kk in (2 * n, 2 * n + 1):
                    b, bh, v, g = order[kk]
                    h = bh % NH
                    pe.wait_ge(exp_done, kk + 1)
                    if kk % NH == 0 and b >= 2:
                        pe.wait_ge(sum_read, b - 1)
                    out = bank[6 + b % 2][:, h * (HD + 1):(h + 1) * (HD + 1)]
                    last = nc.tensor.matmul(out, Ed[:, bh, :], ones9[:, :], start=True, stop=(I == 0))
                    for J in range(I):
                        last = nc.tensor.matmul(out, Eoff[:, kk % 4, J, :], Apos[:, J, bh, :], start=False,
                                                stop=(J == I - 1))
                    last.then_inc(sum_mm, 1)

            for n in range(BH // 2):
                logits(n)
                if n >= 1:
                    sums(n - 1)
            sums(BH // 2 - 1)

        @block.scalar
        def _(act):
            for kk, (b, bh, v, g) in enumerate(order):
                act.wait_ge(logit_mm, kk // 2 + 1)
                if I:
                    if kk >= 4:
                        act.wait_ge(sum_mm, kk - 3)
                    nc.scalar.activation(Eoff[:, kk % 4, 0:I, :].rearrange("p j q -> p (j q)"),
                                         bank[kk % RING][:, 0:I * P], ACT.Exp, scale=scale)
                nc.scalar.activation(Ed[:, bh, :], bank[kk % RING][:, I * P:keys], ACT.Exp, scale=scale).then_inc(exp_done, 1)

        @block.vector
        def _(dve):
            for b in range(B):
                dve.wait_ge(sum_mm, NH * (b + 1))
                nc.vector.tensor_copy(R[:, b * NH:(b + 1) * NH, :].rearrange("p h d -> p (h d)"),
                                      bank[6 + b % 2][:, 0:NH * (HD + 1)]).then_inc(sum_read, 1)


def solve_block(nc, I, s, Ed, R, Rb, rZ, Pn, pd, prod, A, Apos, ident, bank):
    with ExitStack() as ctx:
        sb, sem = tensors(nc, ctx)
        upd_mm, upd_copied, sums_turned = sem("upd_mm"), sem("upd_copied"), sem("sums_turned")
        probs_turned, probs_read, dve_done = sem("probs_turned"), sem("probs_read"), sem("solve_dve")
        rz_done, solved, rows_turned, rows_copied = sem("rz_done"), sem("solved"), sem("rows_turned"), sem("rows_copied")
        block = ctx.enter_context(nc.Block())
        r0, t0 = s * SB, I * P + s * SB
        PER = 512 // SB
        NG = SB // PER
        upd = R[0:SB, :, 0:HD]

        @block.tensor
        def _(pe):
            if s == 0:
                for d in range(HD + 1):
                    last = nc.tensor.transpose(bank[d // 4][:, (d % 4) * P:(d % 4 + 1) * P], R[:, :, d], ident[:, :])
                last.then_inc(sums_turned, 1)
            else:
                for bh in range(BH):
                    last = nc.tensor.matmul(bank[bh // 64][0:SB, (bh % 64) * HD:(bh % 64 + 1) * HD],
                                            Ed[0:r0, bh, r0:r0 + SB], Apos[0:r0, I, bh, 0:HD], start=True, stop=True)
                last.then_inc(upd_mm, 1)
                pe.wait_ge(upd_copied, 1)
                for d in range(HD):
                    last = nc.tensor.transpose(bank[2][:, d * SB:(d + 1) * SB], upd[:, :, d], ident[0:SB, 0:SB])
                last.then_inc(sums_turned, 1)
            for n in range(NG):
                if n >= 4:
                    pe.wait_ge(probs_read, n - 3)
                for i in range(PER):
                    last = nc.tensor.transpose(bank[4 + n % 4][:, i * SB:(i + 1) * SB],
                                               Ed[r0:r0 + SB, :, r0 + n * PER + i], ident[r0:r0 + SB, r0:r0 + SB])
                last.then_inc(probs_turned, 1)
            pe.wait_ge(solved, 1)
            for d in range(HD):
                last = nc.tensor.transpose(bank[d // 4][0:r0 + SB, (d % 4) * P:(d % 4 + 1) * P],
                                           A[:, d, I * P:t0 + SB], ident[:, :])
            last.then_inc(rows_turned, 1)

        @block.scalar
        def _(act):
            if s:
                act.wait_ge(upd_mm, 1)
                for i in range(2):
                    last = nc.scalar.copy(upd[:, 64 * i:64 * i + 64, :], bank[i][0:SB, :].rearrange("p (b d) -> p b d", d=HD))
                last.then_inc(upd_copied, 1)
            act.wait_ge(rows_turned, 1)
            for i in range(2):
                last = nc.scalar.copy(Apos[0:r0 + SB, I, :, 4 * i:4 * i + 4].rearrange("p b d -> p d b"),
                                      bank[i][0:r0 + SB, :].rearrange("p (d b) -> p d b", d=4))
            last.then_inc(rows_copied, 1)

        @block.vector
        def _(dve):
            link = Chain(dve, dve_done)
            rows = A[:, :, t0:t0 + SB]
            dve.wait_ge(sums_turned, 1)
            if s == 0:
                link(nc.vector.reciprocal(rZ[:, :], bank[2][:, 0:P]))
                for i in range(2):
                    last = nc.vector.tensor_tensor(Rb[:, 4 * i:4 * i + 4, :], bank[i][:, :].rearrange("p (d q) -> p d q", d=4),
                                                   rZ[:, :].rearrange("p (a q) -> p a q", a=1).broadcast_to([P, 4, P]), ALU.mult)
                link(last)
            else:
                link(nc.vector.tensor_tensor(prod[:, :, :], bank[2][:, :].rearrange("p (d q) -> p d q", d=HD),
                                             rZ[:, r0:r0 + SB].rearrange("p (a q) -> p a q", a=1).broadcast_to([P, HD, SB]), ALU.mult))
                link(nc.vector.tensor_tensor(Rb[:, :, r0:r0 + SB], Rb[:, :, r0:r0 + SB], prod[:, :, :], ALU.add))
            for n in range(NG):
                dve.wait_ge(probs_turned, n + 1)
                z = rZ[:, r0 + n * PER:r0 + (n + 1) * PER].rearrange("p (i a) -> p i a", a=1).broadcast_to([P, PER, SB])
                nc.vector.tensor_tensor(Pn[:, n * PER:(n + 1) * PER, :],
                                        bank[4 + n % 4][:, :].rearrange("p (i j) -> p i j", i=PER), z,
                                        ALU.mult).then_inc(probs_read, 1)
            dve.wait_ge(probs_read, NG)
            diag = Pn.rearrange("p i j -> p (i j)")[:, ::SB + 1]
            link(nc.vector.tensor_copy(pd[:, :], diag))
            link(nc.vector.tensor_tensor(rows, rows, pd[:, :].rearrange("p (a q) -> p a q", a=1).broadcast_to([P, HD, SB]), ALU.mult))
            nc.vector.memset(diag, 1.0)
            link(nc.vector.tensor_tensor(rows, rows, Rb[:, :, r0:r0 + SB], ALU.add))
            for r in range(1, SB):
                n = r + 1
                link(nc.vector.tensor_tensor(prod[:, :, 0:n], A[:, :, t0:t0 + n],
                                             Pn[:, r:r + 1, 0:n].broadcast_to([P, HD, n]), ALU.mult))
                last = nc.vector.tensor_reduce(A[:, :, t0 + r], prod[:, :, 0:n], AX_X, ALU.add)
                if r < SB - 1:
                    link(last)
            last.then_inc(solved, 1)


def project_out(nc, s, w, a_dram):
    bank = w["bank"]
    with ExitStack() as ctx:
        sb, sem = tensors(nc, ctx)
        wdT, bd, aT = sb("wdT", [P, D]), sb("bd", [P, D]), sb("aT", [P, T])
        w_in, a_in, mm, read = sem("wd_in"), [sem(f"a_in{b}") for b in range(B)], sem("wd_mm"), sem("wd_read")
        block = ctx.enter_context(nc.Block())

        @block.sync
        def _(sp):
            sp.dma_start(wdT[:, :], w["wdT"]).then_inc(w_in, 16)
            sp.dma_start(bd[:, :], w["bd"].rearrange("(a d) -> a d", a=1).broadcast_to([P, D])).then_inc(w_in, 16)
            for b in range(B):
                sp.dma_start(aT[:, b * L:(b + 1) * L],
                             a_dram.rearrange("(b h) d t -> b (h d) t", b=B)[b]).then_inc(a_in[b], 16)

        @block.tensor
        def _(pe):
            pe.wait_ge(w_in, 32)
            for b in range(B):
                pe.wait_ge(a_in[b], 16)
                if b >= 2:
                    pe.wait_ge(read, b - 1)
                for t in range(LT):
                    last = nc.tensor.matmul(bank[b % 2][:, t * P:(t + 1) * P], aT[:, (b * LT + t) * P:(b * LT + t + 1) * P],
                                            wdT[:, :], start=True, stop=True)
                last.then_inc(mm, 1)

        @block.vector
        def _(dve):
            dve.wait_ge(w_in, 32)
            for b in range(B):
                dve.wait_ge(mm, b + 1)
                nc.vector.tensor_tensor(s[:, b * LT:(b + 1) * LT, :], bank[b % 2][:, :].rearrange("p (t d) -> p t d", t=LT),
                                        bd[:, :].rearrange("p (a d) -> p a d", a=1).broadcast_to([P, LT, D]),
                                        ALU.add).then_inc(read, 1)


def program(nc, w, cst, out, dbg=None):
    with ExitStack() as ctx:
        sb, sem = tensors(nc, ctx)
        bank = [ctx.enter_context(nc.psum_tensor(f"bank{i}", [P, 512], F32)) for i in range(8)]
        bankh = None
        cwT_dram = nc.dram_tensor("cwT_dram", (E, T), F32).ap()
        const = {n: sb(n + "_c", list(cst[n].shape)) for n in ("ident", "upper", "ones", "iota8")}
        c_in = sem("const_in")
        with nc.Block() as block:
            @block.sync
            def _(sp):
                for n, t in const.items():
                    sp.dma_start(t[:, :], cst[n]).then_inc(c_in, 16)
                sp.wait_ge(c_in, 16 * len(const))

        ident = const["ident"]
        x = sb("x", [P, NT, D])
        xnT = sb("xnT", [P, T])
        vT_dram = nc.dram_tensor("vT_dram", (P, T), F32).ap()
        a_dram = nc.dram_tensor("a_dram", (BH, HD, L), F32).ap()
        more = {**w, **cst, "bank": bank}
        with ExitStack() as layer:
            sb, _ = tensors(nc, layer)
            xn, s = sb("xn", [P, NT, D]), sb("s", [P, NT, D])
            normalise(nc, "n0_", w["L0_attn_x"], x, xn, xnT, ident, bank)
            linear_attention(nc, xn, xnT, s, {n: w["L0_attn_" + n] for n in ("Wq", "Wk", "Wv", "Wo", "bo", "gamma", "beta")},
                             ident, bank)
            gate(nc, "g0_", xnT, w["L0_rwT"], None, cwT_dram, const, bank)
            acc = sb("acc", [P, T])
            experts(nc, "e0_", xnT, acc, w["L0_w1T"], w["L0_w2T"], w["L0_b1T"], w["L0_ffn_b2"], cwT_dram, bank)
            combine(nc, "c0_", x, s, acc, x, None, ident, bank)
            normalise(nc, "n1_", None, x, xn, xnT, ident, bank)
        with ExitStack() as layer:
            sb, _ = tensors(nc, layer)
            A = sb("A", [P, HD, L])
            q, k = sb("q", [P, T]), sb("k", [P, T])
            project_qkv(nc, xnT, q, k, more, vT_dram, A)
            solve_attention(nc, q, k, A, {**more, "ident": ident}, a_dram)
        with ExitStack() as layer:
            sb, _ = tensors(nc, layer)
            s = sb("s1", [P, NT, D])
            project_out(nc, s, more, a_dram)
            gate(nc, "g1_", xnT, w["L1_ffn_w_g"], CAP, cwT_dram, const, bank)
            acc = sb("acc1", [P, T])
            experts(nc, "e1_", xnT, acc, w["L1_ffn_c_fc"], w["L1_ffn_c_proj"], None, None, cwT_dram, bank)
            combine(nc, "c1_", x, s, acc, x, out, ident, bank)


def _layouts(a):
    w = {n: a[n] for n in ("L0_attn_x", "L0_attn_Wq", "L0_attn_Wk", "L0_attn_Wv", "L0_attn_Wo", "L0_attn_bo",
                           "L0_attn_gamma", "L0_attn_beta", "L0_ffn_b2")}
    w["L0_rwT"] = a["L0_ffn_router_w"].T
    w["L0_w1T"] = a["L0_ffn_w1"].transpose(0, 2, 1)
    w["L0_w2T"] = a["L0_ffn_w2"].transpose(0, 2, 1)
    w["L0_b1T"] = a["L0_ffn_b1"].reshape(E, HC, P).transpose(0, 2, 1)
    for n in ("L1_ffn_w_g", "L1_ffn_c_fc", "L1_ffn_c_proj"):
        w[n] = a[n]
    swap = np.arange(D)
    swap[0::HD], swap[1::HD] = np.arange(1, D, HD), np.arange(0, D, HD)
    wq, wk, _ = a["L1_attn_Wqkv"].reshape(3, D, D)
    bq, bk, bv = a["L1_attn_bqkv"].reshape(3, D)
    w["wqkvT"] = a["L1_attn_Wqkv"].T
    w["wswapT"] = np.concatenate([wq[swap], wk[swap]]).T
    w["qkv_bias"] = np.stack([bq, bk, bv, bq[swap], bk[swap]], axis=1)
    w["wdT"] = a["L1_attn_Wd"].T
    w["bd"] = a["L1_attn_bd"]
    return w


def _constants():
    i = np.arange(P)
    t = np.arange(L, dtype=np.float32)
    rot = np.zeros((P, 2, L), np.float32)
    rot[:, 0], rot[0::HD, 0], rot[1::HD, 0] = 1.0, np.cos(t), np.cos(t)
    rot[0::HD, 1], rot[1::HD, 1] = -np.sin(t), np.sin(t)
    later = np.where(i[None, :] > i[:, None], BIG, 0.0)
    return {
        "rot": rot,
        "keep": (i[:, None] // HD % 4 == np.arange(4)).astype(np.float32),
        "masks": np.stack([later, later.T], axis=1).astype(np.float32),
        "ident": np.eye(P, dtype=np.float32),
        "upper": (i[:, None] < i[None, :]).astype(np.float32),
        "ones": np.ones((P, P), np.float32),
        "iota8": np.tile(np.arange(8, dtype=np.float32), (P, 1)),
    }


def kernel(**inputs):
    import concourse.bacc as _bacc
    from concourse import mybir as _mybir
    from concourse.bass_utils import run_bass_kernel_spmd as _run

    nc = _bacc.Bacc("TRN2", target_bir_lowering=False, num_devices=1)
    arrays = {}

    def dram(group):
        args = {}
        for name, a in group.items():
            a = np.ascontiguousarray(a)
            arrays[f"in_{name}_dram"] = a
            args[name] = nc.dram_tensor(f"in_{name}_dram", a.shape, _mybir.dt.from_np(a.dtype), kind="ExternalInput").ap()
        return args

    w = dram(_layouts({n: np.asarray(v) for n, v in inputs.items()}))
    cst = dram(_constants())
    out = nc.dram_tensor("out_0_dram", (B, L, D), F32, kind="ExternalOutput").ap()
    program(nc, w, cst, out)
    r = _run(nc, [arrays], core_ids=[0])
    return r.results[0]["out_0_dram"]
```

```python
from contextlib import ExitStack
from itertools import count

import concourse.bass as bass
import numpy as np
from concourse import mybir

P = 128
B, L, D = 8, 512, 128
T = B * L
NT = T // P
LT = L // P
E, H = 8, 512
HC = H // P
NH = 16
HD = D // NH
BH = B * NH
CAP = 1280
SB = 32
NSUB = P // SB
STEP_ROWS = 10
NSLOT = NH // 2
K_PARTS = (0, 1, 2, 0, 1, 0)
Q_PARTS = (0, 0, 0, 1, 1, 2)
ROWS = len(K_PARTS) * HD
EPS = 1e-5
BIG = -2.0 ** 100

F32 = mybir.dt.float32
BF16 = mybir.dt.bfloat16
U32 = mybir.dt.uint32
ALU = mybir.AluOpType
ACT = mybir.ActivationFunctionType
AX_X = mybir.AxisListType.X


STAGES = count()


class Chain:

    def __init__(self, eng, sem):
        self.eng, self.sem, self.n = eng, sem, 0

    def __call__(self, ins):
        self.n += 1
        ins.then_inc(self.sem, 1)
        self.eng.wait_ge(self.sem, self.n)


def tensors(nc, ctx):
    sems, stage = [], next(STAGES)

    def sb(name, shape, dt=F32):
        return ctx.enter_context(nc.sbuf_tensor(name, shape, dt))

    def sem(name):
        sems.append(nc.alloc_semaphore(f"{name}_{stage}"))
        return sems[-1]

    def clear():
        if sems:
            nc.clear_and_free_semaphores(sems)
            nc.all_engine_barrier()

    ctx.callback(clear)

    return sb, sem


def normalise(nc, name, x_dram, x, xn, xnT, ident, bank):
    G = LT
    with ExitStack() as ctx:
        sb, sem = tensors(nc, ctx)
        stats = sb(name + "stats", [P, NT, 6])
        mv = sb(name + "mv", [P, NT, 2])
        rstd = sb(name + "rstd", [P, NT])
        x_in = [sem(f"{name}x_in{g}") for g in range(B)]
        dve_done, xn_ready = sem(name + "dve_done"), sem(name + "xn_ready")
        turned, copied = sem(name + "turned"), sem(name + "copied")
        var_ready, std_ready = sem(name + "var_ready"), sem(name + "std_ready")
        block = ctx.enter_context(nc.Block())

        @block.sync
        def _(sp):
            if x_dram is not None:
                for g in range(B):
                    sp.dma_start(x[:, g * G:(g + 1) * G, :],
                                 x_dram[g].rearrange("(t p) d -> p t d", p=P)).then_inc(x_in[g], 16)

        @block.vector
        def _(dve):
            link = Chain(dve, dve_done)
            for g in range(B):
                s = slice(g * G, (g + 1) * G)
                if x_dram is not None:
                    dve.wait_ge(x_in[g], 16)
                for t in range(g * G, (g + 1) * G):
                    last = nc.vector.bn_stats(stats[:, t, :], x[:, t, :])
                link(last)
                for t in range(g * G, (g + 1) * G):
                    last = nc.vector.bn_aggr(mv[:, t, :], stats[:, t, :])
                link(last)
                nc.vector.tensor_scalar(rstd[:, s], mv[:, s, 1], EPS, None, ALU.add).then_inc(var_ready, 1)
            for g in range(B):
                dve.wait_ge(std_ready, g + 1)
                s = slice(g * G, (g + 1) * G)
                link(nc.vector.reciprocal(rstd[:, s], rstd[:, s]))
                for t in range(g * G, (g + 1) * G):
                    last = nc.vector.tensor_scalar(xn[:, t, :], x[:, t, :], mv[:, t, 0:1], rstd[:, t:t + 1],
                                                   ALU.subtract, ALU.mult)
                last.then_inc(xn_ready, 1)

        @block.tensor
        def _(pe):
            for g in range(B):
                pe.wait_ge(xn_ready, g + 1)
                if g >= 2:
                    pe.wait_ge(copied, g - 1)
                for t in range(G):
                    last = nc.tensor.transpose(bank[g % 2][:, t * P:(t + 1) * P], xn[:, g * G + t, :], ident[:, :])
                last.then_inc(turned, 1)

        @block.scalar
        def _(act):
            for g in range(B):
                act.wait_ge(var_ready, g + 1)
                nc.scalar.activation(rstd[:, g * G:(g + 1) * G], rstd[:, g * G:(g + 1) * G], ACT.Sqrt).then_inc(std_ready, 1)
            for g in range(B):
                act.wait_ge(turned, g + 1)
                nc.scalar.copy(xnT[:, g * L:(g + 1) * L], bank[g % 2][:, :]).then_inc(copied, 1)


def linear_attention(nc, xn, xnT, s, w, ident, bank):
    with ExitStack() as ctx:
        sb, sem = tensors(nc, ctx)
        wk, wqv, wo = sb("wk", [P, D]), sb("wqv", [P, 2, D]), sb("wo", [P, D])
        rows = sb("rows", [P, 3, D])
        ek, ekT = sb("ek", [P, L]), sb("ekT", [P, LT, P])
        eq, eqT = sb("eq", [P, LT, P]), sb("eqT", [P, L])
        v = sb("v", [P, LT, P])
        ctxT, cw = sb("ctxT", [P, P]), sb("cw", [P, P])
        neg_kmax, ksum, rk = sb("neg_kmax", [P, 1]), sb("ksum", [P, 1]), sb("rk", [P, 1])
        neg_qmax, qsum, rq = sb("neg_qmax", [P, LT]), sb("qsum", [P, LT]), sb("rq", [P, LT])
        stats, mv, rstd = sb("ystats", [P, LT, 6]), sb("ymv", [P, NT, 2]), sb("yrstd", [P, NT])
        w_in = sem("attn_w_in")
        k_mm, qv_mm, k_max, q_max = sem("k_mm"), sem("qv_mm"), sem("k_max"), sem("q_max")
        k_exp, q_exp, v_copy = sem("k_exp"), sem("q_exp"), sem("v_copy")
        k_turned, q_turned, k_copied, q_copied = sem("k_turned"), sem("q_turned"), sem("k_copied"), sem("q_copied")
        ctx_mm, ctx_copied, cw_mm, cw_copied = sem("ctx_mm"), sem("ctx_copied"), sem("cw_mm"), sem("cw_copied")
        var_ready, std_ready = sem("yvar_ready"), sem("ystd_ready")
        out_mm, out_read, dve_done = sem("out_mm"), sem("out_read"), sem("attn_dve_done")
        block = ctx.enter_context(nc.Block())
        ps_k, ps_qv, ps_kT, ps_qT, ps_c, ps_o = bank[0], (bank[1], bank[2]), bank[3], bank[4], bank[5], bank[6]

        @block.sync
        def _(sp):
            for dst, src in ((wk[:, :], w["Wk"]), (wqv[:, 0, :], w["Wq"]), (wqv[:, 1, :], w["Wv"]), (wo[:, :], w["Wo"])):
                sp.dma_start(dst, src).then_inc(w_in, 16)
            for i, n in enumerate(("bo", "gamma", "beta")):
                sp.dma_start(rows[:, i, :], w[n].rearrange("(a d) -> a d", a=1).broadcast_to([P, D])).then_inc(w_in, 16)

        @block.tensor
        def _(pe):
            def project(b):
                if b >= 1:
                    pe.wait_ge(k_exp, b)
                nc.tensor.matmul(ps_k[:, :], wk[:, :], xnT[:, b * L:(b + 1) * L], start=True, stop=True).then_inc(k_mm, 1)
                if b >= 1:
                    pe.wait_ge(q_exp, b)
                    pe.wait_ge(v_copy, b)
                for t in range(LT):
                    last = nc.tensor.matmul(ps_qv[t // 2][:, (t % 2) * 256:(t % 2 + 1) * 256],
                                            xnT[:, b * L + t * P:b * L + (t + 1) * P],
                                            wqv[:, :, :].rearrange("p a d -> p (a d)"), start=True, stop=True)
                last.then_inc(qv_mm, 1)

            pe.wait_ge(w_in, 16 * 7)
            project(0)
            for b in range(B):
                pe.wait_ge(k_exp, b + 1)
                if b >= 1:
                    pe.wait_ge(k_copied, b)
                for t in range(LT):
                    last = nc.tensor.transpose(ps_kT[:, t * P:(t + 1) * P], ek[:, t * P:(t + 1) * P], ident[:, :])
                last.then_inc(k_turned, 1)
                pe.wait_ge(q_exp, b + 1)
                if b >= 1:
                    pe.wait_ge(q_copied, b)
                for t in range(LT):
                    last = nc.tensor.transpose(ps_qT[:, t * P:(t + 1) * P], eq[:, t, :], ident[:, :])
                last.then_inc(q_turned, 1)
                if b + 1 < B:
                    project(b + 1)
                pe.wait_ge(k_copied, b + 1)
                pe.wait_ge(v_copy, b + 1)
                if b >= 1:
                    pe.wait_ge(cw_copied, b)
                for t in range(LT):
                    last = nc.tensor.matmul(ps_c[:, 0:P], v[:, t, :], ekT[:, t, :], start=(t == 0), stop=(t == LT - 1))
                last.then_inc(ctx_mm, 1)
                pe.wait_ge(ctx_copied, b + 1)
                nc.tensor.matmul(ps_c[:, P:2 * P], ctxT[:, :], wo[:, :], start=True, stop=True).then_inc(cw_mm, 1)
                pe.wait_ge(cw_copied, b + 1)
                pe.wait_ge(q_copied, b + 1)
                if b >= 1:
                    pe.wait_ge(out_read, b)
                for t in range(LT):
                    last = nc.tensor.matmul(ps_o[:, t * P:(t + 1) * P], eqT[:, t * P:(t + 1) * P], cw[:, :],
                                            start=True, stop=True)
                last.then_inc(out_mm, 1)

        @block.scalar
        def _(act):
            for b in range(B):
                act.wait_ge(k_max, b + 1)
                if b >= 1:
                    act.wait_ge(k_turned, b)
                    act.wait_ge(cw_copied, b)
                nc.scalar.activation(ek[:, :], ps_k[:, :], ACT.Exp, bias=neg_kmax[:, 0:1],
                                     accum_out=ksum[:, 0:1]).then_inc(k_exp, 1)
                act.wait_ge(qv_mm, b + 1)
                act.wait_ge(q_max, b + 1)
                if b >= 1:
                    act.wait_ge(ctx_mm, b)
                for i in range(2):
                    last = nc.scalar.copy(v[:, 2 * i:2 * i + 2, :],
                                          ps_qv[i][:, :].rearrange("p (t a d) -> p t a d", t=2, a=2)[:, :, 1, :])
                last.then_inc(v_copy, 1)
                if b >= 1:
                    act.wait_ge(q_turned, b)
                    act.wait_ge(out_read, b)
                for t in range(LT):
                    last = nc.scalar.activation(eq[:, t, :], ps_qv[t // 2][:, (t % 2) * 256:(t % 2) * 256 + P], ACT.Exp,
                                                bias=neg_qmax[:, t:t + 1], accum_out=qsum[:, t:t + 1])
                last.then_inc(q_exp, 1)
                act.wait_ge(q_turned, b + 1)
                if b >= 1:
                    act.wait_ge(out_mm, b)
                nc.scalar.copy(eqT[:, :], ps_qT[:, :]).then_inc(q_copied, 1)
            act.wait_ge(var_ready, 1)
            nc.scalar.activation(rstd[:, :], rstd[:, :], ACT.Sqrt).then_inc(std_ready, 1)

        @block.vector
        def _(dve):
            link = Chain(dve, dve_done)

            def row(i):
                return rows[:, i:i + 1, :].broadcast_to([P, LT, D])

            def maxima(b):
                dve.wait_ge(k_mm, b + 1)
                nc.vector.tensor_reduce(neg_kmax[:, :], ps_k[:, :], AX_X, ALU.max, negate=True).then_inc(k_max, 1)
                dve.wait_ge(qv_mm, b + 1)
                for i in range(2):
                    last = nc.vector.tensor_reduce(neg_qmax[:, 2 * i:2 * i + 2],
                                                   ps_qv[i][:, :].rearrange("p (t a d) -> p t a d", t=2, a=2)[:, :, 0, :],
                                                   AX_X, ALU.max, negate=True)
                last.then_inc(q_max, 1)

            dve.wait_ge(w_in, 16 * 7)
            maxima(0)
            for b in range(B):
                dve.wait_ge(k_turned, b + 1)
                if b >= 1:
                    dve.wait_ge(ctx_mm, b)
                nc.vector.tensor_copy(ekT[:, :, :].rearrange("p t d -> p (t d)"), ps_kT[:, :]).then_inc(k_copied, 1)
                link(nc.vector.reciprocal(rk[:, :], ksum[:, :]))
                dve.wait_ge(q_exp, b + 1)
                link(nc.vector.reciprocal(rq[:, :], qsum[:, :]))
                if b + 1 < B:
                    maxima(b + 1)
                dve.wait_ge(ctx_mm, b + 1)
                if b >= 1:
                    dve.wait_ge(cw_mm, b)
                nc.vector.tensor_copy(ctxT[:, :], ps_c[:, 0:P]).then_inc(ctx_copied, 1)
                dve.wait_ge(cw_mm, b + 1)
                if b >= 1:
                    dve.wait_ge(out_mm, b)
                nc.vector.tensor_scalar(cw[:, :], ps_c[:, P:2 * P], rk[:, 0:1], float(D) ** -0.5, ALU.mult,
                                        ALU.mult).then_inc(cw_copied, 1)
                dve.wait_ge(out_mm, b + 1)
                y = s[:, b * LT:(b + 1) * LT, :]
                for t in range(LT):
                    last = nc.vector.scalar_tensor_tensor(out=y[:, t, :], in0=ps_o[:, t * P:(t + 1) * P],
                                                          scalar=rq[:, t:t + 1], in1=xn[:, b * LT + t, :],
                                                          op0=ALU.mult, op1=ALU.add)
                last.then_inc(out_read, 1)
                dve.wait_ge(out_read, b + 1)
                link(nc.vector.tensor_tensor(y, y, row(0), ALU.add))
                for t in range(LT):
                    last = nc.vector.bn_stats(stats[:, t, :], y[:, t, :])
                link(last)
                for t in range(LT):
                    last = nc.vector.bn_aggr(mv[:, b * LT + t, :], stats[:, t, :])
                link(last)
            nc.vector.tensor_scalar(rstd[:, :], mv[:, :, 1], EPS, None, ALU.add).then_inc(var_ready, 1)
            dve.wait_ge(std_ready, 1)
            link(nc.vector.reciprocal(rstd[:, :], rstd[:, :]))
            for b in range(B):
                y = s[:, b * LT:(b + 1) * LT, :]
                for t in range(b * LT, (b + 1) * LT):
                    last = nc.vector.tensor_scalar(s[:, t, :], s[:, t, :], mv[:, t, 0:1], rstd[:, t:t + 1],
                                                   ALU.subtract, ALU.mult)
                link(last)
                link(nc.vector.tensor_tensor(y, y, row(1), ALU.mult))
                link(nc.vector.tensor_tensor(y, y, row(2), ALU.add))


def gate(nc, name, xnT, wg_dram, capacity, cwT_dram, const, bank):
    with ExitStack() as ctx:
        sb, sem = tensors(nc, ctx)
        wg = sb(name + "wg", [P, E])
        logit = sb(name + "logit", [P, NT, E])
        top = sb(name + "top", [P, NT, 8])
        idx = sb(name + "idx", [P, NT, 8], U32)
        idxf = sb(name + "idxf", [P, 2, NT])
        oh = sb(name + "oh", [P, 2, E, NT])
        wt = sb(name + "wt", [P, 2, NT])
        gap = sb(name + "gap", [P, NT])
        cw = sb(name + "cw", [P, E, NT])
        cw2 = sb(name + "cw2", [P, E, NT])
        cwT = sb(name + "cwT", [P, 2, P])
        totals = sb(name + "totals", [P, 2, E, NT])
        before = sb(name + "before", [P, 2, E, NT])
        w_in, logits_mm, oh_ready = sem(name + "w_in"), sem(name + "logits_mm"), sem(name + "oh_ready")
        gap_ready, gap_exp, dve_done = sem(name + "gap_ready"), sem(name + "gap_exp"), sem(name + "dve_done")
        ranks_mm, cw_ready, cw_turned = sem(name + "ranks_mm"), sem(name + "cw_ready"), sem(name + "cw_turned")
        cw_copied, cw_out = sem(name + "cw_copied"), sem(name + "cw_out")
        block = ctx.enter_context(nc.Block())
        iota8, ones, upper, ident = const["iota8"], const["ones"], const["upper"], const["ident"]

        @block.sync
        def _(sp):
            sp.dma_start(wg[:, :], wg_dram).then_inc(w_in, 16)
            sp.wait_ge(cw_copied, 1)
            for h in range(2):
                sp.dma_start(cwT_dram.rearrange("(h e) (t p) -> h (e t) p", h=2, p=P)[h],
                             cwT[:, h, :]).then_inc(cw_out, 16)
            sp.wait_ge(cw_out, 32)

        @block.tensor
        def _(pe):
            pe.wait_ge(w_in, 16)
            for t in range(NT):
                last = nc.tensor.matmul(bank[0][:, t * E:(t + 1) * E], xnT[:, t * P:(t + 1) * P], wg[:, :],
                                        start=True, stop=True)
            last.then_inc(logits_mm, 1)
            if capacity:
                pe.wait_ge(oh_ready, 1)
                ohf = oh[:, :, :, :].rearrange("p k e t -> p (k e t)")
                nc.tensor.matmul(bank[1][:, :], upper[:, :], ohf, start=True, stop=True)
                nc.tensor.matmul(bank[2][:, :], ones[:, :], ohf, start=True, stop=True).then_inc(ranks_mm, 1)
            pe.wait_ge(cw_ready, 1)
            for h in range(2):
                last = nc.tensor.transpose(bank[3][:, h * P:(h + 1) * P],
                                           cw[:, h * 4:(h + 1) * 4, :].rearrange("p e t -> p (e t)"), ident[:, :])
            last.then_inc(cw_turned, 1)

        @block.scalar
        def _(act):
            act.wait_ge(gap_ready, 1)
            nc.scalar.activation(gap[:, :], gap[:, :], ACT.Exp).then_inc(gap_exp, 1)

        @block.vector
        def _(dve):
            link = Chain(dve, dve_done)
            dve.wait_ge(logits_mm, 1)
            link(nc.vector.tensor_copy(logit[:, :, :].rearrange("p t e -> p (t e)"), bank[0][:, 0:NT * E]))
            for t in range(NT):
                last = nc.vector.max(top[:, t, :], logit[:, t, :])
            link(last)
            for t in range(NT):
                last = nc.vector.max_index(idx[:, t, :], top[:, t, :], logit[:, t, :])
            link(last)
            nc.vector.tensor_tensor(gap[:, :], top[:, :, 1], top[:, :, 0], ALU.subtract).then_inc(gap_ready, 1)
            link(nc.vector.tensor_copy(idxf[:, :, :], idx[:, :, 0:2].rearrange("p t k -> p k t")))
            for k in range(2):
                last = nc.vector.tensor_tensor(oh[:, k, :, :], iota8[:, :].rearrange("p (e a) -> p e a", a=1).broadcast_to([P, E, NT]),
                                               idxf[:, k:k + 1, :].broadcast_to([P, E, NT]), ALU.is_equal)
            last.then_inc(oh_ready, 1)
            dve.wait_ge(oh_ready, 1)
            dve.wait_ge(gap_exp, 1)
            link(nc.vector.tensor_scalar(wt[:, 1, :], gap[:, :], 1.0, None, ALU.add))
            link(nc.vector.reciprocal(wt[:, 0, :], wt[:, 1, :]))
            link(nc.vector.tensor_tensor(wt[:, 1, :], gap[:, :], wt[:, 0, :], ALU.mult))
            if capacity:
                flat = "p k e t -> p (k e t)"
                dve.wait_ge(ranks_mm, 1)
                link(nc.vector.tensor_copy(totals[:, :, :, :].rearrange(flat), bank[2][:, :]))
                for k in range(2):
                    for e in range(E):
                        last = nc.vector.tensor_tensor_scan(before[:, k, e, :], ones[:, 0:NT], totals[:, k, e, :],
                                                            0.0 if k == 0 else before[:, 0, e, NT - 1:NT],
                                                            ALU.mult, ALU.add)
                    link(last)
                link(nc.vector.tensor_tensor(before[:, :, :, :], before[:, :, :, :], totals[:, :, :, :], ALU.subtract))
                link(nc.vector.tensor_tensor(before[:, :, :, :].rearrange(flat), before[:, :, :, :].rearrange(flat), bank[1][:, :], ALU.add))
                link(nc.vector.scalar_tensor_tensor(out=oh[:, :, :, :].rearrange(flat), in0=before[:, :, :, :].rearrange(flat),
                                                    scalar=float(capacity), in1=oh[:, :, :, :].rearrange(flat),
                                                    op0=ALU.is_lt, op1=ALU.mult))
            link(nc.vector.tensor_tensor(cw2[:, :, :], oh[:, 0, :, :], wt[:, 0:1, :].broadcast_to([P, E, NT]), ALU.mult))
            link(nc.vector.tensor_tensor(cw[:, :, :], oh[:, 1, :, :], wt[:, 1:2, :].broadcast_to([P, E, NT]), ALU.mult))
            nc.vector.tensor_tensor(cw[:, :, :], cw[:, :, :], cw2[:, :, :], ALU.add).then_inc(cw_ready, 1)
            dve.wait_ge(cw_turned, 1)
            nc.vector.tensor_copy(cwT[:, :, :].rearrange("p h q -> p (h q)"), bank[3][:, 0:2 * P]).then_inc(cw_copied, 1)


def experts(nc, name, xnT, acc, w1_dram, w2_dram, b1_dram, b2_dram, cwT_dram, bank):
    NC = T // L
    with ExitStack() as ctx:
        sb, sem = tensors(nc, ctx)
        w1 = [sb(f"{name}w1_{i}", [P, H]) for i in range(2)]
        w2 = [sb(f"{name}w2_{i}", [P, HC, D]) for i in range(2)]
        b1 = [sb(f"{name}b1_{i}", [P, HC]) for i in range(2)]
        cwb = [sb(f"{name}cwb_{i}", [P, T]) for i in range(2)]
        b2 = sb(name + "b2", [E, D])
        cwT = sb(name + "cwT8", [E, T])
        h = [sb(f"{name}h{i}", [P, HC, L]) for i in range(2)]
        term = sb(name + "term", [P, 2, L])
        w_in = [sem(f"{name}w_in{i}") for i in range(2)]
        b2_in, up_mm, gelu_done = sem(name + "b2_in"), sem(name + "up_mm"), sem(name + "gelu_done")
        down_mm, term_done, acc_done = sem(name + "down_mm"), sem(name + "term_done"), sem(name + "acc_done")
        bias_mm, acc_set = sem(name + "bias_mm"), sem(name + "acc_set")
        block = ctx.enter_context(nc.Block())
        n_loads = 3 + (b1_dram is not None)

        def landed(eng, i, pair):
            eng.wait_ge(w_in[i], (pair + 1) * 16 * n_loads)

        @block.sync
        def _(sp):
            def load(pair, i):
                e = pair * 2 + i
                sp.dma_start(w1[i][:, :], w1_dram[bass.ds(e, 1)].rearrange("a d h -> (a d) h")).then_inc(w_in[i], 16)
                if b1_dram is not None:
                    sp.dma_start(b1[i][:, :], b1_dram[bass.ds(e, 1)].rearrange("a p c -> (a p) c")).then_inc(w_in[i], 16)
                sp.dma_start(w2[i][:, :, :], w2_dram[bass.ds(e, 1)].rearrange("a (c p) d -> p (a c) d", p=P)).then_inc(w_in[i], 16)
                sp.dma_start(cwb[i][:, :], cwT_dram[bass.ds(e, 1), :].broadcast_to([P, T])).then_inc(w_in[i], 16)

            load(0, 0)
            if b2_dram is not None:
                sp.dma_start(b2[:, :], b2_dram).then_inc(b2_in, 16)
                sp.dma_start(cwT[:, :], cwT_dram).then_inc(b2_in, 16)
            load(0, 1)
            with sp.Fori(1, E // 2) as pair:
                for i in range(2):
                    sp.wait_ge(down_mm, (pair * 2 + i - 1) * NC)
                    sp.wait_ge(term_done, (pair * 2 + i - 1) * NC)
                    load(pair, i)

        @block.tensor
        def _(pe):
            def up(pair, i, c, first):
                k = (pair * 2 + i) * NC + c
                if c == 0:
                    landed(pe, i, pair)
                for hc in range(HC):
                    if not first:
                        pe.wait_ge(gelu_done, k * HC + (hc + 1 - HC))
                    nc.tensor.matmul(bank[hc][:, :], w1[i][:, hc * P:(hc + 1) * P], xnT[:, c * L:(c + 1) * L],
                                     start=True, stop=True).then_inc(up_mm, 1)

            def down(pair, i, c, first):
                k = (pair * 2 + i) * NC + c
                pe.wait_ge(gelu_done, k * HC + HC)
                if not first:
                    pe.wait_ge(term_done, k - 1)
                for hc in range(HC):
                    last = nc.tensor.matmul(bank[4 + c % 2][:, :], w2[i][:, hc, :], h[c % 2][:, hc, :],
                                            start=(hc == 0), stop=(hc == HC - 1))
                last.then_inc(down_mm, 1)

            def step(pair, i, c, peeled):
                up(pair, i, c, peeled and i == 0 and c == 0)
                if c:
                    down(pair, i, c - 1, peeled and i == 0 and c < 3)
                elif i:
                    down(pair, 0, NC - 1, False)
                elif not peeled:
                    down(pair - 1, 1, NC - 1, False)

            if b2_dram is not None:
                pe.wait_ge(b2_in, 32)
                for c in range(NC):
                    if c >= 2:
                        pe.wait_ge(acc_set, c - 1)
                    nc.tensor.matmul(bank[6 + c % 2][:, :], b2[:, :], cwT[:, c * L:(c + 1) * L],
                                     start=True, stop=True).then_inc(bias_mm, 1)
            for i in range(2):
                for c in range(NC):
                    step(0, i, c, True)
            with pe.Fori(1, E // 2) as pair:
                for i in range(2):
                    for c in range(NC):
                        step(pair, i, c, False)
            down(E // 2 - 1, 1, NC - 1, False)

        @block.scalar
        def _(act):
            def step(pair, i, c, first):
                k = (pair * 2 + i) * NC + c
                if c == 0 and b1_dram is not None:
                    landed(act, i, pair)
                if not first:
                    act.wait_ge(down_mm, k - 1)
                for hc in range(HC):
                    act.wait_ge(up_mm, k * HC + (hc + 1))
                    bias = b1[i][:, hc:hc + 1] if b1_dram is not None else 0.0
                    nc.scalar.activation(h[c % 2][:, hc, :], bank[hc][:, :], ACT.Gelu, bias=bias).then_inc(gelu_done, 1)

            for i in range(2):
                for c in range(NC):
                    step(0, i, c, i == 0 and c < 2)
            with act.Fori(1, E // 2) as pair:
                for i in range(2):
                    for c in range(NC):
                        step(pair, i, c, False)

        @block.vector
        def _(dve):
            def weigh(pair, i, c, first):
                k = (pair * 2 + i) * NC + c
                if c == 0:
                    landed(dve, i, pair)
                if not first:
                    dve.wait_ge(acc_done, k - 1)
                dve.wait_ge(down_mm, k + 1)
                nc.vector.tensor_tensor(term[:, c % 2, :], bank[4 + c % 2][:, :], cwb[i][:, c * L:(c + 1) * L],
                                        ALU.mult).then_inc(term_done, 1)

            def add(pair, i, c):
                k = (pair * 2 + i) * NC + c
                dve.wait_ge(term_done, k + 1)
                nc.vector.tensor_tensor(acc[:, c * L:(c + 1) * L], acc[:, c * L:(c + 1) * L], term[:, c % 2, :],
                                        ALU.add).then_inc(acc_done, 1)

            def step(pair, i, c, peeled):
                weigh(pair, i, c, peeled and i == 0 and c < 2)
                if c:
                    add(pair, i, c - 1)
                elif i:
                    add(pair, 0, NC - 1)
                elif not peeled:
                    add(pair - 1, 1, NC - 1)

            if b2_dram is None:
                nc.vector.memset(acc[:, :], 0.0).then_inc(acc_set, NC)
            for c in range(NC if b2_dram is not None else 0):
                dve.wait_ge(bias_mm, c + 1)
                nc.vector.tensor_copy(acc[:, c * L:(c + 1) * L], bank[6 + c % 2][:, :]).then_inc(acc_set, 1)
            dve.wait_ge(acc_set, NC)
            for i in range(2):
                for c in range(NC):
                    step(0, i, c, True)
            with dve.Fori(1, E // 2) as pair:
                for i in range(2):
                    for c in range(NC):
                        step(pair, i, c, False)
            add(E // 2 - 1, 1, NC - 1)


class ExpertSteps:

    NC = T // L

    def __init__(self, nc, sb, sem, xnT, acc, w1_dram, w2_dram, cwT_dram, hidden, up_banks, down_bank):
        self.nc, self.xnT, self.acc, self.h = nc, xnT, acc, hidden
        self.w1_dram, self.w2_dram, self.cwT_dram = w1_dram, w2_dram, cwT_dram
        self.up_banks, self.down_bank = up_banks, down_bank
        self.w1 = [sb(f"step_w1_{i}", [P, H]) for i in range(2)]
        self.w2 = [sb(f"step_w2_{i}", [P, HC, D]) for i in range(2)]
        self.cwb = [sb(f"step_cwb_{i}", [P, L]) for i in range(2)]
        self.term = sb("step_term", [P, 2, L])
        self.w_in = [sem(f"step_w_in{i}") for i in range(2)]
        self.cw_in = [sem(f"step_cw_in{i}") for i in range(2)]
        self.up_mm, self.gelu_done, self.down_mm = sem("step_up_mm"), sem("step_gelu"), sem("step_down_mm")
        self.term_done, self.acc_done = sem("step_term"), sem("step_acc")

    def load_expert(self, sp, e):
        if e >= 2:
            sp.wait_ge(self.down_mm, (e - 1) * self.NC)
        sp.dma_start(self.w1[e % 2][:, :], self.w1_dram[e]).then_inc(self.w_in[e % 2], 16)
        sp.dma_start(self.w2[e % 2][:, :, :], self.w2_dram[e].rearrange("(c p) d -> p c d", p=P)).then_inc(self.w_in[e % 2], 16)

    def load_weights(self, sp, k):
        e, c = divmod(k, self.NC)
        if k >= 2:
            sp.wait_ge(self.term_done, k - 1)
        sp.dma_start(self.cwb[k % 2][:, :], self.cwT_dram[e:e + 1, c * L:(c + 1) * L].broadcast_to([P, L])).then_inc(self.cw_in[k % 2], 16)

    def up(self, pe, k):
        e, c = divmod(k, self.NC)
        pe.wait_ge(self.w_in[e % 2], 32 * (e // 2 + 1))
        for hc in range(HC):
            if k >= 1:
                pe.wait_ge(self.gelu_done, (k - 1) * HC + hc + 1)
            self.nc.tensor.matmul(self.up_banks[hc][:, :], self.w1[e % 2][:, hc * P:(hc + 1) * P],
                                  self.xnT[:, c * L:(c + 1) * L], start=True, stop=True).then_inc(self.up_mm, 1)

    def down(self, pe, k):
        e = k // self.NC
        pe.wait_ge(self.gelu_done, (k + 1) * HC)
        if k >= 1:
            pe.wait_ge(self.term_done, k)
        for hc in range(HC):
            last = self.nc.tensor.matmul(self.down_bank[:, :], self.w2[e % 2][:, hc, :], self.h[k % 2][:, hc, :],
                                         start=(hc == 0), stop=(hc == HC - 1))
        last.then_inc(self.down_mm, 1)

    def gelu(self, act, k):
        if k >= 2:
            act.wait_ge(self.down_mm, k - 1)
        for hc in range(HC):
            act.wait_ge(self.up_mm, k * HC + hc + 1)
            self.nc.scalar.activation(self.h[k % 2][:, hc, :], self.up_banks[hc][:, :], ACT.Gelu).then_inc(self.gelu_done, 1)

    def weigh(self, dve, k):
        c = k % self.NC
        dve.wait_ge(self.cw_in[k % 2], 16 * (k // 2 + 1))
        if k >= self.NC + 2:
            dve.wait_ge(self.acc_done, k - self.NC - 1)
        dve.wait_ge(self.down_mm, k + 1)
        out = self.acc[:, c * L:(c + 1) * L] if k < self.NC else self.term[:, k % 2, :]
        self.nc.vector.tensor_tensor(out, self.down_bank[:, :], self.cwb[k % 2][:, :], ALU.mult).then_inc(self.term_done, 1)

    def add(self, dve, k):
        if k < self.NC:
            return
        c = k % self.NC
        dve.wait_ge(self.term_done, k + 1)
        if k >= 2 * self.NC:
            dve.wait_ge(self.acc_done, k - 2 * self.NC + 1)
        out = self.acc[:, c * L:(c + 1) * L]
        self.nc.vector.tensor_tensor(out, out, self.term[:, k % 2, :], ALU.add).then_inc(self.acc_done, 1)


def combine(nc, name, x, s, acc, out, out_dram, ident, bank):
    with ExitStack() as ctx:
        sb, sem = tensors(nc, ctx)
        g = sb(name + "g", [P, 2, LT, P])
        turned, silu_done, prod_done, done = sem(name + "turned"), sem(name + "silu"), sem(name + "prod"), sem(name + "done")
        stored = sem(name + "stored")
        block = ctx.enter_context(nc.Block())

        @block.tensor
        def _(pe):
            for b in range(B):
                if b >= 2:
                    pe.wait_ge(silu_done, b - 1)
                for t in range(LT):
                    last = nc.tensor.transpose(bank[b % 2][:, t * P:(t + 1) * P],
                                               acc[:, (b * LT + t) * P:(b * LT + t + 1) * P], ident[:, :])
                last.then_inc(turned, 1)

        @block.scalar
        def _(act):
            for b in range(B):
                act.wait_ge(turned, b + 1)
                if b >= 2:
                    act.wait_ge(done, b - 1)
                nc.scalar.activation(g[:, b % 2, :, :].rearrange("p t d -> p (t d)"), bank[b % 2][:, :],
                                     ACT.Silu).then_inc(silu_done, 1)

        @block.vector
        def _(dve):
            for b in range(B):
                ts = slice(b * LT, (b + 1) * LT)
                dve.wait_ge(silu_done, b + 1)
                nc.vector.tensor_tensor(g[:, b % 2, :, :], g[:, b % 2, :, :], s[:, ts, :], ALU.mult).then_inc(prod_done, 1)
                dve.wait_ge(prod_done, b + 1)
                nc.vector.tensor_tensor(out[:, ts, :], g[:, b % 2, :, :], x[:, ts, :], ALU.add).then_inc(done, 1)

        @block.sync
        def _(sp):
            if out_dram is not None:
                for b in range(B):
                    sp.wait_ge(done, b + 1)
                    sp.dma_start(out_dram[b].rearrange("(t p) d -> p t d", p=P),
                                 out[:, b * LT:(b + 1) * LT, :]).then_inc(stored, 16)
                sp.wait_ge(stored, 16 * B)


def project_qkv(nc, xnT, w, k_stack, q_stack, vT_dram, v_heads):
    bank = w["bank"]
    with ExitStack() as ctx:
        sb, sem = tensors(nc, ctx)
        wT, wsT = sb("wqkvT", [P, 3 * D]), sb("wswapT", [P, 2 * D])
        bias = sb("qkv_bias", [P, 5])
        rot = sb("rot", [P, 2, L])
        part = sb("rot_part", [P, 2, L])
        qk = sb("qk", [P, 2, 2, L])
        rest = sb("qk_rest", [P, 2, 2, L])
        split = sb("qk_split", [P, 2, 2, 3, L], BF16)
        v = sb("v_chunk", [P, 2, L])
        w_in, mm, rotated = sem("qkv_w_in"), sem("qkv_mm"), sem("rotated")
        hi_done, rest_done, mid_done, split_done = sem("hi_done"), sem("rest_done"), sem("mid_done"), sem("split_done")
        part_done, v_done, v_out, v_in = sem("part_done"), sem("v_done"), [sem(f"v_out{i}") for i in range(2)], sem("v_in")
        stacked = [sem(f"stacked{i}") for i in range(2)]
        block = ctx.enter_context(nc.Block())
        PER_ROW = 16 * 4 * len(K_PARTS)

        @block.sync
        def _(sp):
            sp.dma_start(wT[:, :], w["wqkvT"]).then_inc(w_in, 16)
            sp.dma_start(wsT[:, :], w["wswapT"]).then_inc(w_in, 16)
            sp.dma_start(bias[:, :], w["qkv_bias"]).then_inc(w_in, 16)
            sp.dma_start(rot[:, :, :], w["rot"]).then_inc(w_in, 16)
            for b in range(B):
                sp.wait_ge(v_done, b + 1)
                sp.dma_start(vT_dram[:, b * L:(b + 1) * L], v[:, b % 2, :]).then_inc(v_out[b % 2], 16)
                for i, (stack, parts) in enumerate(((q_stack, Q_PARTS), (k_stack, K_PARTS))):
                    sp.wait_ge(split_done, 2 * b + i + 1)
                    for term, p in enumerate(parts):
                        for hh in range(2):
                            sp.dma_start(stack[b, hh, term * HD:(term + 1) * HD].rearrange("d s t -> (d s) t"),
                                         split[64 * hh:64 * hh + 64, i, b % 2, p, :]).then_inc(stacked[b % 2], 16)
            for i in range(2):
                sp.wait_ge(v_out[i], 16 * (B // 2))
            for b in range(B):
                sp.dma_start(v_heads[b * NH:(b + 1) * NH, :, :],
                             vT_dram.rearrange("(h d) (b t) -> b h d t", h=NH, b=B)[b]).then_inc(v_in, 16)
            sp.wait_ge(v_in, 16 * B)
            for i in range(2):
                sp.wait_ge(stacked[i], PER_ROW * (B // 2))

        @block.tensor
        def _(pe):
            pe.wait_ge(w_in, 64)
            for b in range(B):
                rhs = xnT[:, b * L:(b + 1) * L]
                if b >= 1:
                    pe.wait_ge(rotated, 2 * b)
                    pe.wait_ge(v_done, b)
                for i in range(5):
                    lhsT = wT[:, i * D:(i + 1) * D] if i < 3 else wsT[:, (i - 3) * D:(i - 2) * D]
                    nc.tensor.matmul(bank[i][:, :], lhsT, rhs, start=True, stop=True).then_inc(mm, 1)

        @block.scalar
        def _(act):
            act.wait_ge(w_in, 64)
            for b in range(B):
                act.wait_ge(mm, 5 * b + 3)
                if b >= 2:
                    act.wait_ge(v_out[b % 2], 16 * (b // 2))
                nc.scalar.activation(v[:, b % 2, :], bank[2][:, :], ACT.Identity, bias=bias[:, 2:3]).then_inc(v_done, 1)
                if b >= 2:
                    act.wait_ge(stacked[b % 2], PER_ROW * (b // 2))
                for i in range(2):
                    act.wait_ge(rotated, 2 * b + i + 1)
                    nc.scalar.copy(split[:, i, b % 2, 0, :], qk[:, i, b % 2, :]).then_inc(hi_done, 1)
                for i in range(2):
                    act.wait_ge(rest_done, 2 * b + i + 1)
                    nc.scalar.copy(split[:, i, b % 2, 1, :], rest[:, i, b % 2, :]).then_inc(mid_done, 1)

        @block.vector
        def _(dve):
            dve.wait_ge(w_in, 64)
            for b in range(B):
                dve.wait_ge(mm, 5 * b + 5)
                for i in range(2):
                    d = qk[:, i, b % 2, :]
                    nc.vector.scalar_tensor_tensor(out=d, in0=bank[i][:, :], scalar=bias[:, i:i + 1], in1=rot[:, 0, :],
                                                   op0=ALU.add, op1=ALU.mult)
                    if b or i:
                        dve.wait_ge(rotated, 2 * b + i)
                    nc.vector.scalar_tensor_tensor(out=part[:, i, :], in0=bank[3 + i][:, :], scalar=bias[:, 3 + i:4 + i],
                                                   in1=rot[:, 1, :], op0=ALU.add, op1=ALU.mult).then_inc(part_done, 1)
                    dve.wait_ge(part_done, 2 * b + i + 1)
                    nc.vector.tensor_tensor(d, d, part[:, i, :], ALU.add).then_inc(rotated, 1)
                for i in range(2):
                    dve.wait_ge(hi_done, 2 * b + i + 1)
                    nc.vector.tensor_tensor(rest[:, i, b % 2, :], qk[:, i, b % 2, :], split[:, i, b % 2, 0, :],
                                            ALU.subtract).then_inc(rest_done, 1)
                for i in range(2):
                    dve.wait_ge(mid_done, 2 * b + i + 1)
                    nc.vector.tensor_tensor(split[:, i, b % 2, 2, :], rest[:, i, b % 2, :], split[:, i, b % 2, 1, :],
                                            ALU.subtract).then_inc(split_done, 1)


def solve_attention(nc, A, xnT, acc, w, k_stack, q_stack, max_dram, sum_dram, a_dram):
    bank, big, ident = w["bank"], w["big"], w["ident"]
    with ExitStack() as ctx:
        sb, sem = tensors(nc, ctx)
        second = sb("Kst1_Pn_upd", [P, NSLOT * L // 2])
        Kst = [sb("Kst0", [P, NSLOT, L], BF16), second[:, :].bitcast(BF16).rearrange("p (s t) -> p s t", s=NSLOT)]
        Pn = second[:, 0:SB * SB].rearrange("p (i j) -> p i j", i=SB)
        upd = second[0:SB, SB * SB:SB * SB + BH * HD].rearrange("p (b d) -> p b d", d=HD)
        Qmax = [sb(f"Qmax{i}", [P, NH, P], BF16) for i in range(2)]
        Qexp = [sb(f"Qexp{i}", [P, NH, P], BF16) for i in range(2)]
        Ed = sb("Ed", [P, BH, P])
        shared = sb("Eoff_RT_hidden", [P, 4 * 2 * L])
        Eoff = shared[:, 0:4 * 3 * 2 * P].rearrange("p (n j h q) -> p n j h q", n=4, j=3, h=2)
        RT = shared[:, 4 * 3 * 2 * P:].rearrange("p (b u q) -> p b u q", b=2, u=LT)
        hidden = [shared[:, i * HC * L:(i + 1) * HC * L].rearrange("p (c t) -> p c t", c=HC) for i in range(2)]
        Apos = sb("Apos", [P, (LT * BH) * (HD + 1) + 32])
        Rb = sb("Rb", [P, HD + 1, P])
        rZ = sb("rZ", [P, P])
        pd = sb("pd", [P, SB])
        prod = sb("prod", [P, HD, SB])
        mx = sb("mx", [P, 2, BH])
        mxp = sb("mxp", [P, 3, BH], BF16)
        mxT = sb("mxT", [P, 3, P], BF16)
        masks = sb("masks", [P, 2, P], BF16)
        identb = sb("identb", [P, P], BF16)
        one = sb("one", [P, 32])
        c_in, set_done = sem("solve_c_in"), sem("set_done")
        steps = ExpertSteps(nc, sb, sem, xnT, acc, w["L1_ffn_c_fc"], w["L1_ffn_c_proj"], w["cwT_dram"], hidden,
                            bank[3:7], bank[7])
        with nc.Block() as block:
            @block.sync
            def _(sp):
                sp.dma_start(Rb[:, 0:2, :], w["masks"]).then_inc(c_in, 16)
                for i in range(2):
                    steps.load_expert(sp, i)
                    steps.load_weights(sp, i)

            @block.vector
            def _(dve):
                nc.vector.tensor_copy(identb[:, :], ident[:, :])
                nc.vector.memset(Kst[0][:, :, :], 1.0)
                for i in range(2):
                    nc.vector.memset(Qexp[i][:, :, :], 0.0)
                dve.wait_ge(c_in, 16)
                nc.vector.tensor_copy(masks[:, :, :], Rb[:, 0:2, :])

            @block.gpsimd
            def _(pool):
                for i in range(2):
                    nc.gpsimd.memset(Qmax[i][:, :, :], 0.0)
                nc.gpsimd.memset(Apos[:, :], 1.0)
                nc.gpsimd.memset(one[:, 0:HD], 0.0)
                nc.gpsimd.memset(one[:, HD + 1:32], 0.0)
                nc.gpsimd.memset(one[:, HD:HD + 1], 1.0).then_inc(set_done, 1)
                pool.wait_ge(set_done, 1)

        for I in range(-1, LT):
            attend(nc, I, Kst, Qmax, Qexp, k_stack, q_stack, max_dram, sum_dram, mx, mxp, mxT, masks, identb, Ed, Eoff, Apos,
                   one, RT, Rb, bank, big)
            if I >= 0:
                for s in range(NSUB):
                    solve_block(nc, I, s, Ed, upd, Rb, rZ, Pn, pd, prod, A, Apos, ident, bank, steps)
        a_out = sem("a_out")
        with nc.Block() as block:
            @block.sync
            def _(sp):
                sp.dma_start(a_dram, A[:, :, :]).then_inc(a_out, 16)
                sp.wait_ge(a_out, 16)


def attend(nc, I, Kst, Qmax, Qexp, k_stack, q_stack, max_dram, sum_dram, mx, mxp, mxT, masks, identb, Ed, Eoff, Apos, one, RT, Rb,
           bank, big):
    now, ahead = I >= 0, I + 1 < LT
    scale = float(HD) ** -0.5
    n_loads = 2 * (1 + 2 * now + ahead)
    keys_now, keys_ahead = (I + 1) * P, (I + 2) * P
    keys = keys_ahead if ahead else keys_now
    with ExitStack() as ctx:
        sb, sem = tensors(nc, ctx)
        loaded = [sem(f"stacks_in{i}") for i in range(2)]
        max_mm, max_done, exp_mm, exp_done = sem("max_mm"), sem("max_done"), sem("exp_mm"), sem("exp_done")
        sum_mm, sum_read, sum_out = sem("sum_mm"), sem("sum_read"), [sem(f"sum_out{i}") for i in range(2)]
        sum_in, ones_set = sem("sum_in"), sem("ones_set")
        parts_done, max_turned, max_copied, max_out = sem("parts"), sem("max_turned"), sem("max_copied"), sem("max_out")
        block = ctx.enter_context(nc.Block())

        @block.gpsimd
        def _(pool):
            for hh in range(2):
                nc.gpsimd.memset(Kst[1][64 * hh + 32:64 * hh + 64, :, :], 1.0).then_inc(ones_set, 1)

        @block.sync
        def _(sp):
            def store_sums(b):
                sp.wait_ge(sum_read, b + 1)
                sp.dma_start(sum_dram[b], RT[:, b % 2, :, :]).then_inc(sum_out[b % 2], 16)

            def regroup(b):
                sp.wait_ge(sum_out[b % 2], 16 * (b // 2 + 1))
                for u in range(LT):
                    sp.dma_start(Rb[b * NH + 4 * u:b * NH + 4 * u + 4, :, :],
                                 sum_dram[b][:, u, :].rearrange("(g r) q -> g r q", g=4)[:, 0:HD + 1, :]).then_inc(sum_in, 16)

            for b in range(B):
                i = b % 2
                if b == 1:
                    sp.wait_ge(ones_set, 2)
                if b >= 2:
                    if now:
                        sp.wait_ge(exp_mm, NSLOT * (b - 1))
                    if ahead:
                        sp.wait_ge(max_mm, NH * (b - 1))
                for hh in range(2):
                    r = slice(64 * hh, 64 * hh + ROWS)
                    sp.dma_start(Kst[i][r, :, 0:keys], k_stack[b, hh, :, :, 0:keys]).then_inc(loaded[i], 16)
                    if ahead:
                        sp.dma_start(Qmax[i][r, hh::2, :], q_stack[b, hh, :, :, keys_now:keys_ahead]).then_inc(loaded[i], 16)
                    if now:
                        sp.dma_start(Qexp[i][r, hh::2, :], q_stack[b, hh, :, :, I * P:keys_now]).then_inc(loaded[i], 16)
                        sp.dma_start(Qexp[i][64 * hh + ROWS:64 * hh + ROWS + 3, hh::2, :],
                                     max_dram[b, hh].rearrange("s p q -> p s q")).then_inc(loaded[i], 16)
                if now and b:
                    store_sums(b - 1)
                if now and b >= 2:
                    regroup(b - 2)
            if now:
                store_sums(B - 1)
                regroup(B - 2)
                regroup(B - 1)
                sp.wait_ge(sum_in, 64 * B)
            if ahead:
                sp.wait_ge(max_copied, 1)
                for b in range(B):
                    for hh in range(2):
                        sp.dma_start(max_dram[b, hh], mxT[b * NH + hh * NSLOT:b * NH + (hh + 1) * NSLOT, :, :]).then_inc(max_out, 16)
                sp.wait_ge(max_out, 16 * 2 * B)

        @block.tensor
        def _(pe):
            def exp_logits(b, s):
                n = b * NSLOT + s
                if n >= 2:
                    pe.wait_ge(exp_done, n - 1)
                for J in range(I + 1):
                    out = big[n % 2][:, J * 2 * P:(J + 1) * 2 * P]
                    last = nc.tensor.matmul(out, Kst[b % 2][:, s, J * P:(J + 1) * P], Qexp[b % 2][:, 2 * s:2 * s + 2, :],
                                            start=True, stop=(J < I), skip_group_check=True)
                last = nc.tensor.matmul(out, identb[:, :], masks[:, 1:2, :].broadcast_to([P, 2, P]), start=False,
                                        stop=True, skip_group_check=True)
                last.then_inc(exp_mm, 1)

            def max_logits(b, s):
                for j in range(2):
                    m = (b * NSLOT + s) * 2 + j
                    if m >= 2:
                        pe.wait_ge(max_done, m - 1)
                    nc.tensor.matmul(bank[4 + m % 2][:, 0:keys_ahead], Qmax[b % 2][:, 2 * s + j, :],
                                     Kst[b % 2][:, s, 0:keys_ahead], start=True, stop=False, skip_group_check=True)
                    nc.tensor.matmul(bank[4 + m % 2][:, keys_now:keys_ahead], identb[:, :], masks[:, 0, :], start=False,
                                     stop=True, skip_group_check=True).then_inc(max_mm, 1)

            def sums(b, u):
                n = b * NSLOT + 2 * u
                pe.wait_ge(exp_done, n + 2)
                if u == 0 and b >= 2:
                    pe.wait_ge(sum_read, b - 1)
                for J in range(I, -1, -1):
                    for g in range(4):
                        bh = b * NH + 4 * u + g
                        row = (J * BH + bh) * (HD + 1)
                        last = nc.tensor.matmul(bank[6 + b % 2][32 * g:32 * g + 32, u * P:(u + 1) * P],
                                                one[:, :] if J == I else Apos[:, row:row + 32],
                                                Ed[:, bh, :] if J == I else Eoff[:, (n + g // 2) % 4, J, g % 2, :],
                                                start=(J == I), stop=(J == 0), skip_group_check=True)
                last.then_inc(sum_mm, 1)

            for b in range(B):
                pe.wait_ge(loaded[b % 2], 16 * n_loads * (b // 2 + 1))
                for s in range(NSLOT):
                    if now:
                        exp_logits(b, s)
                    if ahead:
                        max_logits(b, s)
                    if now and s % 2 == 0 and (b or s):
                        sums(*divmod(b * LT + s // 2 - 1, LT))
            if now:
                sums(B - 1, LT - 1)
            if ahead:
                pe.wait_ge(parts_done, 5)
                pe.wait_ge(max_done, BH)
                for i in range(3):
                    last = nc.tensor.transpose(bank[4][:, :].bitcast(BF16)[:, i * P:(i + 1) * P], mxp[:, i, :], identb[:, :])
                last.then_inc(max_turned, 1)

        @block.scalar
        def _(act):
            for n in range(B * NSLOT if now else 0):
                b, s = divmod(n, NSLOT)
                act.wait_ge(exp_mm, n + 1)
                if I:
                    if n >= 4:
                        act.wait_ge(sum_mm, n // 2 - 1)
                    nc.scalar.activation(Eoff[:, n % 4, 0:I, :, :].rearrange("p j h q -> p (j h q)"),
                                         big[n % 2][:, 0:I * 2 * P], ACT.Exp, scale=scale)
                nc.scalar.activation(Ed[:, 2 * n:2 * n + 2, :].rearrange("p h q -> p (h q)"),
                                     big[n % 2][:, I * 2 * P:(I + 1) * 2 * P], ACT.Exp, scale=scale).then_inc(exp_done, 1)

        @block.vector
        def _(dve):
            for b in range(B):
                if ahead:
                    for h in range(NH):
                        m = b * NH + h
                        dve.wait_ge(max_mm, m + 1)
                        c = b * NH + (h % 2) * NSLOT + h // 2
                        nc.vector.tensor_reduce(mx[:, 0, c:c + 1], bank[4 + m % 2][:, 0:keys_ahead], AX_X, ALU.max,
                                                negate=True).then_inc(max_done, 1)
                if now:
                    dve.wait_ge(sum_mm, LT * (b + 1))
                    if b >= 2:
                        dve.wait_ge(sum_out[b % 2], 16 * (b // 2))
                    nc.vector.tensor_copy(RT[:, b % 2, :, :].rearrange("p u q -> p (u q)"),
                                          bank[6 + b % 2][:, :]).then_inc(sum_read, 1)
            if ahead:
                link = Chain(dve, parts_done)
                dve.wait_ge(max_done, BH)
                link(nc.vector.tensor_copy(mxp[:, 0, :], mx[:, 0, :]))
                link(nc.vector.tensor_tensor(mx[:, 1, :], mx[:, 0, :], mxp[:, 0, :], ALU.subtract))
                link(nc.vector.tensor_copy(mxp[:, 1, :], mx[:, 1, :]))
                link(nc.vector.tensor_tensor(mx[:, 0, :], mx[:, 1, :], mxp[:, 1, :], ALU.subtract))
                link(nc.vector.tensor_copy(mxp[:, 2, :], mx[:, 0, :]))
                dve.wait_ge(max_turned, 1)
                nc.vector.tensor_copy(mxT[:, :, :].rearrange("p a q -> p (a q)"),
                                      bank[4][:, :].bitcast(BF16)[:, 0:3 * P]).then_inc(max_copied, 1)


def solve_block(nc, I, s, Ed, upd, Rb, rZ, Pn, pd, prod, A, Apos, ident, bank, steps):
    with ExitStack() as ctx:
        sb, sem = tensors(nc, ctx)
        upd_mm, upd_copied, upd_turned = sem("upd_mm"), sem("upd_copied"), sem("upd_turned")
        probs_turned, probs_read, dve_done = sem("probs_turned"), sem("probs_read"), sem("solve_dve")
        rz_done, solved, rows_turned, rows_copied = sem("rz_done"), sem("solved"), sem("rows_turned"), sem("rows_copied")
        block = ctx.enter_context(nc.Block())
        r0, t0 = s * SB, I * P + s * SB
        per = steps.NC * E // (LT * NSUB)
        k0 = (I * NSUB + s) * per
        first_down = k0 - (s > 0)
        downs = range(first_down, k0 + per - (s < NSUB - 1))
        PER = 512 // SB
        NG = SB // PER
        solved_rows = Apos[:, I * BH * (HD + 1):(I + 1) * BH * (HD + 1)].rearrange("p (b d) -> p b d", d=HD + 1)

        @block.sync
        def _(sp):
            if s == 0 and I:
                for i in range(2):
                    steps.load_expert(sp, 2 * I + i)
            for k in range(max(k0, 2), k0 + per):
                steps.load_weights(sp, k)

        @block.tensor
        def _(pe):
            if s:
                for bh in range(BH):
                    row = (I * BH + bh) * (HD + 1)
                    last = nc.tensor.matmul(bank[bh // 64][0:SB, (bh % 64) * HD:(bh % 64 + 1) * HD],
                                            Ed[0:r0, bh, r0:r0 + SB], Apos[0:r0, row:row + HD], start=True, stop=True)
                last.then_inc(upd_mm, 1)
                pe.wait_ge(upd_copied, 1)
                for d in range(HD):
                    last = nc.tensor.transpose(bank[2][:, d * SB:(d + 1) * SB], upd[:, :, d], ident[0:SB, 0:SB])
                last.then_inc(upd_turned, 1)
            for n in range(NG):
                for i in range(PER):
                    last = nc.tensor.transpose(bank[n][:, i * SB:(i + 1) * SB],
                                               Ed[r0:r0 + SB, :, r0 + n * PER + i], ident[r0:r0 + SB, r0:r0 + SB])
                last.then_inc(probs_turned, 1)
            for k in range(k0, k0 + per):
                steps.up(pe, k)
                if k - 1 in downs:
                    steps.down(pe, k - 1)
            if s == NSUB - 1:
                steps.down(pe, k0 + per - 1)
            pe.wait_ge(solved, 1)
            for d in range(HD):
                last = nc.tensor.transpose(bank[d // 4][0:r0 + SB, (d % 4) * P:(d % 4 + 1) * P],
                                           A[:, d, I * P:t0 + SB], ident[:, :])
            last.then_inc(rows_turned, 1)

        @block.scalar
        def _(act):
            if s:
                act.wait_ge(upd_mm, 1)
                for i in range(2):
                    last = nc.scalar.copy(upd[:, 64 * i:64 * i + 64, :], bank[i][0:SB, :].rearrange("p (b d) -> p b d", d=HD))
                last.then_inc(upd_copied, 1)
            for k in range(k0, k0 + per):
                steps.gelu(act, k)
            act.wait_ge(rows_turned, 1)
            for i in range(2):
                last = nc.scalar.copy(solved_rows[0:r0 + SB, :, 4 * i:4 * i + 4].rearrange("p b d -> p d b"),
                                      bank[i][0:r0 + SB, :].rearrange("p (d b) -> p d b", d=4))
            last.then_inc(rows_copied, 1)

        @block.vector
        def _(dve):
            link = Chain(dve, dve_done)
            rows = A[:, :, t0:t0 + SB]
            if s == 0:
                link(nc.vector.reciprocal(rZ[:, :], Rb[:, HD, :]))
                link(nc.vector.tensor_tensor(Rb[:, 0:HD, :], Rb[:, 0:HD, :],
                                             rZ[:, :].rearrange("p (a q) -> p a q", a=1).broadcast_to([P, HD, P]), ALU.mult))
            else:
                dve.wait_ge(upd_turned, 1)
                link(nc.vector.tensor_tensor(prod[:, :, :], bank[2][:, 0:HD * SB].rearrange("p (d q) -> p d q", d=HD),
                                             rZ[:, r0:r0 + SB].rearrange("p (a q) -> p a q", a=1).broadcast_to([P, HD, SB]), ALU.mult))
                link(nc.vector.tensor_tensor(Rb[:, 0:HD, r0:r0 + SB], Rb[:, 0:HD, r0:r0 + SB], prod[:, :, :], ALU.add))
            for n in range(NG):
                dve.wait_ge(probs_turned, n + 1)
                z = rZ[:, r0 + n * PER:r0 + (n + 1) * PER].rearrange("p (i a) -> p i a", a=1).broadcast_to([P, PER, SB])
                nc.vector.tensor_tensor(Pn[:, n * PER:(n + 1) * PER, :],
                                        bank[n][:, :].rearrange("p (i j) -> p i j", i=PER), z,
                                        ALU.mult).then_inc(probs_read, 1)
            dve.wait_ge(probs_read, NG)
            diag = Pn.rearrange("p i j -> p (i j)")[:, ::SB + 1]
            link(nc.vector.tensor_copy(pd[:, :], diag))
            link(nc.vector.tensor_tensor(rows, rows, pd[:, :].rearrange("p (a q) -> p a q", a=1).broadcast_to([P, HD, SB]), ALU.mult))
            nc.vector.memset(diag, 1.0)
            link(nc.vector.tensor_tensor(rows, rows, Rb[:, 0:HD, r0:r0 + SB], ALU.add))
            for r in range(1, SB):
                n = r + 1
                link(nc.vector.tensor_tensor(prod[:, :, 0:n], A[:, :, t0:t0 + n],
                                             Pn[:, r:r + 1, 0:n].broadcast_to([P, HD, n]), ALU.mult))
                last = nc.vector.tensor_reduce(A[:, :, t0 + r], prod[:, :, 0:n], AX_X, ALU.add)
                if r < SB - 1:
                    link(last)
                else:
                    last.then_inc(solved, 1)
                if r % STEP_ROWS == STEP_ROWS - 2 and r // STEP_ROWS < len(downs):
                    steps.weigh(dve, downs[r // STEP_ROWS])
                if r % STEP_ROWS == STEP_ROWS - 1 and r // STEP_ROWS < len(downs):
                    steps.add(dve, downs[r // STEP_ROWS])
            for k in downs[SB // STEP_ROWS:]:
                steps.weigh(dve, k)
                steps.add(dve, k)


def project_out(nc, x, x_dram, s, w, a_dram):
    bank = w["bank"]
    with ExitStack() as ctx:
        sb, sem = tensors(nc, ctx)
        wdT, bd, aT = sb("wdT", [P, D]), sb("bd", [P, D]), sb("aT", [P, T])
        x_in = sem("x_in")
        w_in, a_in, mm, read = sem("wd_in"), [sem(f"a_in{b}") for b in range(B)], sem("wd_mm"), sem("wd_read")
        block = ctx.enter_context(nc.Block())

        @block.sync
        def _(sp):
            sp.dma_start(wdT[:, :], w["wdT"]).then_inc(w_in, 16)
            sp.dma_start(bd[:, :], w["bd"].rearrange("(a d) -> a d", a=1).broadcast_to([P, D])).then_inc(w_in, 16)
            for b in range(B):
                sp.dma_start(aT[:, b * L:(b + 1) * L],
                             a_dram.rearrange("(b h) d t -> b (h d) t", b=B)[b]).then_inc(a_in[b], 16)
            sp.dma_start(x[:, :, :].rearrange("p (b t) d -> p b t d", b=B),
                         x_dram.rearrange("b (t p) d -> p b t d", p=P)).then_inc(x_in, 16)
            sp.wait_ge(x_in, 16)

        @block.tensor
        def _(pe):
            pe.wait_ge(w_in, 32)
            for b in range(B):
                pe.wait_ge(a_in[b], 16)
                if b >= 2:
                    pe.wait_ge(read, b - 1)
                for t in range(LT):
                    last = nc.tensor.matmul(bank[b % 2][:, t * P:(t + 1) * P], aT[:, (b * LT + t) * P:(b * LT + t + 1) * P],
                                            wdT[:, :], start=True, stop=True)
                last.then_inc(mm, 1)

        @block.vector
        def _(dve):
            dve.wait_ge(w_in, 32)
            for b in range(B):
                dve.wait_ge(mm, b + 1)
                nc.vector.tensor_tensor(s[:, b * LT:(b + 1) * LT, :], bank[b % 2][:, :].rearrange("p (t d) -> p t d", t=LT),
                                        bd[:, :].rearrange("p (a d) -> p a d", a=1).broadcast_to([P, LT, D]),
                                        ALU.add).then_inc(read, 1)


def program(nc, w, cst, out, dbg=None):
    with ExitStack() as ctx:
        sb, sem = tensors(nc, ctx)
        big = [ctx.enter_context(nc.psum_tensor(f"banks{i}", [P, 1024], F32)) for i in range(4)]
        bank = [big[i // 2][:, (i % 2) * 512:(i % 2 + 1) * 512] for i in range(8)]
        cwT_dram = nc.dram_tensor("cwT_dram", (E, T), F32).ap()
        const = {n: sb(n + "_c", list(cst[n].shape)) for n in ("ident", "upper", "ones", "iota8")}
        c_in = sem("const_in")
        with nc.Block() as block:
            @block.sync
            def _(sp):
                for n, t in const.items():
                    sp.dma_start(t[:, :], cst[n]).then_inc(c_in, 16)
                sp.wait_ge(c_in, 16 * len(const))

        ident = const["ident"]
        xnT = sb("xnT", [P, T])
        x_dram = nc.dram_tensor("x_dram", (B, L, D), F32).ap()
        vT_dram = nc.dram_tensor("vT_dram", (P, T), F32).ap()
        a_dram = nc.dram_tensor("a_dram", (BH, HD, L), F32).ap()
        k_stack = nc.dram_tensor("k_stack", (B, 2, ROWS, NSLOT, L), BF16).ap()
        q_stack = nc.dram_tensor("q_stack", (B, 2, ROWS, NSLOT, L), BF16).ap()
        max_dram = nc.dram_tensor("max_dram", (B, 2, NSLOT, 3, P), BF16).ap()
        sum_dram = nc.dram_tensor("sum_dram", (B, P, LT, P), F32).ap()
        more = {**w, **cst, "bank": bank, "big": big, "ident": ident, "cwT_dram": cwT_dram}
        with ExitStack() as layer:
            sb, _ = tensors(nc, layer)
            x, xn, s = sb("x", [P, NT, D]), sb("xn", [P, NT, D]), sb("s", [P, NT, D])
            normalise(nc, "n0_", w["L0_attn_x"], x, xn, xnT, ident, bank)
            linear_attention(nc, xn, xnT, s, {n: w["L0_attn_" + n] for n in ("Wq", "Wk", "Wv", "Wo", "bo", "gamma", "beta")},
                             ident, bank)
            gate(nc, "g0_", xnT, w["L0_rwT"], None, cwT_dram, const, bank)
            acc = sb("acc", [P, T])
            experts(nc, "e0_", xnT, acc, w["L0_w1T"], w["L0_w2T"], w["L0_b1T"], w["L0_ffn_b2"], cwT_dram, bank)
            combine(nc, "c0_", x, s, acc, x, x_dram, ident, bank)
            normalise(nc, "n1_", None, x, xn, xnT, ident, bank)
        gate(nc, "g1_", xnT, w["L1_ffn_w_g"], CAP, cwT_dram, const, bank)
        acc = ctx.enter_context(nc.sbuf_tensor("acc1", [P, T], F32))
        with ExitStack() as layer:
            sb, _ = tensors(nc, layer)
            A = sb("A", [P, HD, L])
            project_qkv(nc, xnT, more, k_stack, q_stack, vT_dram, A)
            solve_attention(nc, A, xnT, acc, more, k_stack, q_stack, max_dram, sum_dram, a_dram)
        with ExitStack() as layer:
            sb, _ = tensors(nc, layer)
            x, s = sb("x1", [P, NT, D]), sb("s1", [P, NT, D])
            project_out(nc, x, x_dram, s, more, a_dram)
            combine(nc, "c1_", x, s, acc, x, out, ident, bank)


def _layouts(a):
    w = {n: a[n] for n in ("L0_attn_x", "L0_attn_Wq", "L0_attn_Wk", "L0_attn_Wv", "L0_attn_Wo", "L0_attn_bo",
                           "L0_attn_gamma", "L0_attn_beta", "L0_ffn_b2")}
    w["L0_rwT"] = a["L0_ffn_router_w"].T
    w["L0_w1T"] = a["L0_ffn_w1"].transpose(0, 2, 1)
    w["L0_w2T"] = a["L0_ffn_w2"].transpose(0, 2, 1)
    w["L0_b1T"] = a["L0_ffn_b1"].reshape(E, HC, P).transpose(0, 2, 1)
    for n in ("L1_ffn_w_g", "L1_ffn_c_fc", "L1_ffn_c_proj"):
        w[n] = a[n]
    order = np.arange(D).reshape(NSLOT, 2, HD).transpose(1, 2, 0)
    swap = order[:, [1, 0, *range(2, HD)]].ravel()
    order = order.ravel()
    wq, wk, wv = a["L1_attn_Wqkv"].reshape(3, D, D)
    bq, bk, bv = a["L1_attn_bqkv"].reshape(3, D)
    w["wqkvT"] = np.concatenate([wq[order], wk[order], wv]).T
    w["wswapT"] = np.concatenate([wq[swap], wk[swap]]).T
    w["qkv_bias"] = np.stack([bq[order], bk[order], bv, bq[swap], bk[swap]], axis=1)
    w["wdT"] = a["L1_attn_Wd"].T
    w["bd"] = a["L1_attn_bd"]
    return w


def _constants():
    i = np.arange(P)
    t = np.arange(L, dtype=np.float32)
    rot = np.zeros((2, HD, NSLOT, 2, L), np.float32)
    rot[:, :, :, 0], rot[:, :2, :, 0] = 1.0, np.cos(t)
    rot[:, 0, :, 1], rot[:, 1, :, 1] = -np.sin(t), np.sin(t)
    later = np.where(i[None, :] > i[:, None], BIG, 0.0)
    return {
        "rot": rot.reshape(P, 2, L),
        "masks": np.stack([later, later.T], axis=1).astype(np.float32),
        "ident": np.eye(P, dtype=np.float32),
        "upper": (i[:, None] < i[None, :]).astype(np.float32),
        "ones": np.ones((P, P), np.float32),
        "iota8": np.tile(np.arange(8, dtype=np.float32), (P, 1)),
    }


def kernel(**inputs):
    import concourse.bacc as _bacc
    from concourse import mybir as _mybir
    from concourse.bass_utils import run_bass_kernel_spmd as _run

    nc = _bacc.Bacc("TRN2", target_bir_lowering=False, num_devices=1)
    arrays = {}

    def dram(group):
        args = {}
        for name, a in group.items():
            a = np.ascontiguousarray(a)
            arrays[f"in_{name}_dram"] = a
            args[name] = nc.dram_tensor(f"in_{name}_dram", a.shape, _mybir.dt.from_np(a.dtype), kind="ExternalInput").ap()
        return args

    w = dram(_layouts({n: np.asarray(v) for n, v in inputs.items()}))
    cst = dram(_constants())
    out = nc.dram_tensor("out_0_dram", (B, L, D), F32, kind="ExternalOutput").ap()
    program(nc, w, cst, out)
    r = _run(nc, [arrays], core_ids=[0])
    return r.results[0]["out_0_dram"]
```

```python
from contextlib import ExitStack
from itertools import count

import concourse.bass as bass
import numpy as np
from concourse import mybir

P = 128
B, L, D = 8, 512, 128
T = B * L
NT = T // P
LT = L // P
E, H = 8, 512
HC = H // P
NH = 16
HD = D // NH
BH = B * NH
CAP = 1280
GROUP = 4
OWN = 8
PRODS = 4
RING = 32
STEP_COST = 9.0
AHEAD = 16
NSLOT = NH // 2
K_PARTS = (0, 1, 2, 0, 1, 0)
Q_PARTS = (0, 0, 0, 1, 1, 2)
ROWS = len(K_PARTS) * HD
PAD = P // 2 - ROWS
EPS = 1e-5
BIG = -2.0 ** 100

F32 = mybir.dt.float32
BF16 = mybir.dt.bfloat16
F32R = mybir.dt.float32r
U32 = mybir.dt.uint32
ALU = mybir.AluOpType
ACT = mybir.ActivationFunctionType
AX_X = mybir.AxisListType.X


STAGES = count()


class Chain:

    def __init__(self, eng, sem):
        self.eng, self.sem, self.n = eng, sem, 0

    def __call__(self, ins):
        self.n += 1
        ins.then_inc(self.sem, 1)
        self.eng.wait_ge(self.sem, self.n)


def tensors(nc, ctx):
    sems, stage = [], next(STAGES)

    def sb(name, shape, dt=F32):
        return ctx.enter_context(nc.sbuf_tensor(name, shape, dt))

    def sem(name):
        sems.append(nc.alloc_semaphore(f"{name}_{stage}"))
        return sems[-1]

    def clear():
        if sems:
            nc.clear_and_free_semaphores(sems)
            nc.all_engine_barrier()

    ctx.callback(clear)

    return sb, sem


def normalise(nc, name, x_dram, x, xn, xnT, wg, ident, bank, loads=None):
    G = LT
    with ExitStack() as ctx:
        sb, sem = tensors(nc, ctx)
        stats = sb(name + "stats", [P, NT, 6])
        mv = sb(name + "mv", [P, NT, 2])
        rstd = sb(name + "rstd", [P, NT])
        x_in = [sem(f"{name}x_in{g}") for g in range(B)]
        dve_done, xn_ready = sem(name + "dve_done"), sem(name + "xn_ready")
        turned, copied = sem(name + "turned"), sem(name + "copied")
        var_ready, std_ready = sem(name + "var_ready"), sem(name + "std_ready")
        block = ctx.enter_context(nc.Block())

        @block.sync
        def _(sp):
            if x_dram is not None:
                for g in range(B):
                    sp.dma_start(x[:, g * G:(g + 1) * G, :],
                                 x_dram[g].rearrange("(t p) d -> p t d", p=P)).then_inc(x_in[g], 16)
            if loads:
                loads(sp)

        @block.vector
        def _(dve):
            link = Chain(dve, dve_done)

            def statistics(g):
                s = slice(g * G, (g + 1) * G)
                if x_dram is not None:
                    dve.wait_ge(x_in[g], 16)
                for t in range(g * G, (g + 1) * G):
                    last = nc.vector.bn_stats(stats[:, t, :], x[:, t, :])
                link(last)
                for t in range(g * G, (g + 1) * G):
                    last = nc.vector.bn_aggr(mv[:, t, :], stats[:, t, :])
                link(last)
                nc.vector.tensor_scalar(rstd[:, s], mv[:, s, 1], EPS, None, ALU.add).then_inc(var_ready, 1)

            def scale(g):
                dve.wait_ge(std_ready, g + 1)
                s = slice(g * G, (g + 1) * G)
                link(nc.vector.reciprocal(rstd[:, s], rstd[:, s]))
                for t in range(g * G, (g + 1) * G):
                    last = nc.vector.tensor_scalar(xn[:, t, :], x[:, t, :], mv[:, t, 0:1], rstd[:, t:t + 1],
                                                   ALU.subtract, ALU.mult)
                last.then_inc(xn_ready, 1)

            statistics(0)
            for g in range(B):
                if g + 1 < B:
                    statistics(g + 1)
                scale(g)

        @block.tensor
        def _(pe):
            def gate_logits(g):
                pe.wait_ge(copied, g + 1)
                for t in range(g * G, (g + 1) * G):
                    nc.tensor.matmul(bank[7][:, t * E:(t + 1) * E], xnT[:, t * P:(t + 1) * P], wg[:, :], start=True, stop=True)

            for g in range(B):
                pe.wait_ge(xn_ready, g + 1)
                if g >= 2:
                    pe.wait_ge(copied, g - 1)
                for t in range(G):
                    last = nc.tensor.transpose(bank[g % 2][:, t * P:(t + 1) * P], xn[:, g * G + t, :], ident[:, :])
                last.then_inc(turned, 1)
                if g:
                    gate_logits(g - 1)
            gate_logits(B - 1)

        @block.scalar
        def _(act):
            def root(g):
                act.wait_ge(var_ready, g + 1)
                nc.scalar.activation(rstd[:, g * G:(g + 1) * G], rstd[:, g * G:(g + 1) * G], ACT.Sqrt).then_inc(std_ready, 1)

            root(0)
            for g in range(B):
                if g + 1 < B:
                    root(g + 1)
                act.wait_ge(turned, g + 1)
                nc.scalar.copy(xnT[:, g * L:(g + 1) * L], bank[g % 2][:, :]).then_inc(copied, 1)


def linear_attention(nc, xn, xnT, s, rows, mv, rstd, wk, wqv, wo, w_in, ident, bank):
    with ExitStack() as ctx:
        sb, sem = tensors(nc, ctx)
        ek, ekT = sb("ek", [P, L]), sb("ekT", [P, LT, P])
        eq, eqT = sb("eq", [P, LT, P]), sb("eqT", [P, L])
        v = sb("v", [P, LT, P])
        ctxT, cw = sb("ctxT", [P, P]), sb("cw", [P, P])
        neg_kmax, ksum, rk = sb("neg_kmax", [P, 1]), sb("ksum", [P, 2]), sb("rk", [P, 1])
        neg_qmax, qsum, rq = sb("neg_qmax", [P, LT]), sb("qsum", [P, 2, LT]), sb("rq", [P, LT])
        stats = sb("ystats", [P, LT, 6])
        k_mm, qv_mm, k_max, q_max = sem("k_mm"), sem("qv_mm"), sem("k_max"), sem("q_max")
        k_exp, q_exp, v_copy = sem("k_exp"), sem("q_exp"), sem("v_copy")
        k_turned, q_turned, k_copied, q_copied = sem("k_turned"), sem("q_turned"), sem("k_copied"), sem("q_copied")
        ctx_mm, ctx_copied, cw_mm, cw_copied = sem("ctx_mm"), sem("ctx_copied"), sem("cw_mm"), sem("cw_copied")
        var_ready, std_ready = sem("yvar_ready"), sem("ystd_ready")
        out_mm, out_read, dve_done = sem("out_mm"), sem("out_read"), sem("attn_dve_done")
        block = ctx.enter_context(nc.Block())
        ps_k, ps_qv, ps_kT, ps_qT, ps_c, ps_o = bank[0], (bank[1], bank[2]), bank[3], bank[4], bank[5], bank[6]

        @block.tensor
        def _(pe):
            def project(b):
                if b >= 1:
                    pe.wait_ge(k_exp, b)
                nc.tensor.matmul(ps_k[:, :], wk[:, :], xnT[:, b * L:(b + 1) * L], start=True, stop=True).then_inc(k_mm, 1)
                if b >= 1:
                    pe.wait_ge(q_exp, b)
                    pe.wait_ge(v_copy, b)
                for t in range(LT):
                    last = nc.tensor.matmul(ps_qv[t // 2][:, (t % 2) * 256:(t % 2 + 1) * 256],
                                            xnT[:, b * L + t * P:b * L + (t + 1) * P],
                                            wqv[:, :, :].rearrange("p a d -> p (a d)"), start=True, stop=True)
                last.then_inc(qv_mm, 1)

            pe.wait_ge(w_in, 16 * 7)
            def turn_k(b):
                pe.wait_ge(k_exp, b + 1)
                if b >= 1:
                    pe.wait_ge(k_copied, b)
                for t in range(LT):
                    last = nc.tensor.transpose(ps_kT[:, t * P:(t + 1) * P], ek[:, t * P:(t + 1) * P], ident[:, :])
                last.then_inc(k_turned, 1)

            def turn_q(b):
                pe.wait_ge(q_exp, b + 1)
                if b >= 1:
                    pe.wait_ge(q_copied, b)
                for t in range(LT):
                    last = nc.tensor.transpose(ps_qT[:, t * P:(t + 1) * P], eq[:, t, :], ident[:, :])
                last.then_inc(q_turned, 1)

            project(0)
            turn_k(0)
            turn_q(0)
            for b in range(B):
                if b + 1 < B:
                    project(b + 1)
                pe.wait_ge(k_copied, b + 1)
                pe.wait_ge(v_copy, b + 1)
                if b >= 1:
                    pe.wait_ge(cw_copied, b)
                for t in range(LT):
                    last = nc.tensor.matmul(ps_c[:, 0:P], v[:, t, :], ekT[:, t, :], start=(t == 0), stop=(t == LT - 1))
                last.then_inc(ctx_mm, 1)
                if b + 1 < B:
                    turn_k(b + 1)
                pe.wait_ge(ctx_copied, b + 1)
                nc.tensor.matmul(ps_c[:, P:2 * P], ctxT[:, :], wo[:, :], start=True, stop=True).then_inc(cw_mm, 1)
                if b + 1 < B:
                    turn_q(b + 1)
                pe.wait_ge(cw_copied, b + 1)
                pe.wait_ge(q_copied, b + 1)
                if b >= 1:
                    pe.wait_ge(out_read, b)
                for t in range(LT):
                    last = nc.tensor.matmul(ps_o[:, t * P:(t + 1) * P], eqT[:, t * P:(t + 1) * P], cw[:, :],
                                            start=True, stop=True)
                last.then_inc(out_mm, 1)

        @block.scalar
        def _(act):
            for b in range(B):
                act.wait_ge(k_max, b + 1)
                if b >= 1:
                    act.wait_ge(k_turned, b)
                if b >= 2:
                    act.wait_ge(cw_copied, b - 1)
                nc.scalar.activation(ek[:, :], ps_k[:, :], ACT.Exp, bias=neg_kmax[:, 0:1],
                                     accum_out=ksum[:, b % 2:b % 2 + 1]).then_inc(k_exp, 1)
                act.wait_ge(qv_mm, b + 1)
                act.wait_ge(q_max, b + 1)
                if b >= 1:
                    act.wait_ge(ctx_mm, b)
                for i in range(2):
                    last = nc.scalar.copy(v[:, 2 * i:2 * i + 2, :],
                                          ps_qv[i][:, :].rearrange("p (t a d) -> p t a d", t=2, a=2)[:, :, 1, :])
                last.then_inc(v_copy, 1)
                if b >= 1:
                    act.wait_ge(q_turned, b)
                if b >= 2:
                    act.wait_ge(out_read, b - 1)
                for t in range(LT):
                    last = nc.scalar.activation(eq[:, t, :], ps_qv[t // 2][:, (t % 2) * 256:(t % 2) * 256 + P], ACT.Exp,
                                                bias=neg_qmax[:, t:t + 1], accum_out=qsum[:, b % 2, t:t + 1])
                last.then_inc(q_exp, 1)
                act.wait_ge(q_turned, b + 1)
                if b >= 1:
                    act.wait_ge(out_mm, b)
                nc.scalar.copy(eqT[:, :], ps_qT[:, :]).then_inc(q_copied, 1)
            act.wait_ge(var_ready, 1)
            nc.scalar.activation(rstd[:, :], rstd[:, :], ACT.Sqrt).then_inc(std_ready, 1)

        @block.vector
        def _(dve):
            link = Chain(dve, dve_done)

            def row(i):
                return rows[:, i:i + 1, :].broadcast_to([P, LT, D])

            def maxima(b):
                dve.wait_ge(k_mm, b + 1)
                nc.vector.tensor_reduce(neg_kmax[:, :], ps_k[:, :], AX_X, ALU.max, negate=True).then_inc(k_max, 1)
                dve.wait_ge(qv_mm, b + 1)
                for i in range(2):
                    last = nc.vector.tensor_reduce(neg_qmax[:, 2 * i:2 * i + 2],
                                                   ps_qv[i][:, :].rearrange("p (t a d) -> p t a d", t=2, a=2)[:, :, 0, :],
                                                   AX_X, ALU.max, negate=True)
                last.then_inc(q_max, 1)

            dve.wait_ge(w_in, 16 * 7)
            def keys(b):
                dve.wait_ge(k_turned, b + 1)
                if b >= 1:
                    dve.wait_ge(ctx_mm, b)
                nc.vector.tensor_copy(ekT[:, :, :].rearrange("p t d -> p (t d)"), ps_kT[:, :]).then_inc(k_copied, 1)
                if b >= 1:
                    dve.wait_ge(cw_copied, b)
                link(nc.vector.reciprocal(rk[:, :], ksum[:, b % 2:b % 2 + 1]))

            maxima(0)
            keys(0)
            for b in range(B):
                dve.wait_ge(q_exp, b + 1)
                link(nc.vector.reciprocal(rq[:, :], qsum[:, b % 2, :]))
                if b + 1 < B:
                    maxima(b + 1)
                dve.wait_ge(ctx_mm, b + 1)
                if b >= 1:
                    dve.wait_ge(cw_mm, b)
                nc.vector.tensor_copy(ctxT[:, :], ps_c[:, 0:P]).then_inc(ctx_copied, 1)
                dve.wait_ge(cw_mm, b + 1)
                if b >= 1:
                    dve.wait_ge(out_mm, b)
                nc.vector.tensor_scalar(cw[:, :], ps_c[:, P:2 * P], rk[:, 0:1], float(D) ** -0.5, ALU.mult,
                                        ALU.mult).then_inc(cw_copied, 1)
                if b + 1 < B:
                    keys(b + 1)
                dve.wait_ge(out_mm, b + 1)
                y = s[:, b * LT:(b + 1) * LT, :]
                for t in range(LT):
                    last = nc.vector.scalar_tensor_tensor(out=y[:, t, :], in0=ps_o[:, t * P:(t + 1) * P],
                                                          scalar=rq[:, t:t + 1], in1=xn[:, b * LT + t, :],
                                                          op0=ALU.mult, op1=ALU.add)
                last.then_inc(out_read, 1)
                dve.wait_ge(out_read, b + 1)
                link(nc.vector.tensor_tensor(y, y, row(0), ALU.add))
                for t in range(LT):
                    last = nc.vector.bn_stats(stats[:, t, :], y[:, t, :])
                link(last)
                for t in range(LT):
                    last = nc.vector.bn_aggr(mv[:, b * LT + t, :], stats[:, t, :])
                link(last)
            nc.vector.tensor_scalar(rstd[:, :], mv[:, :, 1], EPS, None, ALU.add).then_inc(var_ready, 1)
            dve.wait_ge(std_ready, 1)
            link(nc.vector.reciprocal(rstd[:, :], rstd[:, :]))


def finish_layernorm(nc, pool, done, part, b, s, rows, mv, rstd):
    if part == 0:
        if b:
            pool.wait_ge(done, b)
        for t in range(b * LT, (b + 1) * LT):
            last = nc.gpsimd.tensor_scalar(s[:, t, :], s[:, t, :], mv[:, t, 0:1], rstd[:, t:t + 1], ALU.subtract, ALU.mult)
        last.then_inc(done, 1)
    else:
        y = s[:, b * LT:(b + 1) * LT, :]
        for n, op in ((0, ALU.mult), (1, ALU.add)):
            pool.wait_ge(done, B + 2 * b + n)
            nc.gpsimd.tensor_tensor(y, y, rows[:, n + 1:n + 2, :].broadcast_to([P, LT, D]), op).then_inc(done, 1)


def gate(nc, name, capacity, cw, cwT_dram, const, bank, loads=None):
    with ExitStack() as ctx:
        sb, sem = tensors(nc, ctx)
        logit = sb(name + "logit", [P, NT, E])
        top = sb(name + "top", [P, NT, 8])
        idx = sb(name + "idx", [P, NT, 8], U32)
        idxf = sb(name + "idxf", [P, 2, NT])
        oh = sb(name + "oh", [P, 2, E, NT])
        wt = sb(name + "wt", [P, 2, NT])
        gap = sb(name + "gap", [P, NT])
        cw2 = sb(name + "cw2", [P, E, NT])
        cwT = sb(name + "cwT", [P, 2, P])
        totals = sb(name + "totals", [P, 2, E, NT])
        before = sb(name + "before", [P, 2, E, NT])
        oh_ready = sem(name + "oh_ready")
        gap_ready, gap_exp, dve_done = sem(name + "gap_ready"), sem(name + "gap_exp"), sem(name + "dve_done")
        ranks_mm, cw_ready, cw_turned = sem(name + "ranks_mm"), sem(name + "cw_ready"), sem(name + "cw_turned")
        cw_copied, cw_out = sem(name + "cw_copied"), sem(name + "cw_out")
        block = ctx.enter_context(nc.Block())
        iota8, ones, upper, ident = const["iota8"], const["ones"], const["upper"], const["ident"]

        @block.sync
        def _(sp):
            if loads:
                loads(sp)
            if cwT_dram is not None:
                sp.wait_ge(cw_copied, 1)
                for h in range(2):
                    sp.dma_start(cwT_dram.rearrange("(h e) (t p) -> h (e t) p", h=2, p=P)[h],
                                 cwT[:, h, :]).then_inc(cw_out, 16)
                sp.wait_ge(cw_out, 32)

        @block.tensor
        def _(pe):
            if capacity:
                pe.wait_ge(oh_ready, 1)
                ohf = oh[:, :, :, :].rearrange("p k e t -> p (k e t)")
                nc.tensor.matmul(bank[1][:, :], upper[:, :], ohf, start=True, stop=True)
                nc.tensor.matmul(bank[2][:, :], ones[:, :], ohf, start=True, stop=True).then_inc(ranks_mm, 1)
            if cwT_dram is not None:
                pe.wait_ge(cw_ready, 1)
                for h in range(2):
                    last = nc.tensor.transpose(bank[3][:, h * P:(h + 1) * P],
                                               cw[:, h * 4:(h + 1) * 4, :].rearrange("p e t -> p (e t)"), ident[:, :])
                last.then_inc(cw_turned, 1)

        @block.scalar
        def _(act):
            act.wait_ge(gap_ready, 1)
            nc.scalar.activation(gap[:, :], gap[:, :], ACT.Exp).then_inc(gap_exp, 1)

        @block.vector
        def _(dve):
            link = Chain(dve, dve_done)
            link(nc.vector.tensor_copy(logit[:, :, :].rearrange("p t e -> p (t e)"), bank[7][:, 0:NT * E]))
            for t in range(NT):
                last = nc.vector.max(top[:, t, :], logit[:, t, :])
            link(last)
            for t in range(NT):
                last = nc.vector.max_index(idx[:, t, :], top[:, t, :], logit[:, t, :])
            link(last)
            nc.vector.tensor_tensor(gap[:, :], top[:, :, 1], top[:, :, 0], ALU.subtract).then_inc(gap_ready, 1)
            link(nc.vector.tensor_copy(idxf[:, :, :], idx[:, :, 0:2].rearrange("p t k -> p k t")))
            for k in range(2):
                last = nc.vector.tensor_tensor(oh[:, k, :, :], iota8[:, :].rearrange("p (e a) -> p e a", a=1).broadcast_to([P, E, NT]),
                                               idxf[:, k:k + 1, :].broadcast_to([P, E, NT]), ALU.is_equal)
            last.then_inc(oh_ready, 1)
            dve.wait_ge(oh_ready, 1)
            dve.wait_ge(gap_exp, 1)
            link(nc.vector.tensor_scalar(wt[:, 1, :], gap[:, :], 1.0, None, ALU.add))
            link(nc.vector.reciprocal(wt[:, 0, :], wt[:, 1, :]))
            link(nc.vector.tensor_tensor(wt[:, 1, :], gap[:, :], wt[:, 0, :], ALU.mult))
            if capacity:
                flat = "p k e t -> p (k e t)"
                dve.wait_ge(ranks_mm, 1)
                link(nc.vector.tensor_copy(totals[:, :, :, :].rearrange(flat), bank[2][:, :]))
                for k in range(2):
                    for e in range(E):
                        last = nc.vector.tensor_tensor_scan(before[:, k, e, :], ones[:, 0:NT], totals[:, k, e, :],
                                                            0.0 if k == 0 else before[:, 0, e, NT - 1:NT],
                                                            ALU.mult, ALU.add)
                    link(last)
                link(nc.vector.tensor_tensor(before[:, :, :, :], before[:, :, :, :], totals[:, :, :, :], ALU.subtract))
                link(nc.vector.tensor_tensor(before[:, :, :, :].rearrange(flat), before[:, :, :, :].rearrange(flat), bank[1][:, :], ALU.add))
                link(nc.vector.scalar_tensor_tensor(out=oh[:, :, :, :].rearrange(flat), in0=before[:, :, :, :].rearrange(flat),
                                                    scalar=float(capacity), in1=oh[:, :, :, :].rearrange(flat),
                                                    op0=ALU.is_lt, op1=ALU.mult))
            link(nc.vector.tensor_tensor(cw2[:, :, :], oh[:, 0, :, :], wt[:, 0:1, :].broadcast_to([P, E, NT]), ALU.mult))
            link(nc.vector.tensor_tensor(cw[:, :, :], oh[:, 1, :, :], wt[:, 1:2, :].broadcast_to([P, E, NT]), ALU.mult))
            nc.vector.tensor_tensor(cw[:, :, :], cw[:, :, :], cw2[:, :, :], ALU.add).then_inc(cw_ready, 1)
            if cwT_dram is not None:
                dve.wait_ge(cw_turned, 1)
                nc.vector.tensor_copy(cwT[:, :, :].rearrange("p h q -> p (h q)"), bank[3][:, 0:2 * P]).then_inc(cw_copied, 1)


def experts(nc, name, xnT, acc, w1_dram, w2_dram, b1_dram, b2_dram, cwT_dram, bank, finish):
    NC = T // L
    HALVES = 2
    HH = HC // HALVES
    with ExitStack() as ctx:
        sb, sem = tensors(nc, ctx)
        w1 = [sb(f"{name}w1_{i}", [P, H]) for i in range(2)]
        w2 = [sb(f"{name}w2_{i}", [P, H]) for i in range(2)]
        ws = [sb(f"{name}ws_{i}", [P, 2, 2, H], F32R) for i in range(2)]
        b1 = [sb(f"{name}b1_{i}", [P, HC]) for i in range(2)]
        cwb = [sb(f"{name}cwb_{i}", [P, T]) for i in range(2)]
        b2 = sb(name + "b2", [E, D])
        x_hi, x_lo = sb(name + "x_hi", [P, T], F32R), sb(name + "x_lo", [P, T], F32R)
        h = sb(name + "h", [P, HC, L])
        hs = [sb(f"{name}hs{i}", [P, 2, HC, L], F32R) for i in range(2)]
        cwT = cwb[1][0:E, :]
        term = sb(name + "term", [P, 2, L])
        w_in, aux_in = [sem(f"{name}w_in{i}") for i in range(2)], [sem(f"{name}aux_in{i}") for i in range(2)]
        b2_in, up_mm, gelu_done = sem(name + "b2_in"), sem(name + "up_mm"), sem(name + "gelu_done")
        down_mm, term_done, acc_done = sem(name + "down_mm"), sem(name + "term_done"), sem(name + "acc_done")
        bias_mm, acc_set = sem(name + "bias_mm"), sem(name + "acc_set")
        x_hi_done, x_lo_done, w_hi_done, w_split = sem(name + "x_hi"), sem(name + "x_lo_done"), sem(name + "w_hi"), sem(name + "w_split")
        h_hi_done, h_split, finished = sem(name + "h_hi"), sem(name + "h_split"), sem(name + "finished")
        block = ctx.enter_context(nc.Block())

        def over_steps(step, eng):
            for i in range(2):
                for c in range(NC):
                    step(0, i, c, i == 0)
            with eng.Fori(1, E // 2) as pair:
                for i in range(2):
                    for c in range(NC):
                        step(pair, i, c, False)

        @block.sync
        def _(sp):
            def load_w(e, i):
                sp.dma_start(w1[i][:, :], w1_dram[bass.ds(e, 1)].rearrange("a d h -> (a d) h")).then_inc(w_in[i], 16)
                sp.dma_start(w2[i][:, :].rearrange("p (c d) -> p c d", c=HC),
                             w2_dram[bass.ds(e, 1)].rearrange("a (c p) d -> p (a c) d", p=P)).then_inc(w_in[i], 16)

            def load_aux(e, i):
                sp.dma_start(b1[i][:, :], b1_dram[bass.ds(e, 1)].rearrange("a p c -> (a p) c")).then_inc(aux_in[i], 16)
                sp.dma_start(cwb[i][:, :], cwT_dram[bass.ds(e, 1), :].broadcast_to([P, T])).then_inc(aux_in[i], 16)

            load_w(0, 0)
            sp.dma_start(b2[:, :], b2_dram).then_inc(b2_in, 16)
            sp.dma_start(cwT, cwT_dram).then_inc(b2_in, 16)
            load_aux(0, 0)
            load_w(1, 1)
            sp.wait_ge(bias_mm, NC)
            load_aux(1, 1)
            with sp.Fori(1, E // 2) as pair:
                for i in range(2):
                    e = pair * 2 + i
                    sp.wait_ge(w_split, e - 1)
                    load_w(e, i)
                    sp.wait_ge(term_done, (e - 1) * NC)
                    load_aux(e, i)

        @block.tensor
        def _(pe):
            def three(out, w, left, right, cols, start, stop):
                for n, (a, b) in enumerate(((0, 0), (0, 1), (1, 0))):
                    last = nc.tensor.matmul(out, w[:, left, a, cols], right[b], start=(start and n == 0), stop=(stop and n == 2))
                return last

            def up(pair, i, c, first):
                k = (pair * 2 + i) * NC + c
                if c == 0:
                    pe.wait_ge(w_split, pair * 2 + i + 1)
                if first:
                    pe.wait_ge(x_lo_done, c + 1)
                x = [t[:, c * L:(c + 1) * L] for t in (x_hi, x_lo)]
                for hc in range(HC):
                    if not (first and c == 0):
                        pe.wait_ge(gelu_done, k * HC + (hc + 1 - HC))
                    three(bank[hc][:, :], ws[i], 0, x, slice(hc * P, (hc + 1) * P), True, True).then_inc(up_mm, 1)

            def down(pair, i, c, first):
                k = (pair * 2 + i) * NC + c
                pe.wait_ge(h_split, k * HALVES + HALVES)
                if not first:
                    pe.wait_ge(term_done, k - 1)
                for hc in range(HC):
                    last = three(bank[4 + c % 2][:, :], ws[i], 1, [hs[c % 2][:, j, hc, :] for j in range(2)],
                                 slice(hc * P, (hc + 1) * P), hc == 0, hc == HC - 1)
                last.then_inc(down_mm, 1)

            def step(pair, i, c, first):
                up(pair, i, c, first)
                if c:
                    down(pair, i, c - 1, first and c < 3)
                elif i:
                    down(pair, 0, NC - 1, False)
                elif not first:
                    down(pair - 1, 1, NC - 1, False)

            pe.wait_ge(b2_in, 32)
            for c in range(NC):
                if c >= 2:
                    pe.wait_ge(acc_set, c - 1)
                nc.tensor.matmul(bank[6 + c % 2][:, :], b2[:, :], cwT[:, c * L:(c + 1) * L],
                                 start=True, stop=True).then_inc(bias_mm, 1)
            over_steps(step, pe)
            down(E // 2 - 1, 1, NC - 1, False)

        @block.scalar
        def _(act):
            def step(pair, i, c, first):
                k = (pair * 2 + i) * NC + c
                if c == 0:
                    act.wait_ge(aux_in[i], (pair + 1) * 32)

                def gelu(hc):
                    act.wait_ge(up_mm, k * HC + (hc + 1))
                    if not (first and c == 0) and hc % HH == 0:
                        act.wait_ge(h_split, k * HALVES + (hc // HH + 1 - HALVES))
                    nc.scalar.activation(h[:, hc, :], bank[hc][:, :], ACT.Gelu, bias=b1[i][:, hc:hc + 1]).then_inc(gelu_done, 1)

                def hi(half):
                    act.wait_ge(gelu_done, k * HC + (half + 1) * HH)
                    if half == 0 and not (first and c < 2):
                        act.wait_ge(down_mm, k - 1)
                    nc.scalar.copy(hs[c % 2][:, 0, half * HH:(half + 1) * HH, :], h[:, half * HH:(half + 1) * HH, :]).then_inc(h_hi_done, 1)

                for hc in range(HC):
                    gelu(hc)
                    if hc >= HH and hc % HH == 0:
                        hi(hc // HH - 1)
                hi(HALVES - 1)

            for c in range(NC):
                nc.scalar.copy(x_hi[:, c * L:(c + 1) * L], xnT[:, c * L:(c + 1) * L]).then_inc(x_hi_done, 1)
            over_steps(step, act)

        @block.gpsimd
        def _(pool):
            def step(pair, i, c, first):
                k = (pair * 2 + i) * NC + c
                pool.wait_ge(term_done, k + 1)
                if not (first and c == 0):
                    pool.wait_ge(acc_done, k)
                out = acc[:, c * L:(c + 1) * L]
                nc.gpsimd.tensor_tensor(out, out, term[:, c % 2, :], ALU.add).then_inc(acc_done, 1)
                if isinstance(pair, int):
                    finish_layernorm(nc, pool, finished, i, c, *finish)

            pool.wait_ge(acc_set, NC)
            over_steps(step, pool)

        @block.vector
        def _(dve):
            def split_w(pair, i, first):
                e = pair * 2 + i
                dve.wait_ge(w_in[i], (pair + 1) * 32)
                if not first:
                    dve.wait_ge(down_mm, (e - 1) * NC)
                for n, w in enumerate((w1[i], w2[i])):
                    nc.vector.tensor_copy(ws[i][:, n, 0, :], w[:, :]).then_inc(w_hi_done, 1)
                for n, w in enumerate((w1[i], w2[i])):
                    dve.wait_ge(w_hi_done, e * 2 + (n + 1))
                    last = nc.vector.tensor_tensor(ws[i][:, n, 1, :], w[:, :], ws[i][:, n, 0, :], ALU.subtract)
                last.then_inc(w_split, 1)

            def weigh(pair, i, c, first):
                k = (pair * 2 + i) * NC + c
                if c == 0:
                    dve.wait_ge(aux_in[i], (pair + 1) * 32)
                if not (first and c < 2):
                    dve.wait_ge(acc_done, k - 1)
                dve.wait_ge(down_mm, k + 1)
                nc.vector.tensor_tensor(term[:, c % 2, :], bank[4 + c % 2][:, :], cwb[i][:, c * L:(c + 1) * L],
                                        ALU.mult).then_inc(term_done, 1)

            def lo(pair, i, c, half):
                k = (pair * 2 + i) * NC + c
                dve.wait_ge(h_hi_done, k * HALVES + (half + 1))
                part = slice(half * HH, (half + 1) * HH)
                nc.vector.tensor_tensor(hs[c % 2][:, 1, part, :], h[:, part, :], hs[c % 2][:, 0, part, :],
                                        ALU.subtract).then_inc(h_split, 1)

            def step(pair, i, c, first):
                for half in range(HALVES):
                    lo(pair, i, c, half)
                if c:
                    weigh(pair, i, c - 1, first)
                elif i:
                    weigh(pair, 0, NC - 1, False)
                elif not first:
                    weigh(pair - 1, 1, NC - 1, False)
                if c == 1 and i == 0 and not first:
                    split_w(pair, 1, False)

            def steps(pair, first):
                for i in range(2):
                    for c in range(NC):
                        step(pair, i, c, first and i == 0)

            split_w(0, 0, True)
            for c in range(NC):
                dve.wait_ge(x_hi_done, c + 1)
                cs = slice(c * L, (c + 1) * L)
                nc.vector.tensor_tensor(x_lo[:, cs], xnT[:, cs], x_hi[:, cs], ALU.subtract).then_inc(x_lo_done, 1)
                dve.wait_ge(bias_mm, c + 1)
                nc.vector.tensor_copy(acc[:, cs], bank[6 + c % 2][:, :]).then_inc(acc_set, 1)
            split_w(0, 1, True)
            steps(0, True)
            with dve.Fori(1, E // 2) as pair:
                split_w(pair, 0, False)
                steps(pair, False)
            weigh(E // 2 - 1, 1, NC - 1, False)


class ExpertSteps:

    NC = T // L

    def __init__(self, nc, sb, sem, xnT, acc, w1_dram, w2_dram, cw, hidden, up_banks, down_bank):
        self.nc, self.xnT, self.acc, self.cw, self.h = nc, xnT, acc, cw, hidden
        self.w1_dram, self.w2_dram = w1_dram, w2_dram
        self.up_banks, self.down_bank = up_banks, down_bank
        self.w1 = [sb(f"step_w1_{i}", [P, H]) for i in range(2)]
        self.w2 = [sb(f"step_w2_{i}", [P, HC, D]) for i in range(2)]
        self.term = sb("step_term", [P, 2, LT, D])
        self.w_in = [sem(f"step_w_in{i}") for i in range(2)]
        self.up_mm, self.gelu_done, self.down_mm = sem("step_up_mm"), sem("step_gelu"), sem("step_down_mm")
        self.term_done, self.acc_done = sem("step_term"), sem("step_acc")

    def load_expert(self, sp, e):
        if e >= 2:
            sp.wait_ge(self.down_mm, (e - 1) * self.NC)
        sp.dma_start(self.w1[e % 2][:, :], self.w1_dram[e]).then_inc(self.w_in[e % 2], 16)
        sp.dma_start(self.w2[e % 2][:, :, :], self.w2_dram[e].rearrange("(c p) d -> p c d", p=P)).then_inc(self.w_in[e % 2], 16)

    def up(self, pe, k):
        e, c = divmod(k, self.NC)
        pe.wait_ge(self.w_in[e % 2], 32 * (e // 2 + 1))
        for hc in range(HC):
            if k >= 1:
                pe.wait_ge(self.gelu_done, (k - 1) * HC + hc + 1)
            self.nc.tensor.matmul(self.up_banks[hc][:, :], self.w1[e % 2][:, hc * P:(hc + 1) * P],
                                  self.xnT[:, c * L:(c + 1) * L], start=True, stop=True).then_inc(self.up_mm, 1)

    def down(self, pe, k):
        e = k // self.NC
        pe.wait_ge(self.gelu_done, (k + 1) * HC)
        if k >= 1:
            pe.wait_ge(self.term_done, k)
        for j in range(LT):
            for hc in range(HC):
                last = self.nc.tensor.matmul(self.down_bank[:, j * P:(j + 1) * P], self.h[k % 2][:, hc, j * P:(j + 1) * P],
                                             self.w2[e % 2][:, hc, :], start=(hc == 0), stop=(hc == HC - 1))
        last.then_inc(self.down_mm, 1)

    def gelu(self, act, k):
        if k >= 2:
            act.wait_ge(self.down_mm, k - 1)
        for hc in range(HC):
            act.wait_ge(self.up_mm, k * HC + hc + 1)
            self.nc.scalar.activation(self.h[k % 2][:, hc, :], self.up_banks[hc][:, :], ACT.Gelu).then_inc(self.gelu_done, 1)

    def weigh(self, act, k):
        e, c = divmod(k, self.NC)
        if k >= self.NC + 2:
            act.wait_ge(self.acc_done, k - self.NC - 1)
        act.wait_ge(self.down_mm, k + 1)
        for j in range(LT):
            t = c * LT + j
            out = self.acc[:, t, :] if e == 0 else self.term[:, k % 2, j, :]
            last = self.nc.scalar.activation(out, self.down_bank[:, j * P:(j + 1) * P], ACT.Copy, scale=self.cw[:, e, t:t + 1])
        last.then_inc(self.term_done, 1)

    def add(self, pool, k):
        if k < self.NC:
            return
        c = k % self.NC
        pool.wait_ge(self.term_done, k + 1)
        if k > self.NC:
            pool.wait_ge(self.acc_done, k - self.NC)
        out = self.acc[:, c * LT:(c + 1) * LT, :]
        self.nc.gpsimd.tensor_tensor(out, out, self.term[:, k % 2, :, :], ALU.add).then_inc(self.acc_done, 1)


def combine(nc, name, x, s, acc, out, out_dram, stored, wait, ident, bank):
    with ExitStack() as ctx:
        sb, sem = tensors(nc, ctx)
        g = sb(name + "g", [P, 2, LT, P])
        turned, silu_done, prod_done, done = sem(name + "turned"), sem(name + "silu"), sem(name + "prod"), sem(name + "done")
        block = ctx.enter_context(nc.Block())

        @block.tensor
        def _(pe):
            for b in range(B if ident is not None else 0):
                if b >= 2:
                    pe.wait_ge(silu_done, b - 1)
                for t in range(LT):
                    last = nc.tensor.transpose(bank[b % 2][:, t * P:(t + 1) * P],
                                               acc[:, (b * LT + t) * P:(b * LT + t + 1) * P], ident[:, :])
                last.then_inc(turned, 1)

        @block.scalar
        def _(act):
            for b in range(B):
                if ident is not None:
                    act.wait_ge(turned, b + 1)
                    terms = bank[b % 2][:, :].rearrange("p (t d) -> p t d", t=LT)
                else:
                    terms = acc[:, b * LT:(b + 1) * LT, :]
                if b >= 2:
                    act.wait_ge(done, b - 1)
                nc.scalar.activation(g[:, b % 2, :, :], terms, ACT.Silu).then_inc(silu_done, 1)

        @block.vector
        def _(dve):
            for b in range(B):
                ts = slice(b * LT, (b + 1) * LT)
                dve.wait_ge(silu_done, b + 1)
                nc.vector.tensor_tensor(g[:, b % 2, :, :], g[:, b % 2, :, :], s[:, ts, :], ALU.mult).then_inc(prod_done, 1)
                dve.wait_ge(prod_done, b + 1)
                nc.vector.tensor_tensor(out[:, ts, :], g[:, b % 2, :, :], x[:, ts, :], ALU.add).then_inc(done, 1)

        @block.sync
        def _(sp):
            for b in range(B):
                sp.wait_ge(done, b + 1)
                sp.dma_start(out_dram[b].rearrange("(t p) d -> p t d", p=P),
                             out[:, b * LT:(b + 1) * LT, :]).then_inc(stored, 16)
            if wait:
                sp.wait_ge(stored, 16 * B)


def project_qkv(nc, xnT, wT, wsT, bias, rot, w_in, bank, k_stack, q_stack, vT_dram):
    with ExitStack() as ctx:
        sb, sem = tensors(nc, ctx)
        part = sb("rot_part", [P, 2, L])
        qk = sb("qk", [P, 2, 2, L])
        rest = sb("qk_rest", [P, 2, 2, L])
        split = sb("qk_split", [P, 2, B, 3, L], BF16)
        v = sb("v_chunk", [P, 2, 2, L])
        pad = sb("pad", [PAD, NSLOT * L], BF16)
        mm, rotated = sem("qkv_mm"), sem("rotated")
        hi_done, rest_done, mid_done, split_done = sem("hi_done"), sem("rest_done"), sem("mid_done"), sem("split_done")
        part_done, v_done, v_out = sem("part_done"), sem("v_done"), [sem(f"v_out{i}") for i in range(2)]
        stacked = sem("stacked")
        ones_set, pad_out = sem("ones_set"), sem("pad_out")
        block = ctx.enter_context(nc.Block())

        @block.gpsimd
        def _(pool):
            nc.gpsimd.memset(pad[:, :], 1.0).then_inc(ones_set, 1)

        GROUPS = ((0, 2), (2, 5), (5, B))

        @block.sync
        def _(sp):
            sp.wait_ge(ones_set, 1)
            for b in range(B):
                sp.dma_start(k_stack[b, :, ROWS:].rearrange("h r s t -> r h (s t)"),
                             pad[:, :].rearrange("p (a q) -> p a q", a=1).broadcast_to([PAD, 2, NSLOT * L])).then_inc(pad_out, 16)
            for n in range(B // 2):
                sp.wait_ge(v_done, 2 * n + 2)
                sp.dma_start(vT_dram[:, 2 * n * L:(2 * n + 2) * L], v[:, n % 2, :, :].rearrange("p b t -> p (b t)")).then_inc(v_out[n % 2], 16)
                for b0, b1 in GROUPS:
                    if b1 not in (2 * n + 1, 2 * n + 2):
                        continue
                    for i, (stack, parts) in enumerate(((q_stack, Q_PARTS), (k_stack, K_PARTS))):
                        sp.wait_ge(split_done, 2 * (b1 - 1) + i + 1)
                        for term, p in enumerate(parts):
                            for hh in range(2):
                                sp.dma_start(stack[b0:b1, hh, term * HD:(term + 1) * HD].rearrange("b d s t -> (d s) b t"),
                                             split[64 * hh:64 * hh + 64, i, b0:b1, p, :]).then_inc(stacked, 16)
            for i in range(2):
                sp.wait_ge(v_out[i], 16 * (B // 4))
            sp.wait_ge(stacked, 16 * 4 * len(K_PARTS) * len(GROUPS))
            sp.wait_ge(pad_out, 16 * B)

        @block.tensor
        def _(pe):
            pe.wait_ge(w_in, 64)
            for b in range(B):
                rhs = xnT[:, b * L:(b + 1) * L]
                for n, i in enumerate((0, 3, 1, 4, 2)):
                    if b and n in (0, 2):
                        pe.wait_ge(rotated, 2 * b - 1 + n // 2)
                    if b and n == 4:
                        pe.wait_ge(v_done, b)
                    lhsT = wT[:, i * D:(i + 1) * D] if i < 3 else wsT[:, (i - 3) * D:(i - 2) * D]
                    nc.tensor.matmul(bank[i][:, :], lhsT, rhs, start=True, stop=True).then_inc(mm, 1)

        @block.scalar
        def _(act):
            act.wait_ge(w_in, 64)
            for b in range(B):
                n = b // 2
                for i in range(2):
                    act.wait_ge(rotated, 2 * b + i + 1)
                    nc.scalar.copy(split[:, i, b, 0, :], qk[:, i, b % 2, :]).then_inc(hi_done, 1)
                act.wait_ge(mm, 5 * b + 5)
                if b >= 4:
                    act.wait_ge(v_out[n % 2], 16 * (n // 2))
                nc.scalar.activation(v[:, n % 2, b % 2, :], bank[2][:, :], ACT.Identity, bias=bias[:, 2:3]).then_inc(v_done, 1)
                for i in range(2):
                    act.wait_ge(rest_done, 2 * b + i + 1)
                    nc.scalar.copy(split[:, i, b, 1, :], rest[:, i, b % 2, :]).then_inc(mid_done, 1)

        @block.vector
        def _(dve):
            def rotate(b, i):
                d = qk[:, i, b % 2, :]
                dve.wait_ge(mm, 5 * b + 2 * i + 2)
                nc.vector.scalar_tensor_tensor(out=d, in0=bank[i][:, :], scalar=bias[:, i:i + 1], in1=rot[:, 0, :],
                                               op0=ALU.add, op1=ALU.mult)
                if b or i:
                    dve.wait_ge(rotated, 2 * b + i)
                nc.vector.scalar_tensor_tensor(out=part[:, i, :], in0=bank[3 + i][:, :], scalar=bias[:, 3 + i:4 + i],
                                               in1=rot[:, 1, :], op0=ALU.add, op1=ALU.mult).then_inc(part_done, 1)
                dve.wait_ge(part_done, 2 * b + i + 1)
                nc.vector.tensor_tensor(d, d, part[:, i, :], ALU.add).then_inc(rotated, 1)

            def lowest(b):
                for i in range(2):
                    dve.wait_ge(mid_done, 2 * b + i + 1)
                    nc.vector.tensor_tensor(split[:, i, b, 2, :], rest[:, i, b % 2, :],
                                            split[:, i, b, 1, :], ALU.subtract).then_inc(split_done, 1)

            dve.wait_ge(w_in, 64)
            for b in range(B):
                rotate(b, 0)
                rotate(b, 1)
                if b:
                    lowest(b - 1)
                for i in range(2):
                    dve.wait_ge(hi_done, 2 * b + i + 1)
                    nc.vector.tensor_tensor(rest[:, i, b % 2, :], qk[:, i, b % 2, :], split[:, i, b, 0, :],
                                            ALU.subtract).then_inc(rest_done, 1)
            lowest(B - 1)


def solve_attention(nc, A, Apos, xnT, acc, w, k_stack, q_stack, vT_dram, max_dram, sum_dram):
    bank, big, ident = w["bank"], w["big"], w["ident"]
    with ExitStack() as ctx:
        sb, sem = tensors(nc, ctx)
        probs = sb("Kst_Pn", [P, NSLOT * L])
        assert RING * P == NSLOT * L
        Kst = [probs[:, i * NSLOT * L // 2:(i + 1) * NSLOT * L // 2].bitcast(BF16).rearrange("p (s t) -> p s t", s=NSLOT)
               for i in range(2)]
        Pn = probs[:, :].rearrange("p (i j) -> p i j", i=RING)
        Qmax = [sb(f"Qmax{i}", [P, NH, P], BF16) for i in range(2)]
        Qexp = [sb(f"Qexp{i}", [P, NH, P], BF16) for i in range(2)]
        Ed = sb("Ed", [P, BH, P])
        shared = sb("Eoff_RT_hidden", [P, 4 * 2 * L])
        Eoff = shared[:, 0:4 * 3 * 2 * P].rearrange("p (n j h q) -> p n j h q", n=4, j=3, h=2)
        RT = shared[:, 4 * 3 * 2 * P:].rearrange("p (b u q) -> p b u q", b=2, u=LT)
        hidden = [shared[:, i * HC * L:(i + 1) * HC * L].rearrange("p (c t) -> p c t", c=HC) for i in range(2)]
        Rb = sb("Rb", [P, HD + 1, P])
        rZ = sb("rZ", [P, P])
        prod = sb("prod", [P, PRODS, P])
        mx = sb("mx", [P, 2, BH])
        mxp = sb("mxp", [P, 3, BH], BF16)
        mxT = sb("mxT", [P, 3, P], BF16)
        masks = sb("masks", [P, 2, P], BF16)
        identb = sb("identb", [P, P], BF16)
        one = sb("one", [P, 32])
        c_in = sem("solve_c_in")
        steps = ExpertSteps(nc, sb, sem, xnT, acc, w["L1_ffn_c_fc"], w["L1_ffn_c_proj"], w["cw"], hidden,
                            bank[3:7], bank[7])
        with nc.Block() as block:
            @block.sync
            def _(sp):
                sp.dma_start(Rb[:, 0:2, :], w["masks"]).then_inc(c_in, 16)
                for i in range(2):
                    steps.load_expert(sp, i)

            @block.vector
            def _(dve):
                nc.vector.tensor_copy(identb[:, :], ident[:, :])
                nc.vector.memset(Qmax[1][:, :, :], 0.0)
                dve.wait_ge(c_in, 16)
                nc.vector.tensor_copy(masks[:, :, :], Rb[:, 0:2, :])

            @block.gpsimd
            def _(pool):
                nc.gpsimd.memset(Qmax[0][:, :, :], 0.0)

        for I in range(-1, LT):
            attend(nc, I, A, vT_dram, ident, Kst, Qmax, Qexp, k_stack, q_stack, max_dram, sum_dram, mx, mxp, mxT,
                   masks, identb, Ed, Eoff, Apos, one, RT, Rb, bank, big)
            if I >= 0:
                solve_block(nc, I, Ed, Rb, rZ, Pn, prod, A, ident, bank, steps)
        rows_turned, rows_kept = sem("last_rows_turned"), sem("last_rows_kept")
        with nc.Block() as block:
            @block.tensor
            def _(pe):
                turn_rows(nc, A, LT - 1, ident, bank[0:2], rows_turned)

            @block.scalar
            def _(act):
                keep_rows(nc, act, Apos, LT - 1, bank[0:2], rows_turned, rows_kept)


def attend(nc, I, A, vT_dram, ident, Kst, Qmax, Qexp, k_stack, q_stack, max_dram, sum_dram, mx, mxp, mxT, masks,
           identb, Ed, Eoff, Apos, one, RT, Rb, bank, big):
    now, ahead = I >= 0, I + 1 < LT
    scale = float(HD) ** -0.5
    n_loads = 2 * (2 * now + ahead)
    keys_now, keys_ahead = (I + 1) * P, (I + 2) * P
    keys = keys_ahead if ahead else keys_now
    with ExitStack() as ctx:
        sb, sem = tensors(nc, ctx)
        keys_in = [[sem(f"keys_in{i}_{half}") for half in range(2)] for i in range(2)]
        queries_in = [sem(f"queries_in{i}") for i in range(2)]
        max_mm, max_done, exp_mm, exp_done = sem("max_mm"), sem("max_done"), sem("exp_mm"), sem("exp_done")
        sum_mm, sum_read, sum_out = sem("sum_mm"), sem("sum_read"), [sem(f"sum_out{i}") for i in range(2)]
        sum_in, v_in = sem("sum_in"), sem("v_in")
        parts_done, max_turned, max_copied, max_out = sem("parts"), sem("max_turned"), sem("max_copied"), sem("max_out")
        rows_turned, rows_kept = sem("rows_turned"), sem("rows_kept")
        one_cleared = sem("one_cleared")
        block = ctx.enter_context(nc.Block())
        per_bank = L // keys_ahead if ahead else 1
        max_banks = (bank[4], bank[5], bank[7])
        n_max = NH // per_bank
        n_big = 2 if ahead else 3

        if I < 0:
            @block.gpsimd
            def _(pool):
                for i in range(2):
                    nc.gpsimd.memset(Qexp[i][:, :, :], 0.0)
                nc.gpsimd.memset(Apos[:, :], 1.0)
                nc.gpsimd.memset(one[:, :], 0.0).then_inc(one_cleared, 1)
                pool.wait_ge(one_cleared, 1)
                nc.gpsimd.memset(one[:, HD:HD + 1], 1.0)

        @block.sync
        def _(sp):
            def store_sums(b):
                sp.wait_ge(sum_read, b + 1)
                sp.dma_start(sum_dram[b].rearrange("u p q -> p u q"), RT[:, b % 2, :, :]).then_inc(sum_out[b % 2], 16)

            def regroup(b):
                sp.wait_ge(sum_out[b % 2], 16 * (b // 2 + 1))
                sp.dma_start(Rb[b * NH:(b + 1) * NH, :, :],
                             sum_dram[b].rearrange("u (g r) q -> (u g) r q", g=4)[:, 0:HD + 1, :]).then_inc(sum_in, 16)

            def free(b, pairs):
                if b >= 0 and now:
                    sp.wait_ge(exp_mm, NSLOT * b + pairs)
                if b >= 0 and ahead:
                    sp.wait_ge(max_mm, n_max * b + n_max * pairs // NSLOT)

            def load_keys(b, half):
                slots = slice(half * NSLOT // 2, (half + 1) * NSLOT // 2)
                sp.dma_start(Kst[b % 2][:, slots, 0:keys],
                             k_stack[b, :, :, slots, 0:keys].rearrange("h r s t -> (h r) s t")).then_inc(keys_in[b % 2][half], 16)

            def load_queries(b):
                for hh in range(2):
                    r = slice(64 * hh, 64 * hh + ROWS)
                    if now:
                        sp.dma_start(Qexp[b % 2][r, hh::2, :], q_stack[b, hh, :, :, I * P:keys_now]).then_inc(queries_in[b % 2], 16)
                        sp.dma_start(Qexp[b % 2][64 * hh + ROWS:64 * hh + ROWS + 3, hh::2, :],
                                     max_dram[b, hh].rearrange("s p q -> p s q")).then_inc(queries_in[b % 2], 16)
                    if ahead:
                        sp.dma_start(Qmax[b % 2][r, hh::2, :],
                                     q_stack[b, hh, :, :, keys_now:keys_ahead]).then_inc(queries_in[b % 2], 16)

            for b in range(B):
                free(b - 2, NSLOT // 2)
                load_keys(b, 0)
                free(b - 2, NSLOT)
                load_queries(b)
                load_keys(b, 1)
                if now and b >= 2:
                    store_sums(b - 2)
                if now and b >= 3:
                    regroup(b - 3)
            if now:
                heads = vT_dram.rearrange("(h d) (b t) -> b h d t", h=NH, b=B)
                for b in range(B):
                    sp.dma_start(A[b * NH:(b + 1) * NH, :, I * P:keys_now], heads[b, :, :, I * P:keys_now]).then_inc(v_in, 16)
                store_sums(B - 2)
                regroup(B - 3)
                store_sums(B - 1)
                regroup(B - 2)
                regroup(B - 1)
                sp.wait_ge(sum_in, 16 * B)
                sp.wait_ge(v_in, 16 * B)
            if ahead:
                sp.wait_ge(max_copied, 1)
                sp.dma_start(max_dram.rearrange("b h s p q -> (b h s) p q"), mxT[:, :, :]).then_inc(max_out, 16)
                sp.wait_ge(max_out, 16)

        @block.tensor
        def _(pe):
            def exp_logits(b, s):
                n = b * NSLOT + s
                if n >= n_big:
                    pe.wait_ge(exp_done, n - n_big + 1)
                for J in range(I + 1):
                    out = big[n % n_big][:, J * 2 * P:(J + 1) * 2 * P]
                    last = nc.tensor.matmul(out, Kst[b % 2][:, s, J * P:(J + 1) * P], Qexp[b % 2][:, 2 * s:2 * s + 2, :],
                                            start=True, stop=(J < I), skip_group_check=True)
                last = nc.tensor.matmul(out, identb[:, :], masks[:, 1:2, :].broadcast_to([P, 2, P]), start=False,
                                        stop=True, skip_group_check=True)
                last.then_inc(exp_mm, 1)

            def max_logits(b, n):
                m = b * n_max + n
                out = max_banks[m % 3]
                if m >= 3:
                    pe.wait_ge(max_done, m - 2)
                diagonal = out[:, 0:per_bank * keys_ahead].rearrange("p (h t) -> p h t", h=per_bank)[:, :, keys_now:keys_ahead]
                nc.tensor.matmul(diagonal, identb[:, :], masks[:, 0:1, :].broadcast_to([P, per_bank, P]), start=True,
                                 stop=False, skip_group_check=True)
                for j in range(per_bank):
                    h = n * per_bank + j
                    last = nc.tensor.matmul(out[:, j * keys_ahead:(j + 1) * keys_ahead], Qmax[b % 2][:, h, :],
                                            Kst[b % 2][:, h // 2, 0:keys_ahead], start=False, stop=(j == per_bank - 1),
                                            skip_group_check=True)
                last.then_inc(max_mm, 1)

            def sums(b, u):
                n = b * NSLOT + 2 * u
                pe.wait_ge(exp_done, n + 2)
                if u == 0 and b >= 1:
                    pe.wait_ge(sum_read, b)
                for J in range(I, -1, -1):
                    for g in range(4):
                        bh = b * NH + 4 * u + g
                        row = (J * BH + bh) * (HD + 1)
                        last = nc.tensor.matmul(bank[6][32 * g:32 * g + 32, u * P:(u + 1) * P],
                                                one[:, :] if J == I else Apos[:, row:row + 32],
                                                Ed[:, bh, :] if J == I else Eoff[:, (n + g // 2) % 4, J, g % 2, :],
                                                start=(J == I), stop=(J == 0), skip_group_check=True)
                last.then_inc(sum_mm, 1)

            if I >= 1:
                turn_rows(nc, A, I - 1, ident, bank[6:8], rows_turned)
                pe.wait_ge(rows_kept, 2)
            for b in range(B):
                for s in range(NSLOT):
                    if s == 0:
                        pe.wait_ge(queries_in[b % 2], 16 * n_loads * (b // 2 + 1))
                    if s % (NSLOT // 2) == 0:
                        pe.wait_ge(keys_in[b % 2][2 * s // NSLOT], 16 * (b // 2 + 1))
                    if now:
                        exp_logits(b, s)
                    for n in range(n_max * s // NSLOT, n_max * (s + 1) // NSLOT if ahead else 0):
                        max_logits(b, n)
                    if now and s % 2 == n_big - 2 and (b or s > 1):
                        sums(*divmod(b * LT + s // 2 - 1, LT))
            if now:
                sums(B - 1, LT - 1)
            if ahead:
                pe.wait_ge(parts_done, 5)
                for i in range(3):
                    last = nc.tensor.transpose(bank[4][:, :].bitcast(BF16)[:, i * P:(i + 1) * P], mxp[:, i, :], identb[:, :])
                last.then_inc(max_turned, 1)

        @block.scalar
        def _(act):
            if I >= 1:
                keep_rows(nc, act, Apos, I - 1, bank[6:8], rows_turned, rows_kept)
            for n in range(B * NSLOT if now else 0):
                b, s = divmod(n, NSLOT)
                act.wait_ge(exp_mm, n + 1)
                if I:
                    if n >= 4:
                        act.wait_ge(sum_mm, n // 2 - 1)
                    nc.scalar.activation(Eoff[:, n % 4, 0:I, :, :].rearrange("p j h q -> p (j h q)"),
                                         big[n % n_big][:, 0:I * 2 * P], ACT.Exp, scale=scale)
                nc.scalar.activation(Ed[:, 2 * n:2 * n + 2, :].rearrange("p h q -> p (h q)"),
                                     big[n % n_big][:, I * 2 * P:(I + 1) * 2 * P], ACT.Exp, scale=scale).then_inc(exp_done, 1)

        @block.vector
        def _(dve):
            for b in range(B):
                if ahead:
                    cols = mx[:, 0, b * NH:(b + 1) * NH].rearrange("p (j s) -> p s j", j=2)
                    for n in range(n_max):
                        m = b * n_max + n
                        dve.wait_ge(max_mm, m + 1)
                        h = n * per_bank
                        out = cols[:, h // 2, h % 2:h % 2 + 1] if per_bank == 1 else cols[:, h // 2:(h + per_bank) // 2, :]
                        logits = max_banks[m % 3][:, 0:per_bank * keys_ahead]
                        if per_bank > 1:
                            logits = logits.rearrange("p (s j t) -> p s j t", j=2, t=keys_ahead)
                        nc.vector.tensor_reduce(out, logits, AX_X, ALU.max, negate=True).then_inc(max_done, 1)
                if now:
                    dve.wait_ge(sum_mm, LT * (b + 1))
                    if b >= 2:
                        dve.wait_ge(sum_out[b % 2], 16 * (b // 2))
                    nc.vector.tensor_copy(RT[:, b % 2, :, :].rearrange("p u q -> p (u q)"),
                                          bank[6][:, :]).then_inc(sum_read, 1)
            if ahead:
                link = Chain(dve, parts_done)
                dve.wait_ge(max_done, B * n_max)
                link(nc.vector.tensor_copy(mxp[:, 0, :], mx[:, 0, :]))
                link(nc.vector.tensor_tensor(mx[:, 1, :], mx[:, 0, :], mxp[:, 0, :], ALU.subtract))
                link(nc.vector.tensor_copy(mxp[:, 1, :], mx[:, 1, :]))
                link(nc.vector.tensor_tensor(mx[:, 0, :], mx[:, 1, :], mxp[:, 1, :], ALU.subtract))
                link(nc.vector.tensor_copy(mxp[:, 2, :], mx[:, 0, :]))
                dve.wait_ge(max_turned, 1)
                nc.vector.tensor_copy(mxT[:, :, :].rearrange("p a q -> p (a q)"),
                                      bank[4][:, :].bitcast(BF16)[:, 0:3 * P]).then_inc(max_copied, 1)


def turn_rows(nc, A, I, ident, banks, rows_turned):
    for d in range(HD):
        last = nc.tensor.transpose(banks[d // 4][:, (d % 4) * P:(d % 4 + 1) * P], A[:, d, I * P:(I + 1) * P], ident[:, :])
        if d % 4 == 3:
            last.then_inc(rows_turned, 1)


def keep_rows(nc, act, Apos, I, banks, rows_turned, rows_kept):
    rows = Apos[:, I * BH * (HD + 1):(I + 1) * BH * (HD + 1)].rearrange("p (b d) -> p d b", d=HD + 1)
    for i in range(2):
        act.wait_ge(rows_turned, i + 1)
        nc.scalar.copy(rows[:, 4 * i:4 * i + 4, :], banks[i][:, :].rearrange("p (d b) -> p d b", d=4)).then_inc(rows_kept, 1)


def row_cost(r):
    return 0.55 + 0.0083 * (r + 1)


def solve_block(nc, I, Ed, Rb, rZ, Pn, prod, A, ident, bank, steps):
    per = steps.NC * E // LT
    k0 = I * per
    turned_by = [min(P, AHEAD + next((r for r in range(0, P, GROUP) if sum(map(row_cost, range(r))) > STEP_COST * k), P))
                 for k in range(per)] + [P]
    turned_by = [range(a // GROUP, b // GROUP) for a, b in zip([0] + turned_by, turned_by)]
    with ExitStack() as ctx:
        sb, sem = tensors(nc, ctx)
        rz_done, rb_done = sem("rz_done"), sem("rb_done")
        probs_turned, probs_in = sem("probs_turned"), sem("probs_in")
        own_done, row_done = sem("own_done"), sem("row_done")
        block = ctx.enter_context(nc.Block())
        t0 = I * P

        @block.sync
        def _(sp):
            if I:
                for i in range(2):
                    steps.load_expert(sp, 2 * I + i)

        @block.tensor
        def _(pe):
            def turn(g):
                if g >= 2:
                    pe.wait_ge(probs_in, (g - 1) * GROUP)
                keys = -(-(g + 1) * GROUP // 32) * 32
                for i in range(GROUP):
                    last = nc.tensor.transpose(bank[g % 2][:, i * P:i * P + keys], Ed[0:keys, :, g * GROUP + i],
                                               ident[0:keys, 0:keys])
                last.then_inc(probs_turned, 1)

            for g in turned_by[0]:
                turn(g)
            for k in range(per):
                steps.up(pe, k0 + k)
                for g in turned_by[k + 1]:
                    turn(g)
                steps.down(pe, k0 + k)

        @block.scalar
        def _(act):
            def copy(g):
                act.wait_ge(probs_turned, g + 1)
                if (g + 1) * GROUP > RING:
                    act.wait_ge(row_done, HD * ((g + 1) * GROUP - RING - 1))
                for i in range(GROUP):
                    r = g * GROUP + i
                    nc.scalar.activation(Pn[:, r % RING, 0:r + 1], bank[g % 2][:, i * P:i * P + r + 1], ACT.Copy,
                                         scale=rZ[:, r:r + 1]).then_inc(probs_in, 1)

            act.wait_ge(rz_done, 1)
            for g in turned_by[0]:
                copy(g)
            for k in range(per):
                steps.gelu(act, k0 + k)
                for g in turned_by[k + 1]:
                    copy(g)
                steps.weigh(act, k0 + k)

        @block.gpsimd
        def _(pool):
            def own_terms(g):
                ts = slice(t0 + g * OWN, t0 + (g + 1) * OWN)
                first = g * OWN % RING
                diag = Pn.rearrange("p i j -> p (i j)")[:, first * P + g * OWN:(first + OWN - 1) * P + (g + 1) * OWN:P + 1]
                pool.wait_ge(probs_in, (g + 1) * OWN)
                if g:
                    pool.wait_ge(own_done, 3 * g)
                nc.gpsimd.tensor_tensor(A[:, :, ts], A[:, :, ts], diag.rearrange("p (a i) -> p a i", a=1).broadcast_to([P, HD, OWN]),
                                        ALU.mult).then_inc(own_done, 1)
                pool.wait_ge(own_done, 3 * g + 1)
                nc.gpsimd.memset(diag, 1.0).then_inc(own_done, 1)
                pool.wait_ge(own_done, 3 * g + 2)
                nc.gpsimd.tensor_tensor(A[:, :, ts], A[:, :, ts], Rb[:, 0:HD, g * OWN:(g + 1) * OWN],
                                        ALU.add).then_inc(own_done, 1)

            pool.wait_ge(rb_done, 1)
            g = 0
            for k in range(per + 1):
                while (g + 1) * OWN <= turned_by[k].stop * GROUP:
                    own_terms(g)
                    g += 1
                if k:
                    steps.add(pool, k0 + k - 1)

        @block.vector
        def _(dve):
            nc.vector.reciprocal(rZ[:, :], Rb[:, HD, :]).then_inc(rz_done, 1)
            dve.wait_ge(rz_done, 1)
            nc.vector.tensor_tensor(Rb[:, 0:HD, :], Rb[:, 0:HD, :], rZ[:, :].rearrange("p (a q) -> p a q", a=1).broadcast_to([P, HD, P]),
                                    ALU.mult).then_inc(rb_done, 1)
            for r in range(1, P):
                if r % OWN == 0 or r == 1:
                    dve.wait_ge(own_done, 3 * (r // OWN + 1))
                for d in range(HD):
                    if r > 1 or d >= PRODS:
                        dve.wait_ge(row_done, HD * (r - 1) + d + 1 - PRODS)
                    nc.vector.scalar_tensor_tensor(out=prod[:, d % PRODS, 0:r + 1], in0=A[:, d, t0:t0 + r + 1], scalar=1.0,
                                                   in1=Pn[:, r % RING, 0:r + 1], op0=ALU.mult, op1=ALU.mult,
                                                   accum_out=A[:, d, t0 + r:t0 + r + 1]).then_inc(row_done, 1)


def project_out(nc, x, x_dram, s, w, Apos):
    bank, ident = w["bank"], w["ident"]
    with ExitStack() as ctx:
        sb, sem = tensors(nc, ctx)
        wdT, bd, aT = sb("wdT", [P, D]), sb("bd", [P, D]), sb("aT", [P, T])
        rows = sb("rows_b", [P, 2, LT, P])
        x_in, w_in, picked = sem("x_in"), sem("wd_in"), sem("picked")
        turned, copied, mm, read = sem("a_turned"), sem("a_copied"), sem("wd_mm"), sem("wd_read")
        block = ctx.enter_context(nc.Block())

        @block.sync
        def _(sp):
            sp.dma_start(wdT[:, :], w["wdT"]).then_inc(w_in, 16)
            sp.dma_start(bd[:, :], w["bd"].rearrange("(a d) -> a d", a=1).broadcast_to([P, D])).then_inc(w_in, 16)
            sp.dma_start(x[:, :, :].rearrange("p (b t) d -> p b t d", b=B),
                         x_dram.rearrange("b (t p) d -> p b t d", p=P)).then_inc(x_in, 16)
            sp.wait_ge(x_in, 16)

        @block.gpsimd
        def _(pool):
            for b in range(B):
                if b >= 2:
                    pool.wait_ge(turned, b - 1)
                if b:
                    pool.wait_ge(picked, b)
                nc.gpsimd.tensor_copy(rows[:, b % 2, :, :].rearrange("p i (h d) -> p i h d", h=NH),
                                      Apos[:, 0:LT * BH * (HD + 1)].rearrange("p (i b h d) -> p b i h d", i=LT, b=B, h=NH)[:, b, :, :, 0:HD]
                                      ).then_inc(picked, 1)

        @block.tensor
        def _(pe):
            def project(b):
                pe.wait_ge(copied, b + 1)
                if b >= 2:
                    pe.wait_ge(read, b - 1)
                for t in range(LT):
                    last = nc.tensor.matmul(bank[b % 2][:, t * P:(t + 1) * P], aT[:, (b * LT + t) * P:(b * LT + t + 1) * P],
                                            wdT[:, :], start=True, stop=True)
                last.then_inc(mm, 1)

            pe.wait_ge(w_in, 32)
            for b in range(B):
                pe.wait_ge(picked, b + 1)
                if b >= 2:
                    pe.wait_ge(copied, b - 1)
                for i in range(LT):
                    last = nc.tensor.transpose(bank[2 + b % 2][:, i * P:(i + 1) * P], rows[:, b % 2, i, :], ident[:, :])
                last.then_inc(turned, 1)
                if b:
                    project(b - 1)
            project(B - 1)

        @block.scalar
        def _(act):
            for b in range(B):
                act.wait_ge(turned, b + 1)
                nc.scalar.copy(aT[:, b * L:(b + 1) * L], bank[2 + b % 2][:, :]).then_inc(copied, 1)

        @block.vector
        def _(dve):
            dve.wait_ge(w_in, 32)
            for b in range(B):
                dve.wait_ge(mm, b + 1)
                nc.vector.tensor_tensor(s[:, b * LT:(b + 1) * LT, :], bank[b % 2][:, :].rearrange("p (t d) -> p t d", t=LT),
                                        bd[:, :].rearrange("p (a d) -> p a d", a=1).broadcast_to([P, LT, D]),
                                        ALU.add).then_inc(read, 1)


def program(nc, w, cst, out):
    with ExitStack() as ctx:
        sb, sem = tensors(nc, ctx)
        big = [ctx.enter_context(nc.psum_tensor(f"banks{i}", [P, 1024], F32)) for i in range(4)]
        bank = [big[i // 2][:, (i % 2) * 512:(i % 2 + 1) * 512] for i in range(8)]
        cwT_dram = nc.dram_tensor("cwT_dram", (E, T), F32).ap()
        const = {n: sb(n + "_c", list(cst[n].shape)) for n in ("ident", "upper", "ones", "iota8")}
        wg = [sb(f"wg{i}", [P, E]) for i in range(2)]
        c_in = sem("const_in")
        with nc.Block() as block:
            @block.sync
            def _(sp):
                for n, t in const.items():
                    sp.dma_start(t[:, :], cst[n]).then_inc(c_in, 16)
                for t, n in zip(wg, ("L0_rwT", "L1_ffn_w_g")):
                    sp.dma_start(t[:, :], w[n]).then_inc(c_in, 16)
                sp.wait_ge(c_in, 16 * (len(const) + 2))

        ident = const["ident"]
        xnT, cw = sb("xnT", [P, T]), sb("gate_cw", [P, E, NT])
        x_dram = nc.dram_tensor("x_dram", (B, L, D), F32).ap()
        vT_dram = nc.dram_tensor("vT_dram", (P, T), F32).ap()
        k_stack = nc.dram_tensor("k_stack", (B, 2, ROWS + PAD, NSLOT, L), BF16).ap()
        q_stack = nc.dram_tensor("q_stack", (B, 2, ROWS, NSLOT, L), BF16).ap()
        max_dram = nc.dram_tensor("max_dram", (B, 2, NSLOT, 3, P), BF16).ap()
        sum_dram = nc.dram_tensor("sum_dram", (B, LT, P, P), F32).ap()
        more = {**w, **cst, "bank": bank, "big": big, "ident": ident, "cw": cw}
        with ExitStack() as layer:
            sb, sem = tensors(nc, layer)
            x_stored = sem("x_stored")
            x, s, acc = sb("x", [P, NT, D]), sb("s", [P, NT, D]), sb("acc", [P, T])
            rows, mv, rstd = sb("rows", [P, 3, D]), sb("ymv", [P, NT, 2]), sb("yrstd", [P, NT])
            with ExitStack() as part:
                sb, sem = tensors(nc, part)
                xn = sb("xn", [P, NT, D])
                wk, wqv, wo, w_in = sb("wk", [P, D]), sb("wqv", [P, 2, D]), sb("wo", [P, D]), sem("attn_w_in")

                def attention_weights(sp):
                    for dst, n in ((wk[:, :], "Wk"), (wqv[:, 0, :], "Wq"), (wqv[:, 1, :], "Wv"), (wo[:, :], "Wo")):
                        sp.dma_start(dst, w["L0_attn_" + n]).then_inc(w_in, 16)
                    for i, n in enumerate(("bo", "gamma", "beta")):
                        sp.dma_start(rows[:, i, :],
                                     w["L0_attn_" + n].rearrange("(a d) -> a d", a=1).broadcast_to([P, D])).then_inc(w_in, 16)

                normalise(nc, "n0_", w["L0_attn_x"], x, xn, xnT, wg[0], ident, bank, attention_weights)
                linear_attention(nc, xn, xnT, s, rows, mv, rstd, wk, wqv, wo, w_in, ident, bank)
            gate(nc, "g0_", None, cw, cwT_dram, const, bank)
            experts(nc, "e0_", xnT, acc, w["L0_w1T"], w["L0_w2T"], w["L0_b1T"], w["L0_ffn_b2"], cwT_dram, bank,
                    (s, rows, mv, rstd))
            combine(nc, "c0_", x, s, acc, x, x_dram, x_stored, False, ident, bank)
            sb, _ = tensors(nc, layer)
            normalise(nc, "n1_", None, x, sb("xn1", [P, NT, D]), xnT, wg[1], ident, bank,
                      lambda sp: sp.wait_ge(x_stored, 16 * B))
        acc = ctx.enter_context(nc.sbuf_tensor("acc1", [P, NT, D], F32))
        Apos = ctx.enter_context(nc.sbuf_tensor("Apos", [P, (LT * BH) * (HD + 1) + 32], F32))
        with ExitStack() as layer:
            sb, _ = tensors(nc, layer)
            A = sb("A", [P, HD, L])
            with ExitStack() as part:
                sb, sem = tensors(nc, part)
                wT, wsT = sb("wqkvT", [P, 3 * D]), sb("wswapT", [P, 2 * D])
                bias = sb("qkv_bias", [P, 5])
                rot = sb("rot", [P, 2, L])
                w_in = sem("qkv_w_in")

                def qkv_weights(sp):
                    for dst, n in ((wT[:, :], "wqkvT"), (wsT[:, :], "wswapT"), (bias[:, :], "qkv_bias"), (rot[:, :, :], "rot")):
                        sp.dma_start(dst, more[n]).then_inc(w_in, 16)

                gate(nc, "g1_", CAP, cw, None, const, bank, qkv_weights)
                project_qkv(nc, xnT, wT, wsT, bias, rot, w_in, bank, k_stack, q_stack, vT_dram)
            solve_attention(nc, A, Apos, xnT, acc, more, k_stack, q_stack, vT_dram, max_dram, sum_dram)
        with ExitStack() as layer:
            sb, sem = tensors(nc, layer)
            out_stored = sem("out_stored")
            x, s = sb("x1", [P, NT, D]), sb("s1", [P, NT, D])
            project_out(nc, x, x_dram, s, more, Apos)
            combine(nc, "c1_", x, s, acc, x, out, out_stored, True, None, bank)


def _layouts(a):
    w = {n: a[n] for n in ("L0_attn_x", "L0_attn_Wq", "L0_attn_Wk", "L0_attn_Wv", "L0_attn_Wo", "L0_attn_bo",
                           "L0_attn_gamma", "L0_attn_beta", "L0_ffn_b2")}
    w["L0_rwT"] = a["L0_ffn_router_w"].T
    w["L0_w1T"] = a["L0_ffn_w1"].transpose(0, 2, 1)
    w["L0_w2T"] = a["L0_ffn_w2"].transpose(0, 2, 1)
    w["L0_b1T"] = a["L0_ffn_b1"].reshape(E, HC, P).transpose(0, 2, 1)
    for n in ("L1_ffn_w_g", "L1_ffn_c_fc", "L1_ffn_c_proj"):
        w[n] = a[n]
    order = np.arange(D).reshape(NSLOT, 2, HD).transpose(1, 2, 0)
    swap = order[:, [1, 0, *range(2, HD)]].ravel()
    order = order.ravel()
    wq, wk, wv = a["L1_attn_Wqkv"].reshape(3, D, D)
    bq, bk, bv = a["L1_attn_bqkv"].reshape(3, D)
    w["wqkvT"] = np.concatenate([wq[order], wk[order], wv]).T
    w["wswapT"] = np.concatenate([wq[swap], wk[swap]]).T
    w["qkv_bias"] = np.stack([bq[order], bk[order], bv, bq[swap], bk[swap]], axis=1)
    w["wdT"] = a["L1_attn_Wd"].T
    w["bd"] = a["L1_attn_bd"]
    return w


def _constants():
    i = np.arange(P)
    t = np.arange(L, dtype=np.float32)
    rot = np.zeros((2, HD, NSLOT, 2, L), np.float32)
    rot[:, :, :, 0], rot[:, :2, :, 0] = 1.0, np.cos(t)
    rot[:, 0, :, 1], rot[:, 1, :, 1] = -np.sin(t), np.sin(t)
    later = np.where(i[None, :] > i[:, None], BIG, 0.0)
    return {
        "rot": rot.reshape(P, 2, L),
        "masks": np.stack([later, later.T], axis=1).astype(np.float32),
        "ident": np.eye(P, dtype=np.float32),
        "upper": (i[:, None] < i[None, :]).astype(np.float32),
        "ones": np.ones((P, P), np.float32),
        "iota8": np.tile(np.arange(8, dtype=np.float32), (P, 1)),
    }


def kernel(**inputs):
    import concourse.bacc as _bacc
    from concourse import mybir as _mybir
    from concourse.bass_utils import run_bass_kernel_spmd as _run

    nc = _bacc.Bacc("TRN2", target_bir_lowering=False, num_devices=1)
    arrays = {}

    def dram(group):
        args = {}
        for name, a in group.items():
            a = np.ascontiguousarray(a)
            arrays[f"in_{name}_dram"] = a
            args[name] = nc.dram_tensor(f"in_{name}_dram", a.shape, _mybir.dt.from_np(a.dtype), kind="ExternalInput").ap()
        return args

    w = dram(_layouts({n: np.asarray(v) for n, v in inputs.items()}))
    cst = dram(_constants())
    out = nc.dram_tensor("out_0_dram", (B, L, D), F32, kind="ExternalOutput").ap()
    program(nc, w, cst, out)
    r = _run(nc, [arrays], core_ids=[0])
    return r.results[0]["out_0_dram"]
```
